# Optimizing a Trainium2 kernel written in Bass

```python
import numpy as np
import jax
import jax.numpy as jnp

def _softmax(x, axis=-1):
    return jax.nn.softmax(x, axis=axis)

def _gelu(x):
    return jax.nn.gelu(x, approximate=True)

def _silu(x):
    return jax.nn.silu(x)

def _sigmoid(x):
    return jax.nn.sigmoid(x)

def _layernorm(x, axis=-1, eps=1e-05):
    m = jnp.mean(x, axis=axis, keepdims=True)
    v = jnp.var(x, axis=axis, keepdims=True)
    return (x - m) / jnp.sqrt(v + eps)

def _scatter_add(tgt, idx, src, axis=0):
    return tgt.at[idx].add(src)

def _segment_sum(src, seg, n):
    return jax.ops.segment_sum(src, seg, n)
kernel_name = 'mk_gnn_ffn_d2_gnn_r8_6fffb8'

def setup_inputs(seed: int=0):
    np.random.seed(seed)
    _w = jnp.asarray

    def _rec_inputs():
        import jax
        import jax.numpy as jnp
        _gk = jax.random.key(seed)
        x = -0.0003713 + 1 * jax.random.normal(jax.random.fold_in(_gk, 1), (6250, 256), jnp.float32)
        _s = jax.random.randint(jax.random.fold_in(_gk, 2), (50000,), 0, 6250, jnp.int32)
        _d = jax.random.randint(jax.random.fold_in(_gk, 3), (50000,), 0, 6250, jnp.int32)
        _loop = jnp.arange(6250, dtype=jnp.int32)
        src = jnp.concatenate([_s, _d, _loop])
        dst = jnp.concatenate([_d, _s, _loop])
        _o = jnp.argsort(dst, stable=True)
        src = src[_o]
        dst = dst[_o]
        edge_weight1 = 0.000937891 + 0.999965 * jax.random.normal(jax.random.fold_in(_gk, 13), (106250, 1), jnp.float32)
        return (x, src, dst, edge_weight1)
    x, src, dst, edge_weight1 = _rec_inputs()

    def _L0_gnn_setup():
        import jax, jax.numpy as jnp
        import numpy as np
        DIM = 256
        H = 8
        HD = DIM // H
        N = 6250
        E = 100000
        FFN = 4 * DIM
        EPS = 1e-05

        def layer_norm(x, g, b):
            mu = jnp.mean(x, axis=-1, keepdims=True)
            var = jnp.mean((x - mu) ** 2, axis=-1, keepdims=True)
            return (x - mu) * jax.lax.rsqrt(var + EPS) * g + b

        def _mhsa(h, edge_bias, src, dst, Wq, Wk, Wv, Wp, bp):
            n = h.shape[0]
            Q = (h @ Wq).reshape(n, H, HD)
            K = (h @ Wk).reshape(n, H, HD)
            V = (h @ Wv).reshape(n, H, HD)
            score = jnp.einsum('ehd,ehd->eh', K[src], Q[dst]) / np.sqrt(HD) + edge_bias
            m = jax.ops.segment_max(score, dst, num_segments=n)
            ex = jnp.exp(score - m[dst])
            denom = jax.ops.segment_sum(ex, dst, num_segments=n)
            attn = ex / denom[dst]
            out = jax.ops.segment_sum(attn[:, :, None] * V[src], dst, num_segments=n)
            return out.reshape(n, DIM) @ Wp + bp
        key = jax.random.key(seed)
        ks = jax.random.split(key, 16)
        s = 1.0 / np.sqrt(DIM)
        inp = {'h': jax.random.normal(ks[0], (N, DIM), jnp.float32), 'edge_bias': jax.random.normal(ks[1], (E, 1), jnp.float32), 'src': jax.random.randint(ks[2], (E,), 0, N, jnp.int32), 'dst': jax.random.randint(ks[3], (E,), 0, N, jnp.int32), 'Wq': jax.random.normal(ks[4], (DIM, DIM), jnp.float32) * s, 'Wk': jax.random.normal(ks[5], (DIM, DIM), jnp.float32) * s, 'Wv': jax.random.normal(ks[6], (DIM, DIM), jnp.float32) * s, 'Wp': jax.random.normal(ks[7], (DIM, DIM), jnp.float32) * s, 'bp': jnp.zeros((DIM,), jnp.float32), 'ln1_g': jnp.ones((DIM,), jnp.float32), 'ln1_b': jnp.zeros((DIM,), jnp.float32), 'ln2_g': jnp.ones((DIM,), jnp.float32), 'ln2_b': jnp.zeros((DIM,), jnp.float32), 'W1': jax.random.normal(ks[8], (DIM, FFN), jnp.float32) * s, 'b1': jnp.zeros((FFN,), jnp.float32), 'W2': jax.random.normal(ks[9], (FFN, DIM), jnp.float32) * (1.0 / np.sqrt(FFN)), 'b2': jnp.zeros((DIM,), jnp.float32)}
        return inp
    _L0_gnn_all = _L0_gnn_setup()
    _L0_gnn_in = {k: v for k, v in _L0_gnn_all.items() if k in ('Wq', 'Wk', 'Wv', 'Wp', 'bp', 'ln1_g', 'ln1_b', 'ln2_g', 'ln2_b', 'W1', 'b1', 'W2', 'b2')}
    del _L0_gnn_all

    def _L0_ffn_setup():
        import jax, jax.numpy as jnp
        import numpy as np
        B, S, D = (8, 512, 256)
        H = 4 * D
        CAPACITY = 0.5
        key = jax.random.key(seed)
        ks = jax.random.split(key, 6)
        x = jax.random.normal(ks[0], (B, S, D), dtype=jnp.float32)
        attention_mask = jnp.zeros((B, 1, 1, S), dtype=jnp.float32)
        wr = jax.random.normal(ks[1], (D, 1), dtype=jnp.float32) * 0.02
        br = jnp.zeros((1,), dtype=jnp.float32)
        w1 = jax.random.normal(ks[2], (D, H), dtype=jnp.float32) * 0.02
        b1 = jnp.zeros((H,), dtype=jnp.float32)
        w2 = jax.random.normal(ks[3], (H, D), dtype=jnp.float32) * 0.02
        b2 = jnp.zeros((D,), dtype=jnp.float32)
        return {'x': x, 'attention_mask': attention_mask, 'wr': wr, 'br': br, 'w1': w1, 'b1': b1, 'w2': w2, 'b2': b2}
    _L0_ffn_all = _L0_ffn_setup()
    _L0_ffn_in = {k: v for k, v in _L0_ffn_all.items() if k in ('attention_mask', 'wr', 'br', 'w1', 'b1', 'w2', 'b2')}
    del _L0_ffn_all

    def _L1_gnn_setup():
        import jax, jax.numpy as jnp
        import numpy as np
        N = 6250
        E = 50000
        IN_DIM = 256
        H = 8
        D = 32
        LN_EPS = 1e-05
        key = jax.random.key(seed)
        k_x, k_e, k_w, k_a = jax.random.split(key, 4)
        x = jax.random.normal(k_x, (N, IN_DIM), dtype=jnp.float32)
        edge_index = jax.random.randint(k_e, (2, E), 0, N, dtype=jnp.int32)
        w_lim = np.sqrt(6.0 / (IN_DIM + H * D)) * np.sqrt(2.0)
        W = jax.random.uniform(k_w, (IN_DIM, H * D), minval=-w_lim, maxval=w_lim, dtype=jnp.float32)
        a_lim = np.sqrt(6.0 / (2 * D + 1))
        k_as, k_ad = jax.random.split(k_a)
        a_src = jnp.broadcast_to(jax.random.uniform(k_as, (1, D), minval=-a_lim, maxval=a_lim, dtype=jnp.float32), (H, D)).copy()
        a_dst = jnp.broadcast_to(jax.random.uniform(k_ad, (1, D), minval=-a_lim, maxval=a_lim, dtype=jnp.float32), (H, D)).copy()
        gamma = jnp.ones((H * D,), dtype=jnp.float32)
        beta = jnp.zeros((H * D,), dtype=jnp.float32)
        return {'x': x, 'edge_index': edge_index, 'W': W, 'a_src': a_src, 'a_dst': a_dst, 'gamma': gamma, 'beta': beta}
    _L1_gnn_all = _L1_gnn_setup()
    _L1_gnn_in = {k: v for k, v in _L1_gnn_all.items() if k in ('W', 'a_src', 'a_dst', 'gamma', 'beta')}
    del _L1_gnn_all

    def _L1_ffn_setup():
        import jax, jax.numpy as jnp
        import numpy as np
        N_EXPERTS = 8
        TOP_K = 2
        key = jax.random.key(seed)
        ks = jax.random.split(key, 5)
        B, T, C, E, H = (8, 256, 256, 8, 682)
        scale = 1.0 / np.sqrt(C)
        return {'x': jax.random.normal(ks[0], (B, T, C), dtype=jnp.float32), 'router_w': jax.random.normal(ks[1], (E, C), dtype=jnp.float32) * scale, 'w1': jax.random.normal(ks[2], (E, H, C), dtype=jnp.float32) * scale, 'w2': jax.random.normal(ks[3], (E, C, H), dtype=jnp.float32) * (1.0 / np.sqrt(H)), 'w3': jax.random.normal(ks[4], (E, H, C), dtype=jnp.float32) * scale}
    _L1_ffn_all = _L1_ffn_setup()
    _L1_ffn_in = {k: v for k, v in _L1_ffn_all.items() if k in ('router_w', 'w1', 'w2', 'w3')}
    del _L1_ffn_all
    return {'x': x, 'src': src, 'dst': dst, 'edge_weight1': edge_weight1, 'L0_gnn_Wq': _L0_gnn_in['Wq'], 'L0_gnn_Wk': _L0_gnn_in['Wk'], 'L0_gnn_Wv': _L0_gnn_in['Wv'], 'L0_gnn_Wp': _L0_gnn_in['Wp'], 'L0_gnn_bp': _L0_gnn_in['bp'], 'L0_gnn_ln1_g': _L0_gnn_in['ln1_g'], 'L0_gnn_ln1_b': _L0_gnn_in['ln1_b'], 'L0_gnn_ln2_g': _L0_gnn_in['ln2_g'], 'L0_gnn_ln2_b': _L0_gnn_in['ln2_b'], 'L0_gnn_W1': _L0_gnn_in['W1'], 'L0_gnn_b1': _L0_gnn_in['b1'], 'L0_gnn_W2': _L0_gnn_in['W2'], 'L0_gnn_b2': _L0_gnn_in['b2'], 'L0_ffn_attention_mask': _L0_ffn_in['attention_mask'], 'L0_ffn_wr': _L0_ffn_in['wr'], 'L0_ffn_br': _L0_ffn_in['br'], 'L0_ffn_w1': _L0_ffn_in['w1'], 'L0_ffn_b1': _L0_ffn_in['b1'], 'L0_ffn_w2': _L0_ffn_in['w2'], 'L0_ffn_b2': _L0_ffn_in['b2'], 'L1_gnn_W': _L1_gnn_in['W'], 'L1_gnn_a_src': _L1_gnn_in['a_src'], 'L1_gnn_a_dst': _L1_gnn_in['a_dst'], 'L1_gnn_gamma': _L1_gnn_in['gamma'], 'L1_gnn_beta': _L1_gnn_in['beta'], 'L1_ffn_router_w': _L1_ffn_in['router_w'], 'L1_ffn_w1': _L1_ffn_in['w1'], 'L1_ffn_w2': _L1_ffn_in['w2'], 'L1_ffn_w3': _L1_ffn_in['w3']}

def reference(x, src, dst, edge_weight1, L0_gnn_Wq, L0_gnn_Wk, L0_gnn_Wv, L0_gnn_Wp, L0_gnn_bp, L0_gnn_ln1_g, L0_gnn_ln1_b, L0_gnn_ln2_g, L0_gnn_ln2_b, L0_gnn_W1, L0_gnn_b1, L0_gnn_W2, L0_gnn_b2, L0_ffn_attention_mask, L0_ffn_wr, L0_ffn_br, L0_ffn_w1, L0_ffn_b1, L0_ffn_w2, L0_ffn_b2, L1_gnn_W, L1_gnn_a_src, L1_gnn_a_dst, L1_gnn_gamma, L1_gnn_beta, L1_ffn_router_w, L1_ffn_w1, L1_ffn_w2, L1_ffn_w3):
    import jax
    import jax.numpy as jnp

    def _L0_gnn_ref(h, edge_bias, src, dst, Wq, Wk, Wv, Wp, bp, ln1_g, ln1_b, ln2_g, ln2_b, W1, b1, W2, b2):
        import jax, jax.numpy as jnp
        import numpy as np
        DIM = 256
        H = 8
        HD = DIM // H
        N = 6250
        E = 100000
        FFN = 4 * DIM
        EPS = 1e-05

        def layer_norm(x, g, b):
            mu = jnp.mean(x, axis=-1, keepdims=True)
            var = jnp.mean((x - mu) ** 2, axis=-1, keepdims=True)
            return (x - mu) * jax.lax.rsqrt(var + EPS) * g + b

        def _mhsa(h, edge_bias, src, dst, Wq, Wk, Wv, Wp, bp):
            n = h.shape[0]
            Q = (h @ Wq).reshape(n, H, HD)
            K = (h @ Wk).reshape(n, H, HD)
            V = (h @ Wv).reshape(n, H, HD)
            score = jnp.einsum('ehd,ehd->eh', K[src], Q[dst]) / np.sqrt(HD) + edge_bias
            m = jax.ops.segment_max(score, dst, num_segments=n)
            ex = jnp.exp(score - m[dst])
            denom = jax.ops.segment_sum(ex, dst, num_segments=n)
            attn = ex / denom[dst]
            out = jax.ops.segment_sum(attn[:, :, None] * V[src], dst, num_segments=n)
            return out.reshape(n, DIM) @ Wp + bp
        attn_out = _mhsa(h, edge_bias, src, dst, Wq, Wk, Wv, Wp, bp)
        h1 = layer_norm(h + attn_out, ln1_g, ln1_b)
        ffn_out = jax.nn.gelu(h1 @ W1 + b1, approximate=False) @ W2 + b2
        return layer_norm(h1 + ffn_out, ln2_g, ln2_b)

    def _L0_ffn_ref(x, attention_mask, wr, br, w1, b1, w2, b2):
        import jax, jax.numpy as jnp
        import numpy as np
        B, S, D = (8, 512, 256)
        H = 4 * D
        CAPACITY = 0.5
        b, s, d = x.shape
        weights = (jnp.einsum('bsd,do->bso', x, wr) + br)[..., 0]
        k = max(1, int(CAPACITY * s))
        kk = k - 1 if k > 1 else 1
        _, idx = jax.lax.top_k(weights, k)
        sel_idx = idx[:, :kk]
        sel = jnp.take_along_axis(x, sel_idx[:, :, None], axis=1)
        h = jax.nn.gelu(jnp.einsum('bkd,dh->bkh', sel, w1) + b1)
        y = jnp.einsum('bkh,hd->bkd', h, w2) + b2
        w_sel = jnp.take_along_axis(weights, sel_idx, axis=1)
        y = y * w_sel[..., None]
        batch_idx = jnp.arange(b)[:, None]
        processed = jnp.zeros_like(x).at[batch_idx, sel_idx].set(y)
        return processed + x

    def _L1_gnn_ref(x, edge_index, W, a_src, a_dst, gamma, beta):
        import jax, jax.numpy as jnp
        import numpy as np
        N = 6250
        E = 50000
        IN_DIM = 256
        H = 8
        D = 32
        LN_EPS = 1e-05
        n = x.shape[0]
        src, dst = (edge_index[0], edge_index[1])
        hh = (x @ W).reshape(n, H, D)
        s_src = jnp.einsum('nhd,hd->nh', hh, a_src)
        s_dst = jnp.einsum('nhd,hd->nh', hh, a_dst)
        scores = jax.nn.leaky_relu(s_src[src] + s_dst[dst], negative_slope=0.2)
        m = jax.ops.segment_max(scores, dst, num_segments=n)
        e = jnp.exp(scores - m[dst])
        denom = jax.ops.segment_sum(e, dst, num_segments=n)
        alpha = e / denom[dst]
        msgs = hh[src] * alpha[:, :, None]
        out = jax.ops.segment_sum(msgs, dst, num_segments=n).reshape(n, H * D)
        out = out + x
        mu = jnp.mean(out, axis=-1, keepdims=True)
        var = jnp.mean(jnp.square(out - mu), axis=-1, keepdims=True)
        out = (out - mu) / jnp.sqrt(var + LN_EPS) * gamma + beta
        return jax.nn.elu(out)

    def _L1_ffn_ref(x, router_w, w1, w2, w3):
        import jax, jax.numpy as jnp
        import numpy as np
        N_EXPERTS = 8
        TOP_K = 2
        B, T, C = x.shape
        flat = x.reshape(-1, C)
        logits = flat @ router_w.T
        probs = jax.nn.softmax(logits, axis=-1)
        topk_probs, topk_idx = jax.lax.top_k(probs, TOP_K)
        topk_probs = topk_probs / (jnp.sum(topk_probs, axis=-1, keepdims=True) + 1e-09)
        onehot = jax.nn.one_hot(topk_idx, N_EXPERTS, dtype=flat.dtype)
        gates = jnp.einsum('nk,nke->ne', topk_probs, onehot)
        h1 = jnp.einsum('nc,ehc->neh', flat, w1)
        h3 = jnp.einsum('nc,ehc->neh', flat, w3)
        h = jax.nn.silu(h1) * h3
        y = jnp.einsum('neh,ech->nec', h, w2)
        out = jnp.einsum('ne,nec->nc', gates, y)
        return out.reshape(B, T, C)
    edge_index = jnp.stack([src, dst])
    x = x + _L0_gnn_ref(_layernorm(x, axis=-1), edge_weight1, src, dst, L0_gnn_Wq, L0_gnn_Wk, L0_gnn_Wv, L0_gnn_Wp, L0_gnn_bp, L0_gnn_ln1_g, L0_gnn_ln1_b, L0_gnn_ln2_g, L0_gnn_ln2_b, L0_gnn_W1, L0_gnn_b1, L0_gnn_W2, L0_gnn_b2)
    x = x + _L0_ffn_ref(_layernorm(x, axis=-1)[None], L0_ffn_attention_mask, L0_ffn_wr, L0_ffn_br, L0_ffn_w1, L0_ffn_b1, L0_ffn_w2, L0_ffn_b2)[0]
    x = x + _L1_gnn_ref(_layernorm(x, axis=-1), edge_index, L1_gnn_W, L1_gnn_a_src, L1_gnn_a_dst, L1_gnn_gamma, L1_gnn_beta)
    x = x + _L1_ffn_ref(_layernorm(x, axis=-1)[None], L1_ffn_router_w, L1_ffn_w1, L1_ffn_w2, L1_ffn_w3)[0]
    return x

_drawn_inputs = setup_inputs


def setup_inputs(seed=0):
    import zlib

    import numpy as np

    out = dict(_drawn_inputs(seed))
    spreads = {'L0_gnn_bp': (0.0, 0.1),
     'L0_gnn_ln1_g': (1.0, 0.2),
     'L0_gnn_ln1_b': (0.0, 0.1),
     'L0_gnn_ln2_g': (1.0, 0.2),
     'L0_gnn_ln2_b': (0.0, 0.1),
     'L0_gnn_b1': (0.0, 0.1),
     'L0_gnn_b2': (0.0, 0.1),
     'L0_ffn_b1': (0.0, 0.8),
     'L0_ffn_b2': (0.0, 0.8),
     'L1_gnn_gamma': (1.0, 0.6),
     'L1_gnn_beta': (0.0, 0.268)}
    factors = {'L0_ffn_wr': 4.566, 'L0_ffn_w1': 6.745, 'L0_ffn_w2': 6.43, 'L1_gnn_a_dst': 3.851}
    for name, (base, spread) in spreads.items():
        noise = np.random.default_rng([zlib.crc32(name.encode()), seed]).standard_normal(out[name].shape)
        drawn = base * np.exp(spread * noise) if base else spread * noise
        out[name] = jnp.asarray(drawn.astype(out[name].dtype))
    for name, factor in factors.items():
        out[name] = (out[name] * factor).astype(out[name].dtype)
    return out
```

```python
from contextlib import ExitStack

import concourse.bass as bass
from concourse import mybir

F32 = mybir.dt.float32
I32 = mybir.dt.int32
BF16 = mybir.dt.bfloat16
ALU = mybir.AluOpType
ACT = mybir.ActivationFunctionType
AX = mybir.AxisListType

P = 128
N = 6250
D = 256
H = 8
HD = D // H
FF = 4 * D
E = 106250
KC = D // P
BLOCKS = 50
NPAD = BLOCKS * P
LAST_BLOCK = (N - 1) // P
PAIRS = BLOCKS // 2
EDGE_TILES = -(-E // P)
TILE_ROWS = EDGE_TILES + 1
EPAD = TILE_ROWS * P
WINDOWS = 7
STEPS = P * WINDOWS
TGROUPS = WINDOWS
DST_PAD = 1 << 20
BIG = 1.0e30
NEG = -1.0e38
U = 8
EDGE_ITERS = STEPS // (2 * U)
AGG = D + H
LN_EPS = 1e-5
KEEP = 3124
EXPERTS = 8
EH = 682
MAX_TILES = (2 * N) // P + EXPERTS
SLOTS = MAX_TILES * P
EC = -(-EH // P)
EHALF = EH // 2
assert STEPS >= EDGE_TILES + LAST_BLOCK and KEEP == int(0.5 * N) - 1


class Phase:

    def __init__(self, nc, name):
        self.nc, self.name, self.ctx, self.sems = nc, name, ExitStack(), []

    def __enter__(self):
        return self

    def __exit__(self, *e):
        self.ctx.close()
        if self.sems:
            for first in (s for s in self.sems if s - 1 not in self.sems):
                self.nc.gpsimd.sem_clear(range(first, next(i for i in range(first, 257) if i not in self.sems)))
            self.nc.all_engine_barrier()

    def sb(self, name, shape, dt=F32):
        return self.ctx.enter_context(self.nc.sbuf_tensor(f"{self.name}_{name}", shape, dt))

    def ps(self, name, shape, dt=F32):
        return self.ctx.enter_context(self.nc.psum_tensor(f"{self.name}_{name}", shape, dt))

    def sem(self, name):
        sem = self.ctx.enter_context(self.nc.semaphore(f"{self.name}_{name}"))
        self.sems.append(sem.num)
        return sem

    def sems_of_pool(self, name, count):
        return [self.nc.alloc_semaphore(f"{self.name}_{name}{i}") for i in range(count)]

    def block(self):
        return self.ctx.enter_context(self.nc.Block())


class Chain:

    def __init__(self, eng, sem):
        self.eng, self.sem, self.n = eng, sem, 0

    def after(self, ins):
        self.n += 1
        ins.then_inc(self.sem, 1)
        self.eng.wait_ge(self.sem, self.n)
        return ins


def step_tables(nc, g):
    with Phase(nc, "tab") as m:
        last_dst = m.sb("last_dst", [P, TGROUPS], I32)
        last_blk = m.sb("last_blk", [P, TGROUPS], I32)
        ends = m.sb("ends", [P, TGROUPS])
        tile_no = m.sb("tile_no", [P, TGROUPS])
        beyond = m.sb("beyond", [P, TGROUPS])
        step_row = m.sb("step_row", [P, STEPS])
        step_pw = m.sb("step_pw", [P, WINDOWS])
        cmp = m.sb("cmp", [P, TGROUPS, STEPS])
        ones = m.sb("ones", [P, 1])
        tile_f = m.sb("tile_f", [P, WINDOWS])
        tile_idx = m.sb("tile_idx", [P, WINDOWS], I32)
        blk = m.sb("blk", [P, WINDOWS])
        e_row = m.sb("e_row", [1, STEPS])
        b_row = m.sb("b_row", [1, STEPS])
        dst_i = m.sb("dst_i", [P, WINDOWS, P], I32)
        src_i = m.sb("src_i", [P, WINDOWS, P], I32)
        dst_x = m.sb("dst_x", [P, STEPS + 2])
        src_f = m.sb("src_f", [P, WINDOWS, P])
        rel = m.sb("rel", [P, WINDOWS, P])
        over = m.sb("over", [P, WINDOWS, P])
        src_c = m.sb("src_c", [P, STEPS])
        ps_e = m.ps("ps_e", [P, 512])
        ps_r = [m.ps(f"ps_r{i}", [P, 512]) for i in range(2)]
        ps_t = [m.ps(f"ps_t{i}", [P, 512]) for i in range(3)]
        s_in, s_iota, s_set, s_cmp, s_pe, s_idx = (m.sem(x) for x in ("in", "iota", "set", "cmp", "pe", "idx"))
        s_v, s_cols, s_copied, s_side = (m.sem(x) for x in ("v", "cols", "copied", "side"))
        s_dst, s_src, s_bias = m.sems_of_pool("gathered", 3)
        block = m.block()
        dst_runs = dst_x[:, 1:STEPS + 1]

        @block.sync
        def _(sp):
            full = (TGROUPS - 1) * P
            sp.wait_ge(s_set, 1)
            with nc.allow_non_contiguous_dma(reason="one word of each edge tile"):
                sp.dma_start(last_dst[:, 0:TGROUPS - 1],
                             g.dst_rows[0:full, P - 1:P].rearrange("(k p) o -> p (k o)", p=P)).then_inc(s_in, 16)
                sp.dma_start(last_dst[0:TILE_ROWS - full, TGROUPS - 1:TGROUPS],
                             g.dst_rows[full:TILE_ROWS, P - 1:P]).then_inc(s_in, 16)
                sp.wait_ge(s_cols, 1)
                sp.dma_start(dst_x[1:P, 0:1], dst_x[0:P - 1, STEPS:STEPS + 1]).then_inc(s_side, 16)
                sp.dma_start(dst_x[0:P - 1, STEPS + 1:STEPS + 2], dst_x[1:P, 1:2]).then_inc(s_side, 16)
            sp.wait_ge(s_side, 32)

        @block.gpsimd
        def _(pool):
            nc.gpsimd.iota(step_row[:], [[1, STEPS]], 0, 0, allow_small_or_imprecise_dtypes=True).then_inc(s_iota, 1)
            nc.gpsimd.iota(tile_no[:], [[P, TGROUPS]], 0, 1, allow_small_or_imprecise_dtypes=True).then_inc(s_iota, 1)
            nc.gpsimd.iota(step_pw[:], [[1, WINDOWS]], 0, WINDOWS, allow_small_or_imprecise_dtypes=True).then_inc(s_iota, 1)
            pool.wait_ge(s_idx, 1)
            for w in range(WINDOWS):
                idx = bass.IndirectOffsetOnAxis(tile_idx[:, w:w + 1], 0)
                nc.gpsimd.indirect_dma_start(dst_i[:, w, :], None, g.dst_rows, idx).then_inc(s_dst, 16)
                nc.gpsimd.indirect_dma_start(src_i[:, w, :], None, g.src_rows, idx).then_inc(s_src, 16)
                nc.gpsimd.indirect_dma_start(g.run_bias[:, w * P:(w + 1) * P], None, g.bias_rows, idx).then_inc(s_bias, 16)
            pool.wait_ge(s_dst, 16 * WINDOWS)
            pool.wait_ge(s_src, 16 * WINDOWS)
            pool.wait_ge(s_bias, 16 * WINDOWS)

        @block.tensor
        def _(pe):
            by_w = cmp[:].rearrange("q k (p w) -> q k w p", w=WINDOWS)
            pe.wait_ge(s_cmp, TGROUPS)
            for w in range(WINDOWS):
                for k in range(TGROUPS):
                    last = nc.tensor.matmul(ps_e[:, w:w + 1], by_w[:, k, w, :], ones[:],
                                            start=(k == 0), stop=(k == TGROUPS - 1))
            last.then_inc(s_pe, 1)
            for i, (a, b) in enumerate(((0, 512), (512, STEPS))):
                for k in range(TGROUPS):
                    last = nc.tensor.matmul(ps_r[i][0:1, 0:b - a], ones[:], cmp[:, k, a:b],
                                            start=(k == 0), stop=(k == TGROUPS - 1))
            last.then_inc(s_pe, 1)
            pe.wait_ge(s_cols, 2)
            n = 0
            for rows in (rel, src_f):
                for w in range(WINDOWS):
                    if n >= 3:
                        pe.wait_ge(s_copied, n - 2)
                    nc.tensor.transpose(ps_t[n % 3][:, 0:P], rows[:, w, :], g.ident[:]).then_inc(s_pe, 1)
                    n += 1

        @block.vector
        def _(v):
            ch = Chain(v, s_v)
            nc.vector.memset(last_dst[:], DST_PAD).then_inc(s_set, 1)
            ch.after(nc.vector.memset(ones[:], 1.0))
            ch.after(nc.vector.memset(dst_x[:], -1.0))
            v.wait_ge(s_in, 32)
            ch.after(nc.vector.tensor_scalar(last_blk[:], last_dst[:], 7, None, ALU.arith_shift_right))
            ch.after(nc.vector.tensor_scalar(ends[:], last_blk[:], float(LAST_BLOCK), None, ALU.min))
            v.wait_ge(s_iota, 3)
            ch.after(nc.vector.tensor_tensor(ends[:], ends[:], tile_no[:], ALU.add))
            ch.after(nc.vector.tensor_scalar(beyond[:], tile_no[:], float(EDGE_TILES), BIG, ALU.is_ge, ALU.mult))
            ch.after(nc.vector.tensor_tensor(ends[:], ends[:], beyond[:], ALU.add))
            for k in range(TGROUPS):
                nc.vector.tensor_scalar(cmp[:, k, :], step_row[:], ends[:, k:k + 1], None, ALU.is_gt).then_inc(s_cmp, 1)
            v.wait_ge(s_pe, 1)
            nc.vector.tensor_copy(tile_idx[:], ps_e[:, 0:WINDOWS]).then_inc(s_idx, 1)
            ch.after(nc.vector.tensor_copy(tile_f[:], ps_e[:, 0:WINDOWS]))
            ch.after(nc.vector.tensor_tensor(blk[:], step_pw[:], tile_f[:], ALU.subtract))
            ch.after(nc.vector.tensor_scalar(blk[:], blk[:], float(LAST_BLOCK), float(-P), ALU.min, ALU.mult))
            v.wait_ge(s_pe, 2)
            nc.vector.tensor_copy(e_row[0:1, 0:512], ps_r[0][0:1, 0:512]).then_inc(s_v, 1)
            ch.n += 1
            ch.after(nc.vector.tensor_copy(e_row[0:1, 512:STEPS], ps_r[1][0:1, 0:STEPS - 512]))
            ch.after(nc.vector.tensor_tensor(b_row[:], step_row[0:1, :], e_row[:], ALU.subtract))
            ch.after(nc.vector.tensor_scalar(b_row[:], b_row[:], float(LAST_BLOCK), None, ALU.min))
            ch.after(nc.vector.tensor_copy(g.step_block[:], b_row[:]))
            v.wait_ge(s_dst, 16 * WINDOWS)
            nc.vector.tensor_copy(dst_runs, dst_i[:].rearrange("p w j -> p (w j)")).then_inc(s_cols, 1)
            v.wait_ge(s_src, 16 * WINDOWS)
            nc.vector.tensor_copy(src_f[:], src_i[:]).then_inc(s_v, 1)
            ch.n += 1
            v.wait_ge(s_cols, 1)
            ch.after(nc.vector.tensor_tensor(rel[:], dst_runs.rearrange("p (w j) -> p w j", w=WINDOWS),
                                             blk[:].unsqueeze(2).to_broadcast([P, WINDOWS, P]), ALU.add))
            v.sem_inc(s_cols, 1)
            ch.after(nc.vector.tensor_scalar(over[:], rel[:], float(P), NEG, ALU.is_ge, ALU.mult))
            ch.after(nc.vector.tensor_scalar(g.run_off[:].rearrange("p (w j) -> p w j", w=WINDOWS), rel[:],
                                             0.0, NEG, ALU.is_lt, ALU.mult))
            ch.after(nc.vector.tensor_tensor(g.run_off[:].rearrange("p (w j) -> p w j", w=WINDOWS),
                                             g.run_off[:].rearrange("p (w j) -> p w j", w=WINDOWS), over[:], ALU.add))
            v.wait_ge(s_bias, 16 * WINDOWS)
            ch.after(nc.vector.tensor_tensor(g.run_bias[:], g.run_bias[:], g.run_off[:], ALU.add))
            v.wait_ge(s_side, 32)
            ch.after(nc.vector.tensor_tensor(g.run_new[:], dst_x[:, 1:STEPS + 2], dst_x[:, 0:STEPS + 1], ALU.not_equal))
            ch.after(nc.vector.tensor_scalar(g.run_new[:], g.run_new[:], NEG, None, ALU.mult))
            by_w = [g.step_dst[:].rearrange("q (p w) -> q w p", w=WINDOWS),
                    g.step_src[:].rearrange("q (p w) -> q w p", w=WINDOWS)]
            n = 0
            for dest in by_w:
                for w in range(WINDOWS):
                    v.wait_ge(s_pe, 3 + n)
                    nc.vector.tensor_copy(dest[:, w, :], ps_t[n % 3][:, 0:P]).then_inc(s_copied, 1)
                    n += 1
            v.wait_ge(s_copied, n)


SOFT_EXP_AT = 52


def edge_softmax(nc, g, scores, runs_bias, scale):
    with Phase(nc, g.next_name("soft")) as m:
        val = m.sb("val", [P, H, STEPS])
        fwd = m.sb("fwd", [P, H, STEPS])
        bwd = m.sb("bwd", [P, H, STEPS])
        keep = m.sb("keep", [P, 2, H])
        tails = m.sb("tails", [P, 2, H])
        neg = m.sb("neg", [H, 2, P + 1])
        keep_t = m.sb("keep_t", [H, 2, P])
        tails_t = m.sb("tails_t", [H, 2, P])
        carry = m.sb("carry", [P, 2, H])
        ps = [m.ps(f"ps{i}", [P, 4, P]) for i in range(4)]
        ps_k = m.ps("ps_k", [H, 4, P])
        ps_c = m.ps("ps_c", [P, 2, H])
        s_v, s_tr, s_evac, s_tail, s_tailt, s_carry, s_back, s_exp, s_p, s_pevac = (
            m.sem(x) for x in ("v", "tr", "evac", "tail", "tailt", "carry", "back", "exp", "p", "pevac"))
        block = m.block()
        by_w = scores[:].rearrange("q (p w) h -> q w h p", w=WINDOWS)
        groups = [(h, w) for h in range(H) for w in (0, 4)]

        @block.tensor
        def _(pe):
            for n, (h, w0) in enumerate(groups):
                if n >= 4:
                    pe.wait_ge(s_evac, n - 3)
                for w in range(w0, min(w0 + 4, WINDOWS)):
                    last = nc.tensor.transpose(ps[n % 4][:, w - w0, :], by_w[:, w, h, :], g.ident[:])
                last.then_inc(s_tr, 1)
            pe.wait_ge(s_tail, 1)
            for i, t in enumerate((keep[:, 0], keep[:, 1], tails[:, 0], tails[:, 1])):
                last = nc.tensor.transpose(ps_k[:, i, :], t, g.ident[:])
            last.then_inc(s_tailt, 1)
            pe.wait_ge(s_carry, 1)
            nc.tensor.transpose(ps_c[:, 0, :], neg[:, 0, 0:P], g.ident[0:H, 0:H])
            nc.tensor.transpose(ps_c[:, 1, :], neg[:, 1, 1:P + 1], g.ident[0:H, 0:H]).then_inc(s_back, 1)
            for n, (h, w0) in enumerate(groups):
                if w0 == 0:
                    pe.wait_ge(s_exp, h + 1)
                if n >= 4:
                    pe.wait_ge(s_pevac, n - 3)
                for w in range(w0, min(w0 + 4, WINDOWS)):
                    last = nc.tensor.transpose(ps[n % 4][:, w - w0, :], val[:, h, w * P:(w + 1) * P], g.ident[:])
                last.then_inc(s_p, 1)

        @block.scalar
        def _(act):
            for h in range(H):
                act.wait_ge(s_v, SOFT_EXP_AT + h)
                nc.scalar.activation(val[:, h, :], val[:, h, :], ACT.Exp).then_inc(s_exp, 1)

        @block.vector
        def _(v):
            ch = Chain(v, s_v)
            ch.after(nc.vector.memset(neg[:], NEG))
            for n, (h, w0) in enumerate(groups):
                v.wait_ge(s_tr, n + 1)
                w1 = min(w0 + 4, WINDOWS)
                nc.vector.scalar_tensor_tensor(val[:, h, w0 * P:w1 * P], ps[n % 4][:, 0:w1 - w0, :].rearrange("p a b -> p (a b)"),
                                               scale, runs_bias[:, w0 * P:w1 * P], ALU.mult, ALU.add).then_inc(s_evac, 1)
            v.wait_ge(s_evac, len(groups))
            start, end = g.run_new[:, 0:STEPS], g.run_new[:, 1:STEPS + 1]

            def scans(first):
                for h in range(H):
                    nc.vector.tensor_tensor_scan(fwd[:, h, :], start, val[:, h, :],
                                                 NEG if first else carry[:, 0, h:h + 1], ALU.add, ALU.max).then_inc(s_v, 1)
                    nc.vector.tensor_tensor_scan(bwd[:, h, ::-1], end[:, ::-1], val[:, h, ::-1],
                                                 NEG if first else carry[:, 1, h:h + 1], ALU.add, ALU.max).then_inc(s_v, 1)
                    ch.n += 2
                v.wait_ge(s_v, ch.n)

            scans(True)
            ch.after(nc.vector.tensor_reduce(keep[:, 0, 0:1], start, AX.X, ALU.min))
            ch.after(nc.vector.tensor_reduce(keep[:, 1, 0:1], end, AX.X, ALU.min))
            ch.after(nc.vector.tensor_copy(keep[:, :, 1:H], keep[:, :, 0:1].to_broadcast([P, 2, H - 1])))
            ch.after(nc.vector.tensor_copy(tails[:, 0, :], fwd[:, :, STEPS - 1]))
            ch.after(nc.vector.tensor_copy(tails[:, 1, :], bwd[:, :, 0]))
            v.sem_inc(s_tail, 1)
            v.wait_ge(s_tailt, 1)
            ch.after(nc.vector.tensor_copy(keep_t[:], ps_k[:, 0:2, :]))
            ch.after(nc.vector.tensor_copy(tails_t[:], ps_k[:, 2:4, :]))
            ch.after(nc.vector.tensor_tensor_scan(neg[:, 0, 1:P + 1], keep_t[:, 0, :], tails_t[:, 0, :], NEG, ALU.add, ALU.max))
            ch.after(nc.vector.tensor_tensor_scan(neg[:, 1, P - 1::-1], keep_t[:, 1, ::-1], tails_t[:, 1, ::-1], NEG, ALU.add, ALU.max))
            v.sem_inc(s_carry, 1)
            v.wait_ge(s_back, 1)
            ch.after(nc.vector.tensor_copy(carry[:], ps_c[:]))
            scans(False)
            for h in range(H):
                ch.after(nc.vector.tensor_tensor(fwd[:, h, :], fwd[:, h, :], bwd[:, h, :], ALU.max))
            assert ch.n + 1 == SOFT_EXP_AT, ch.n
            for h in range(H):
                nc.vector.tensor_tensor(val[:, h, :], val[:, h, :], fwd[:, h, :], ALU.subtract).then_inc(s_v, 1)
            for n, (h, w0) in enumerate(groups):
                v.wait_ge(s_p, n + 1)
                w1 = min(w0 + 4, WINDOWS)
                nc.vector.tensor_copy(by_w[:, w0:w1, h, :], ps[n % 4][:, 0:w1 - w0, :]).then_inc(s_pevac, 1)
            v.wait_ge(s_pevac, len(groups))


HALVES = STEPS // U
RING = 4
assert HALVES % RING == 0


def turns(eng, body, first=0):
    for n in range(first, RING):
        body(n, n, True)
    with eng.Fori(1, HALVES // RING - 1) as it:
        for r in range(RING):
            body(it * RING + r, r, True)
    for r in range(RING):
        body(HALVES - RING + r, r, r + 1 < RING)


def step_blocks(nc, g, engine, n):
    return nc.values_load_multi_w_load_instructions(
        g.step_block[0:1, bass.ds(n * U, U)], [engine], min_val=0, max_val=LAST_BLOCK,
        skip_runtime_bounds_check_because="made on the chip and clamped")[1]


def pick(nc, g, out, n):
    return nc.vector.tensor_tensor(out, g.step_dst[:, bass.ds(n * U, U)].unsqueeze(2).to_broadcast([P, U, P]),
                                   g.lane[:].unsqueeze(1).to_broadcast([P, U, P]), ALU.is_equal)


def edge_scores(nc, g, scores, rows, width, node_vals):
    dots = width == D
    per_bank = 512 // D if dots else U
    banks = U // per_bank
    with Phase(nc, g.next_name("score")) as m:
        ring = m.sb("ring", [P, RING, U, width])
        idx = m.sb("idx", [P, RING, U], I32)
        sel = m.sb("sel", [P, 2, U, P])
        sel_t = m.sb("sel_t", [P, 2, U, P])
        prod = m.sb("prod", [P, 2, U, width])
        ps_t = [m.ps(f"ps_t{i}", [P, 4, P]) for i in range(2)]
        ps_q = [m.ps(f"ps_q{i}", [P, per_bank, width]) for i in range(banks)]
        s_used, s_idx, s_sel, s_selt, s_tpe, s_q, s_qfree, s_red = (
            m.sem(x) for x in ("used", "idx", "sel", "selt", "tpe", "q", "qfree", "red"))
        s_row = m.sems_of_pool("row", RING)
        block = m.block()

        @block.gpsimd
        def _(pool):
            def gather(n, slot, more):
                pool.wait_ge(s_idx, n + 1)
                pool.nop(nofuse=True)
                for u in range(U):
                    nc.gpsimd.indirect_dma_start(ring[:, slot, u, :], None, rows,
                                                 bass.IndirectOffsetOnAxis(idx[:, slot, u:u + 1], 0)
                                                 ).then_inc(s_row[slot], 16)
            turns(pool, gather)

        @block.scalar
        def _(act):
            def index(n, slot):
                if not isinstance(n, int) or n >= RING:
                    act.wait_ge(s_used, n + (1 - RING))
                nc.scalar.activation(idx[:, slot, :], g.step_src[:, bass.ds(n * U, U)], ACT.Copy).then_inc(s_idx, 1)

            def transposed(n, slot):
                for i in range(2):
                    act.wait_ge(s_tpe, n * 2 + i + 1)
                    nc.scalar.activation(sel_t[:, slot % 2, 4 * i:4 * i + 4, :], ps_t[i][:], ACT.Copy).then_inc(s_selt, 1)

            for n in range(RING - 1):
                index(n, n)
            transposed(0, 0)

            def half(n, slot, more):
                if not isinstance(n, int) or n < HALVES - RING + 1:
                    index(n + (RING - 1), (slot + RING - 1) % RING)
                if more:
                    if not isinstance(n, int) or n >= 1:
                        act.wait_ge(s_q, n * banks)
                    transposed(n + 1, slot + 1)
            turns(act, half)

        @block.tensor
        def _(pe):
            pe.sem_inc(s_qfree, banks)

            def transposes(n, slot):
                pe.wait_ge(s_sel, n + 1)
                if not isinstance(n, int) or n > 0:
                    pe.wait_ge(s_selt, n * 2)
                for u in range(U):
                    last = nc.tensor.transpose(ps_t[u // 4][:, u % 4, :], sel[:, slot % 2, u, :], g.ident[:])
                    if u % 4 == 3:
                        last.then_inc(s_tpe, 1)

            transposes(0, 0)

            def half(n, slot, more):
                blocks = step_blocks(nc, g, mybir.EngineType.PE, n)
                for u in range(U):
                    if u == U // 2 and more:
                        transposes(n + 1, slot + 1)
                    j = u // per_bank
                    if u % 4 == 0:
                        pe.wait_ge(s_selt, n * 2 + u // 4 + 1)
                    if u % per_bank == 0:
                        pe.wait_ge(s_qfree, n * banks + j + 1)
                    last = nc.tensor.matmul(ps_q[j][:, u % per_bank, :], sel_t[:, slot % 2, u, :],
                                            node_vals[:, bass.ds(blocks[u], 1), :].rearrange("p a d -> p (a d)"),
                                            start=True, stop=True)
                    if u % per_bank == per_bank - 1:
                        last.then_inc(s_q, 1)
            turns(pe, half)

        @block.vector
        def _(v):
            pick(nc, g, sel[:, 0], 0).then_inc(s_sel, 1)

            def half(n, slot, more):
                par = slot % 2
                if more:
                    if not isinstance(n, int) or n >= 1:
                        v.wait_ge(s_tpe, n * 2)
                    pick(nc, g, sel[:, 1 - par], n + 1).then_inc(s_sel, 1)
                v.wait_ge(s_row[slot], (n + (RING - slot)) * (16 * U // RING))
                if not isinstance(n, int) or n >= 2:
                    v.wait_ge(s_red, n - 1)
                for j in range(banks):
                    v.wait_ge(s_q, n * banks + j + 1)
                    nc.vector.tensor_tensor(prod[:, par, j * per_bank:(j + 1) * per_bank, :], ps_q[j][:],
                                            ring[:, slot, j * per_bank:(j + 1) * per_bank, :],
                                            ALU.mult if dots else ALU.add).then_inc(s_qfree, 1)
                v.wait_ge(s_qfree, n * banks + 2 * banks)
                v.sem_inc(s_used, 1)
                out = scores[:, bass.ds(n * U, U), :]
                if dots:
                    nc.vector.tensor_reduce(out.rearrange("p u h -> p (u h)"),
                                            prod[:, par].rearrange("p u (h d) -> p (u h) d", h=H),
                                            AX.X, ALU.add).then_inc(s_red, 1)
                else:
                    x = prod[:, par].rearrange("p u h -> p (u h)")
                    nc.vector.scalar_tensor_tensor(out.rearrange("p u h -> p (u h)"), x, 0.2, x,
                                                   ALU.mult, ALU.max).then_inc(s_red, 1)
            turns(v, half)
            v.wait_ge(s_red, HALVES)


def aggregate(nc, g, acc, probs, rows):
    with Phase(nc, g.next_name("agg")) as m:
        ring = m.sb("ring", [P, RING, U, D])
        idx = m.sb("idx", [P, RING, U], I32)
        sel = m.sb("sel", [P, 2, U, P])
        msg = m.sb("msg", [P, 2, U, AGG])
        ps = [m.ps(f"ps{i}", [P, 512]) for i in range(U)]
        s_used, s_idx, s_sel, s_pcol, s_msg, s_mm, s_add = (
            m.sem(x) for x in ("used", "idx", "sel", "pcol", "msg", "mm", "add"))
        s_row = m.sems_of_pool("row", RING)
        block = m.block()

        @block.gpsimd
        def _(pool):
            def gather(n, slot, more):
                pool.wait_ge(s_idx, n + 1)
                pool.nop(nofuse=True)
                for u in range(U):
                    nc.gpsimd.indirect_dma_start(ring[:, slot, u, :], None, rows,
                                                 bass.IndirectOffsetOnAxis(idx[:, slot, u:u + 1], 0)
                                                 ).then_inc(s_row[slot], 16)
            turns(pool, gather)

        @block.scalar
        def _(act):
            def index(n, slot):
                if not isinstance(n, int) or n >= RING:
                    act.wait_ge(s_used, n + (1 - RING))
                nc.scalar.activation(idx[:, slot, :], g.step_src[:, bass.ds(n * U, U)], ACT.Copy).then_inc(s_idx, 1)

            for n in range(RING - 1):
                index(n, n)

            def half(n, slot, more):
                if not isinstance(n, int) or n < HALVES - RING + 1:
                    index(n + (RING - 1), (slot + RING - 1) % RING)
                if not isinstance(n, int) or n >= 2:
                    act.wait_ge(s_mm, n * U - U)
                nc.scalar.activation(msg[:, slot % 2, :, D:AGG], probs[:, bass.ds(n * U, U), :], ACT.Copy).then_inc(s_pcol, 1)
            turns(act, half)

        @block.tensor
        def _(pe):
            pe.sem_inc(s_add, U)

            def half(n, slot, more):
                pe.wait_ge(s_msg, n + 1)
                pe.wait_ge(s_pcol, n + 1)
                for u in range(U):
                    pe.wait_ge(s_add, n * U + u + 1)
                    nc.tensor.matmul(ps[u][:, 0:AGG], sel[:, slot % 2, u, :], msg[:, slot % 2, u, :],
                                     start=True, stop=True).then_inc(s_mm, 1)
            turns(pe, half)

        @block.vector
        def _(v):
            def message(n, slot, u):
                return nc.vector.tensor_tensor(msg[:, slot % 2, u, 0:D].rearrange("p (h d) -> p h d", h=H),
                                               ring[:, slot, u, :].rearrange("p (h d) -> p h d", h=H),
                                               probs[:, bass.ds(n * U + u, 1), :].rearrange("p a h -> p (a h)")
                                               .unsqueeze(2).to_broadcast([P, H, HD]), ALU.mult)

            def start(n, slot):
                pick(nc, g, sel[:, slot % 2], n).then_inc(s_sel, 1)
                v.wait_ge(s_row[slot], (n + (RING - slot)) * (16 * U // RING))

            def finish(n):
                v.wait_ge(s_sel, n * 2 + 2)
                v.sem_inc(s_used, 1)
                v.sem_inc(s_msg, 1)

            start(0, 0)
            for u in range(U):
                ins = message(0, 0, u)
            ins.then_inc(s_sel, 1)
            finish(0)

            def half(n, slot, more):
                if more:
                    if not isinstance(n, int) or n >= 1:
                        v.wait_ge(s_mm, n * U)
                    start(n + 1, (slot + 1) % RING)
                blocks = step_blocks(nc, g, mybir.EngineType.DVE, n)
                for u in range(U):
                    if more:
                        ins = message(n + 1, (slot + 1) % RING, u)
                        if u == U - 1:
                            ins.then_inc(s_sel, 1)
                            finish(n + 1)
                    v.wait_ge(s_mm, n * U + u + 1)
                    v.wait_ge(s_add, n * U + u + U)
                    at = acc[:, bass.ds(blocks[u], 1), :].rearrange("p a d -> p (a d)")
                    nc.vector.tensor_tensor(at, at, ps[u][:, 0:AGG], ALU.add).then_inc(s_add, 1)
            turns(v, half)
            v.wait_ge(s_add, STEPS + U)


class Count:

    def __init__(self, eng, sem, n, per):
        self.eng, self.sem, self.n, self.per, self.i = eng, sem, n, per, 0

    def step(self, ins):
        self.i += 1
        return ins.then_inc(self.sem, 1)

    def here(self):
        self.eng.wait_ge(self.sem, self.n * self.per + self.i)

    def then(self, ins):
        self.step(ins)
        self.here()

    def done(self):
        assert self.i == self.per, self.i


def rounds(eng, body, count=PAIRS):
    assert count % 2 == 1
    body(0, 0, 2)
    body(1, 1, 2)
    with eng.Fori(1, count // 2 - 1) as it:
        body(it * 2, 0, 2)
        body(it * 2 + 1, 1, 2)
    for left in (2, 1, 0):
        body(count - 1 - left, left % 2, left)


def late(n, by):
    return not isinstance(n, int) or n >= by


def pair_rows(dram, n):
    return dram.rearrange("(b p) d -> p b d", p=P)[:, bass.ds(n * 2, 2), :]


LN_STEPS = 5


def norm_begin(nc, c, stat, x, s_var):
    for b in range(2):
        c.step(nc.vector.bn_stats(stat[:, 6 * b:6 * b + 6], x[:, b, :]))
    c.here()
    c.eng.nop(nofuse=True)
    for b in range(2):
        c.step(nc.vector.bn_aggr(stat[:, 12 + 2 * b:14 + 2 * b], stat[:, 6 * b:6 * b + 6]))
    c.here()
    nc.vector.tensor_scalar(stat[:, 16:18], stat[:, 12:16].rearrange("p (b s) -> p b s", b=2)[:, :, 1],
                            LN_EPS, None, ALU.add).then_inc(s_var, 1)


def norm_end(nc, c, stat, out, x, s_rstd, k, per):
    c.eng.wait_ge(s_rstd, c.n * per + k + 1)
    for b in range(2):
        ins = nc.vector.tensor_scalar(out[:, b, :], x[:, b, :], stat[:, 12 + 2 * b:13 + 2 * b], stat[:, 18 + b:19 + b],
                                      ALU.subtract, ALU.mult)
    c.then(ins)


def norm_pair(nc, g, c, stat, out, x, s_var, s_rstd, k, per):
    norm_begin(nc, c, stat, x, s_var)
    norm_end(nc, c, stat, out, x, s_rstd, k, per)


def spread(row, n):
    return row.rearrange("(a n) -> a n", a=1).to_broadcast([P, n])


def project_qkv(nc, g, q):
    with Phase(nc, "qkv") as m:
        w = m.sb("w", [P, KC, 3 * D])
        x = m.sb("x", [P, 2, 2, D])
        xn = m.sb("xn", [P, 2, 2, D])
        xt = m.sb("xt", [P, 2, KC, 2, P])
        kv = m.sb("kv", [P, 2, 2, 2 * D])
        stat = m.sb("stat", [P, 2, 20])
        ps_t = [m.ps(f"ps_t{i}", [P, 2, KC, P]) for i in range(2)]
        ps_kv = [[m.ps(f"ps_kv{i}{b}", [P, 2 * D]) for b in range(2)] for i in range(2)]
        ps_q = [m.ps(f"ps_q{i}", [P, 2, D]) for i in range(2)]
        s_w, s_ln, s_var, s_rstd, s_t, s_xt, s_mm, s_out = (
            m.sem(k) for k in ("w", "ln", "var", "rstd", "t", "xt", "mm", "out"))
        s_x, s_xnst, s_kvst = ([m.sem(f"{k}{i}") for i in range(2)] for k in ("x", "xnst", "kvst"))
        block = m.block()
        LN = LN_STEPS

        @block.sync
        def _(sp):
            def load(n, slot):
                sp.dma_start(x[:, slot], pair_rows(g.x, n)).then_inc(s_x[slot], 16)

            load(0, 0)
            load(1, 1)
            for i, t in enumerate((g.Wk, g.Wv, g.Wq)):
                sp.dma_start(w[:, :, i * D:(i + 1) * D], t.rearrange("(k p) n -> p k n", p=P)).then_inc(s_w, 16)

            def turn(n, slot, more):
                sp.wait_ge(s_ln, n * LN + LN)
                if more == 2:
                    load(n + 2, slot)
                sp.dma_start(pair_rows(g.norm, n), xn[:, slot]).then_inc(s_xnst[slot], 16)
                sp.wait_ge(s_out, n * 3 + 2)
                sp.dma_start(pair_rows(g.k_rows, n), kv[:, slot, :, 0:D]).then_inc(s_kvst[slot], 16)
                sp.dma_start(pair_rows(g.v_rows, n), kv[:, slot, :, D:2 * D]).then_inc(s_kvst[slot], 16)
            rounds(sp, turn)
            for i, turns_ in enumerate((PAIRS // 2 + 1, PAIRS // 2)):
                sp.wait_ge(s_xnst[i], 16 * turns_)
                sp.wait_ge(s_kvst[i], 32 * turns_)

        @block.gpsimd
        def _(pool):
            def turn(n, slot, more):
                pool.wait_ge(s_var, n + 1)
                nc.gpsimd.tensor_tensor(stat[:, slot, 18:20], stat[:, slot, 16:18], g.minus_half[:], ALU.pow).then_inc(s_rstd, 1)
            rounds(pool, turn)

        @block.vector
        def _(v):
            def turn(n, slot, more):
                c = Count(v, s_ln, n, LN)
                v.wait_ge(s_x[slot], (n + (2 - slot)) * 8)
                if late(n, 2):
                    v.wait_ge(s_xnst[slot], (n - slot) * 8)
                    v.wait_ge(s_t, n - 1)
                norm_pair(nc, g, c, stat[:, slot], xn[:, slot], x[:, slot], s_var, s_rstd, 0, 1)
                c.done()
            rounds(v, turn)

        @block.tensor
        def _(pe):
            def transposes(n, slot):
                pe.wait_ge(s_ln, n * LN + LN)
                if late(n, 2):
                    pe.wait_ge(s_xt, n - 1)
                for b in range(2):
                    for k in range(KC):
                        last = nc.tensor.transpose(ps_t[slot][:, b, k, :], xn[:, slot, b, k * P:(k + 1) * P], g.ident[:])
                last.then_inc(s_t, 1)

            transposes(0, 0)
            pe.wait_ge(s_w, 48)

            def turn(n, slot, more):
                pe.wait_ge(s_xt, n + 1)
                if late(n, 2):
                    pe.wait_ge(s_out, n * 3 - 3)
                for b in range(2):
                    for k in range(KC):
                        last = nc.tensor.matmul(ps_kv[slot][b][:], xt[:, slot, k, b, :], w[:, k, 0:2 * D],
                                                start=(k == 0), stop=(k == KC - 1))
                    last.then_inc(s_mm, 1)
                if more:
                    transposes(n + 1, 1 - slot)
                for b in range(2):
                    for k in range(KC):
                        last = nc.tensor.matmul(ps_q[slot][:, b, :], xt[:, slot, k, b, :], w[:, k, 2 * D:3 * D],
                                                start=(k == 0), stop=(k == KC - 1))
                last.then_inc(s_mm, 1)
            rounds(pe, turn)

        @block.scalar
        def _(act):
            def evac_xt(n, slot):
                act.wait_ge(s_t, n + 1)
                if late(n, 2):
                    act.wait_ge(s_mm, n * 3 - 3)
                nc.scalar.activation(xt[:, slot].rearrange("p k b n -> p b k n"), ps_t[slot][:], ACT.Copy).then_inc(s_xt, 1)

            evac_xt(0, 0)

            def turn(n, slot, more):
                if late(n, 2):
                    act.wait_ge(s_kvst[slot], (n - slot) * 16)
                for b in range(2):
                    act.wait_ge(s_mm, n * 3 + b + 1)
                    nc.scalar.activation(kv[:, slot, b, :], ps_kv[slot][b][:], ACT.Copy).then_inc(s_out, 1)
                if more:
                    evac_xt(n + 1, 1 - slot)
                act.wait_ge(s_mm, n * 3 + 3)
                nc.scalar.activation(q[:, bass.ds(n * 2, 2), :], ps_q[slot][:], ACT.Copy).then_inc(s_out, 1)
            rounds(act, turn)
            act.wait_ge(s_out, 3 * PAIRS)


def attention_out(nc, g, acc):
    with Phase(nc, "att") as m:
        w = m.sb("w", [P, KC, D])
        vec = m.sb("vec", [P, 3, D])
        h0 = m.sb("h0", [P, 2, 2, D])
        rec = m.sb("rec", [P, 2, 2, H])
        o = m.sb("o", [P, 2, 2, D])
        ot = m.sb("ot", [P, 2, KC, 2, P])
        t = m.sb("t", [P, 2, D])
        tn = m.sb("tn", [P, 2, D])
        h1 = m.sb("h1", [P, 2, 2, D])
        stat = m.sb("stat", [P, 20])
        ps_t = [m.ps(f"ps_t{i}", [P, 2, KC, P]) for i in range(2)]
        ps_o = [m.ps(f"ps_o{i}", [P, 2, D]) for i in range(2)]
        s_w, s_o, s_c, s_var, s_rstd, s_t, s_ot, s_mm = (
            m.sem(k) for k in ("w", "o", "c", "var", "rstd", "t", "ot", "mm"))
        s_x, s_st = ([m.sem(f"{k}{i}") for i in range(2)] for k in ("x", "st"))
        block = m.block()
        OPS, OUT = 3, 4 + LN_STEPS

        @block.sync
        def _(sp):
            sp.dma_start(w[:], g.Wp.rearrange("(k p) n -> p k n", p=P)).then_inc(s_w, 16)
            for i, r in enumerate((g.bp, g.ln1_g, g.ln1_b)):
                sp.dma_start(vec[:, i, :], spread(r, D)).then_inc(s_w, 16)

            def turn(n, slot, more):
                if late(n, 2):
                    sp.wait_ge(s_c, n * OUT - OUT)
                sp.dma_start(h0[:, slot], pair_rows(g.norm, n)).then_inc(s_x[slot], 16)
                if late(n, 1):
                    sp.wait_ge(s_c, n * OUT)
                    sp.dma_start(pair_rows(g.hidden, n - 1), h1[:, 1 - slot]).then_inc(s_st[1 - slot], 16)
            rounds(sp, turn)
            sp.wait_ge(s_c, PAIRS * OUT)
            sp.dma_start(pair_rows(g.hidden, PAIRS - 1), h1[:, 0]).then_inc(s_st[0], 16)
            sp.wait_ge(s_st[0], 16 * (PAIRS // 2 + 1))
            sp.wait_ge(s_st[1], 16 * (PAIRS // 2))

        @block.gpsimd
        def _(pool):
            def turn(n, slot, more):
                pool.wait_ge(s_var, n + 1)
                nc.gpsimd.tensor_tensor(stat[:, 18:20], stat[:, 16:18], g.minus_half[:], ALU.pow).then_inc(s_rstd, 1)
            rounds(pool, turn)

        @block.tensor
        def _(pe):
            pe.wait_ge(s_w, 64)

            def transposes(n, slot):
                pe.wait_ge(s_o, n * OPS + OPS)
                if late(n, 2):
                    pe.wait_ge(s_ot, n - 1)
                for b in range(2):
                    for k in range(KC):
                        last = nc.tensor.transpose(ps_t[slot][:, b, k, :], o[:, slot, b, k * P:(k + 1) * P], g.ident[:])
                last.then_inc(s_t, 1)
            transposes(0, 0)

            def turn(n, slot, more):
                pe.wait_ge(s_ot, n + 1)
                if late(n, 2):
                    pe.wait_ge(s_c, n * OUT - OUT)
                for b in range(2):
                    for k in range(KC):
                        last = nc.tensor.matmul(ps_o[slot][:, b, :], ot[:, slot, k, b, :], w[:, k, :],
                                                start=(k == 0), stop=(k == KC - 1))
                last.then_inc(s_mm, 1)
                if more:
                    transposes(n + 1, 1 - slot)
            rounds(pe, turn)

        @block.scalar
        def _(act):
            def turn(n, slot, more):
                act.wait_ge(s_t, n + 1)
                if late(n, 2):
                    act.wait_ge(s_mm, n - 1)
                nc.scalar.activation(ot[:, slot].rearrange("p k b n -> p b k n"), ps_t[slot][:], ACT.Copy).then_inc(s_ot, 1)
            rounds(act, turn)

        @block.vector
        def _(v):
            v.wait_ge(s_w, 64)

            def normalise(n, slot):
                c = Count(v, s_o, n, OPS)
                a = acc[:, bass.ds(n * 2, 2), :]
                c.then(nc.vector.tensor_scalar(rec[:, slot], a[:, :, D:AGG], 0.5, None, ALU.max))
                c.then(nc.vector.reciprocal(rec[:, slot], rec[:, slot]))
                if late(n, 2):
                    v.wait_ge(s_t, n - 1)
                c.step(nc.vector.tensor_tensor(o[:, slot].rearrange("p b (h d) -> p b h d", h=H),
                                               a[:, :, 0:D].rearrange("p b (h d) -> p b h d", h=H),
                                               rec[:, slot].unsqueeze(3).to_broadcast([P, 2, H, HD]), ALU.mult))
                c.done()
            normalise(0, 0)
            normalise(1, 1)

            def turn(n, slot, more):
                c = Count(v, s_c, n, OUT)
                wide = lambda i: vec[:, i, :].unsqueeze(1).to_broadcast([P, 2, D])
                v.wait_ge(s_mm, n + 1)
                v.wait_ge(s_x[slot], (n + (2 - slot)) * 8)
                c.then(nc.vector.tensor_tensor(t[:], ps_o[slot][:], wide(0), ALU.add))
                c.then(nc.vector.tensor_tensor(t[:], t[:], h0[:, slot], ALU.add))
                norm_begin(nc, c, stat, t, s_var)
                if more == 2:
                    normalise(n + 2, slot)
                norm_end(nc, c, stat, tn, t, s_rstd, 0, 1)
                c.then(nc.vector.tensor_tensor(tn[:], tn[:], wide(1), ALU.mult))
                if late(n, 2):
                    v.wait_ge(s_st[slot], (n - slot) * 8)
                c.then(nc.vector.tensor_tensor(h1[:, slot], tn[:], wide(2), ALU.add))
                c.done()
            rounds(v, turn)


def ffn(nc, g, name, rows, w1, b1, w2, func, hidden, loads, width, epilogue, per, norms, vectors, stores, outs):
    chunks = -(-hidden // P)
    with Phase(nc, name) as m:
        wa = m.sb("wa", [P, KC, hidden])
        wb = m.sb("wb", [P, chunks, D])
        ba = m.sb("ba", [P, chunks])
        vec = m.sb("vec", [P, len(vectors), D])
        hx = m.sb("hx", [P, 2, 2, D])
        xt = m.sb("xt", [P, 2, KC, 2 * P])
        ht = m.sb("ht", [P, 2, chunks, 2 * P])
        lin = m.sb("lin", [P, 2, max(1, len(loads)), 2, D])
        lout = m.sb("lout", [P, 2, len(outs), 2, D])
        tmp = m.sb("tmp", [P, 3, 2, D])
        stat = m.sb("stat", [P, max(1, norms), 20])
        ps_t = m.ps("ps_t", [P, KC, 2, P])
        ps_h = [m.ps(f"ps_h{i}", [P, 2 * P]) for i in range(4)]
        ps_y = [m.ps(f"ps_y{i}", [P, 2, D]) for i in range(2)]
        s_w, s_c, s_var, s_rstd, s_t, s_xt, s_up, s_act, s_y = (
            m.sem(k) for k in ("w", "c", "var", "rstd", "t", "xt", "up", "act", "y"))
        s_x, s_l, s_st = ([m.sem(f"{k}{i}") for i in range(2)] for k in ("x", "l", "st"))
        block = m.block()
        nw = 3 + len(vectors)
        size = lambda c: min(P, hidden - c * P)

        @block.sync
        def _(sp):
            def load(n, slot):
                if late(n, 2):
                    sp.wait_ge(s_t, n - 1)
                sp.dma_start(hx[:, slot], pair_rows(rows, n)).then_inc(s_x[slot], 16)
            load(0, 0)
            sp.dma_start(wa[:], w1.rearrange("(k p) n -> p k n", p=P)).then_inc(s_w, 16)
            sp.dma_start(wb[:], w2.rearrange("(c p) n -> p c n", p=P)).then_inc(s_w, 16)
            with nc.allow_non_contiguous_dma(reason="a bias by partition"):
                sp.dma_start(ba[:], b1.rearrange("(c p) -> p c", p=P)).then_inc(s_w, 16)
            for i, r in enumerate(vectors):
                sp.dma_start(vec[:, i, :], spread(r, D)).then_inc(s_w, 16)

            def store(n, slot):
                sp.wait_ge(s_c, n * per + per)
                for i, r in enumerate(outs):
                    sp.dma_start(pair_rows(r, n), lout[:, slot, i]).then_inc(s_st[slot], 16)

            def turn(n, slot, more):
                if more:
                    load(n + 1, 1 - slot)
                if loads and late(n, 2):
                    sp.wait_ge(s_c, n * per - per)
                for i, r in enumerate(loads):
                    sp.dma_start(lin[:, slot, i], pair_rows(r, n)).then_inc(s_l[slot], 16)
                if late(n, 1):
                    store(n - 1, 1 - slot)
            rounds(sp, turn)
            store(PAIRS - 1, 0)
            sp.wait_ge(s_st[0], 16 * len(outs) * (PAIRS // 2 + 1))
            sp.wait_ge(s_st[1], 16 * len(outs) * (PAIRS // 2))

        @block.gpsimd
        def _(pool):
            def turn(n, slot, more):
                for k in range(norms):
                    pool.wait_ge(s_var, n * norms + k + 1)
                    nc.gpsimd.tensor_tensor(stat[:, k, 18:20], stat[:, k, 16:18], g.minus_half[:], ALU.pow).then_inc(s_rstd, 1)
            if norms:
                rounds(pool, turn)

        @block.tensor
        def _(pe):
            def transposes(n, slot):
                pe.wait_ge(s_x[slot], (n + (2 - slot)) * 8)
                if late(n, 1):
                    pe.wait_ge(s_xt, n)
                for b in range(2):
                    for k in range(KC):
                        last = nc.tensor.transpose(ps_t[:, k, b, :], hx[:, slot, b, k * P:(k + 1) * P], g.ident[:])
                last.then_inc(s_t, 1)
            transposes(0, 0)
            pe.wait_ge(s_w, 16 * nw)

            def turn(n, slot, more):
                pe.wait_ge(s_xt, n + 1)
                for c in range(chunks):
                    if late(n, 1) or c >= 4:
                        pe.wait_ge(s_act, n * chunks + c - 3)
                    for k in range(KC):
                        last = nc.tensor.matmul(ps_h[c % 4][0:size(c), :], wa[:, k, c * P:c * P + size(c)], xt[:, slot, k, :],
                                                start=(k == 0), stop=(k == KC - 1))
                    last.then_inc(s_up, 1)
                if more:
                    transposes(n + 1, 1 - slot)
                if late(n, 2):
                    pe.wait_ge(s_c, n * per - per)
                for b in range(2):
                    for c in range(chunks):
                        if b == 0:
                            pe.wait_ge(s_act, n * chunks + c + 1)
                        last = nc.tensor.matmul(ps_y[slot][:, b, :], ht[0:size(c), slot, c, b * P:(b + 1) * P],
                                                wb[0:size(c), c, :], start=(c == 0), stop=(c == chunks - 1))
                last.then_inc(s_y, 1)
            rounds(pe, turn)

        @block.scalar
        def _(act):
            act.wait_ge(s_w, 16 * nw)

            def evac_xt(n, slot):
                act.wait_ge(s_t, n + 1)
                nc.scalar.activation(xt[:, slot, :, :], ps_t[:].rearrange("p k b n -> p k (b n)"), ACT.Copy).then_inc(s_xt, 1)
            evac_xt(0, 0)

            def turn(n, slot, more):
                if late(n, 2):
                    act.wait_ge(s_y, n - 1)
                for c in range(chunks):
                    act.wait_ge(s_up, n * chunks + c + 1)
                    nc.scalar.activation(ht[0:size(c), slot, c, :], ps_h[c % 4][0:size(c), :], func,
                                         bias=ba[0:size(c), c:c + 1]).then_inc(s_act, 1)
                if more:
                    evac_xt(n + 1, 1 - slot)
            rounds(act, turn)

        @block.vector
        def _(v):
            v.wait_ge(s_w, 16 * nw)

            def turn(n, slot, more):
                c = Count(v, s_c, n, per)
                v.wait_ge(s_y, n + 1)
                if loads:
                    v.wait_ge(s_l[slot], (n + (2 - slot)) * (8 * len(loads)))
                if late(n, 2):
                    v.wait_ge(s_st[slot], (n - slot) * (8 * len(outs)))
                epilogue(nc, g, c, n, ps_y[slot], [lin[:, slot, i] for i in range(len(loads))],
                         [vec[:, i, :] for i in range(len(vectors))], [tmp[:, i] for i in range(3)],
                         [lout[:, slot, i] for i in range(len(outs))], [stat[:, k] for k in range(norms)], s_var, s_rstd)
                c.done()
            rounds(v, turn)


def wide(row):
    return row.unsqueeze(1).to_broadcast([P, 2, D])


def after_graph(nc, g, c, n, y, loads, vecs, tmp, outs, stats, s_var, s_rstd):
    hid, x = loads
    b2, ln_g, ln_b, wr = vecs
    t, u, z = tmp
    c.then(nc.vector.tensor_tensor(t, y[:], wide(b2), ALU.add))
    c.then(nc.vector.tensor_tensor(t, t, hid, ALU.add))
    norm_pair(nc, g, c, stats[0], u, t, s_var, s_rstd, 0, 2)
    c.then(nc.vector.tensor_tensor(u, u, wide(ln_g), ALU.mult))
    c.then(nc.vector.tensor_tensor(u, u, wide(ln_b), ALU.add))
    c.then(nc.vector.tensor_tensor(z, u, x, ALU.add))
    norm_pair(nc, g, c, stats[1], outs[1], z, s_var, s_rstd, 1, 2)
    c.then(nc.vector.tensor_tensor(outs[0], z, outs[1], ALU.add))
    c.then(nc.vector.tensor_tensor(t, outs[1], wide(wr), ALU.mult))
    c.then(nc.vector.tensor_reduce(g.weight[:, bass.ds(n * 2, 2)], t, AX.X, ALU.add))


def weighted(nc, g, c, n, y, loads, vecs, tmp, outs, stats, s_var, s_rstd):
    c.then(nc.vector.tensor_tensor(tmp[0], y[:], wide(vecs[0]), ALU.add))
    c.then(nc.vector.tensor_tensor(outs[0], tmp[0], g.weight[:, bass.ds(n * 2, 2)].unsqueeze(2).to_broadcast([P, 2, D]), ALU.mult))


HALF_BITS = 16
DIGIT = 4
TRIES = (1 << DIGIT) - 1
assert NPAD < 1 << HALF_BITS


def keep_top(nc, g):
    with Phase(nc, "top") as m:
        br = m.sb("br", [P, 1])
        bits = m.sb("bits", [P, BLOCKS], I32)
        sign = m.sb("sign", [P, BLOCKS], I32)
        half_i = m.sb("half_i", [P, BLOCKS], I32)
        real = m.sb("real", [P, BLOCKS])
        high = m.sb("high", [P, BLOCKS])
        low = m.sb("low", [P, BLOCKS])
        t = m.sb("t", [P, BLOCKS])
        hit = m.sb("hit", [P, TRIES, BLOCKS])
        same = m.sb("same", [P, BLOCKS])
        cnt = m.sb("cnt", [P, TRIES])
        ones = m.sb("ones", [P, P])
        thr = m.sb("thr", [P, 3])
        tries = m.sb("tries", [P, TRIES])
        cand = m.sb("cand", [P, TRIES])
        passed = m.sb("passed", [P, TRIES])
        zeros = m.sb("zeros", [P, 3 * D])
        need = m.sb("need", [P, 1])
        digit = m.sb("digit", [P, 1])
        ps = m.ps("ps", [P, 512])
        s_in, s_v, s_pe, s_cnt, s_pool, s_zero = (m.sem(x) for x in ("in", "v", "pe", "cnt", "pool", "zero"))
        block = m.block()
        counts = 3 * (HALF_BITS // DIGIT) + 2
        per = zeros.shape[1] // D
        assert MAX_TILES % per == 0

        @block.sync
        def _(sp):
            sp.dma_start(br[:], g.br.rearrange("(a n) -> a n", a=1).to_broadcast([P, 1])).then_inc(s_in, 16)
            rows = g.slot_rows[0:SLOTS, :].rearrange("(a p r) d -> a p (r d)", p=P, r=per)
            sp.wait_ge(s_pool, 2)
            with sp.Fori(0, MAX_TILES // per) as i:
                sp.dma_start(rows[bass.ds(i, 1)].rearrange("a p d -> p (a d)"), zeros[:]).then_inc(s_zero, 16)
            sp.wait_ge(s_zero, 16 * (MAX_TILES // per))

        @block.gpsimd
        def _(pool):
            nc.gpsimd.iota(tries[:], [[1, TRIES]], 1, 0, allow_small_or_imprecise_dtypes=True).then_inc(s_pool, 1)
            nc.gpsimd.memset(zeros[:], 0.0).then_inc(s_pool, 1)

        @block.tensor
        def _(pe):
            with pe.Fori(0, counts) as i:
                pe.wait_ge(s_cnt, i + 1)
                nc.tensor.matmul(ps[:, 0:TRIES], ones[:], cnt[:], start=True, stop=True).then_inc(s_pe, 1)

        @block.vector
        def _(v):
            ch = Chain(v, s_v)
            ts, tt = nc.vector.tensor_scalar, nc.vector.tensor_tensor
            ch.after(nc.vector.memset(ones[:], 1.0))
            ch.after(nc.vector.memset(thr[:], 0.0))
            v.wait_ge(s_in, 16)
            v.wait_ge(s_pool, 1)
            ch.after(ts(g.weight[:], g.weight[:], br[:, 0:1], None, ALU.add))
            ch.after(ts(real[:], g.node[:], float(N), None, ALU.is_lt))
            w = g.weight[:].bitcast(I32)
            ch.after(ts(sign[:], w, 31, None, ALU.arith_shift_right))
            ch.after(ts(sign[:], sign[:], -2147483648, None, ALU.bitwise_or))
            ch.after(tt(bits[:], w, sign[:], ALU.bitwise_xor))
            for half, op, by in ((high, ALU.logical_shift_right, 16), (low, ALU.bitwise_and, 0xFFFF)):
                ch.after(ts(half_i[:], bits[:], by, None, op))
                ch.after(ts(half[:], half_i[:], 1.0, None, ALU.add))
                ch.after(tt(half[:], half[:], real[:], ALU.mult))
                ch.after(ts(half[:], half[:], -1.0, None, ALU.add))
            ch.after(nc.vector.memset(need[:], float(KEEP)))
            done = [0]

            def total():
                nc.vector.tensor_reduce(cnt[:], hit[:], AX.X, ALU.add).then_inc(s_cnt, 1)
                done[0] += 1
                v.wait_ge(s_pe, done[0])

            def search(val, at, op, pred):
                for shift in range(HALF_BITS - DIGIT, -1, -DIGIT):
                    ch.after(ts(cand[:], tries[:], float(1 << shift), thr[:, at:at + 1], ALU.mult, ALU.add))
                    ch.after(tt(hit[:], val[:].unsqueeze(1).to_broadcast([P, TRIES, BLOCKS]),
                                cand[:].unsqueeze(2).to_broadcast([P, TRIES, BLOCKS]), op))
                    total()
                    ch.after(ts(passed[:], ps[:, 0:TRIES], need[:, 0:1], None, pred))
                    ch.after(nc.vector.tensor_reduce(digit[:], passed[:], AX.X, ALU.add))
                    ch.after(ts(digit[:], digit[:], float(1 << shift), None, ALU.mult))
                    ch.after(tt(thr[:, at:at + 1], thr[:, at:at + 1], digit[:], ALU.add))

            def above(val, at):
                ch.after(ts(hit[:, 0, :], val[:], thr[:, at:at + 1], None, ALU.is_gt))
                ch.after(tt(g.keep[:], g.keep[:], hit[:, 0, :], ALU.add))
                total()
                ch.after(tt(need[:], need[:], ps[:, 0:1], ALU.subtract))

            def among(val, at):
                ch.after(ts(t[:], val[:], thr[:, at:at + 1], None, ALU.is_equal))

            ch.after(nc.vector.memset(g.keep[:], 0.0))
            search(high, 0, ALU.is_ge, ALU.is_ge)
            above(high, 0)
            among(high, 0)
            ch.after(ts(low[:], low[:], 1.0, None, ALU.add))
            ch.after(tt(low[:], low[:], t[:], ALU.mult))
            ch.after(ts(low[:], low[:], -1.0, None, ALU.add))
            search(low, 1, ALU.is_ge, ALU.is_ge)
            above(low, 1)
            among(low, 1)
            ch.after(ts(same[:], t[:], -float(NPAD), float(NPAD), ALU.mult, ALU.add))
            ch.after(tt(same[:], same[:], g.node[:], ALU.add))
            search(same, 2, ALU.is_lt, ALU.is_lt)
            ch.after(ts(hit[:, 0, :], same[:], thr[:, 2:3], None, ALU.is_le))
            ch.after(tt(g.keep[:], g.keep[:], hit[:, 0, :], ALU.add))
            assert done[0] == counts


def project_heads(nc, g, s_dst):
    with Phase(nc, "hds") as m:
        w = m.sb("w", [P, KC, D])
        vec = m.sb("vec", [P, 2, D])
        r = m.sb("r", [P, 2, 2, 2, D])
        x2 = m.sb("x2", [P, 2, 2, D])
        xn = m.sb("xn", [P, 2, 2, D])
        xt = m.sb("xt", [P, 2, KC, 2, P])
        hh = m.sb("hh", [P, 2, 2, D])
        att = m.sb("att", [P, 2, 2, D])
        src = m.sb("src", [P, 2, 2, H])
        stat = m.sb("stat", [P, 2, 20])
        ps_t = [m.ps(f"ps_t{i}", [P, 2, KC, P]) for i in range(2)]
        ps_o = [m.ps(f"ps_o{i}", [P, 2, D]) for i in range(2)]
        s_w, s_ln, s_var, s_rstd, s_t, s_xt, s_mm, s_hh, s_a = (
            m.sem(k) for k in ("w", "ln", "var", "rstd", "t", "xt", "mm", "hh", "a"))
        s_x, s_xnst, s_hst, s_sst = ([m.sem(f"{k}{i}") for i in range(2)] for k in ("x", "xnst", "hst", "sst"))
        block = m.block()
        LN, AT = 1 + LN_STEPS, 2

        @block.sync
        def _(sp):
            def load(n, slot):
                sp.dma_start(r[:, slot, 0], pair_rows(g.resid, n)).then_inc(s_x[slot], 16)
                sp.dma_start(r[:, slot, 1], pair_rows(g.token_y, n)).then_inc(s_x[slot], 16)
            load(0, 0)
            load(1, 1)
            sp.dma_start(w[:], g.W.rearrange("(k p) n -> p k n", p=P)).then_inc(s_w, 16)
            for i, a in enumerate((g.a_src, g.a_dst)):
                sp.dma_start(vec[:, i, :], spread(a.rearrange("h d -> (h d)"), D)).then_inc(s_w, 16)

            def turn(n, slot, more):
                sp.wait_ge(s_ln, n * LN + LN)
                if more == 2:
                    load(n + 2, slot)
                sp.dma_start(pair_rows(g.norm, n), xn[:, slot]).then_inc(s_xnst[slot], 16)
                sp.dma_start(pair_rows(g.x2, n), x2[:, slot]).then_inc(s_xnst[slot], 16)
                sp.wait_ge(s_hh, n + 1)
                sp.dma_start(pair_rows(g.v_rows, n), hh[:, slot]).then_inc(s_hst[slot], 16)
                if late(n, 1):
                    store_src(n - 1, 1 - slot)

            def store_src(n, slot):
                sp.wait_ge(s_a, n * AT * 2 + 2)
                sp.dma_start(pair_rows(g.s_src, n), src[:, slot]).then_inc(s_sst[slot], 16)
            rounds(sp, turn)
            store_src(PAIRS - 1, 0)
            for i, k in enumerate((PAIRS // 2 + 1, PAIRS // 2)):
                sp.wait_ge(s_xnst[i], 32 * k)
                sp.wait_ge(s_hst[i], 16 * k)
                sp.wait_ge(s_sst[i], 16 * k)

        @block.gpsimd
        def _(pool):
            def turn(n, slot, more):
                pool.wait_ge(s_var, n + 1)
                nc.gpsimd.tensor_tensor(stat[:, slot, 18:20], stat[:, slot, 16:18], g.minus_half[:], ALU.pow).then_inc(s_rstd, 1)
            rounds(pool, turn)

        @block.vector
        def _(v):
            def begin(n, slot):
                c = Count(v, s_ln, n, LN)
                v.wait_ge(s_x[slot], (n + (2 - slot)) * 16)
                if late(n, 2):
                    v.wait_ge(s_xnst[slot], (n - slot) * 16)
                    v.wait_ge(s_t, n - 1)
                for b in range(2):
                    ins = nc.vector.scalar_tensor_tensor(x2[:, slot, b, :], r[:, slot, 1, b, :],
                                                         g.keep[:, bass.ds(n * 2 + b, 1)], r[:, slot, 0, b, :],
                                                         ALU.mult, ALU.add)
                c.then(ins)
                norm_begin(nc, c, stat[:, slot], x2[:, slot], s_var)
                return c

            def end(c, slot):
                norm_end(nc, c, stat[:, slot], xn[:, slot], x2[:, slot], s_rstd, 0, 1)
                c.done()

            def attend(n, slot):
                v.wait_ge(s_hh, n + 1)
                c = Count(v, s_a, n, 2 * AT)
                if late(n, 2):
                    v.wait_ge(s_sst[slot], (n - slot) * 8)
                outs = (src[:, slot], s_dst[:, bass.ds(n * 2, 2), :])
                for i in range(2):
                    c.then(nc.vector.tensor_tensor(att[:, i], hh[:, slot], wide(vec[:, i, :]), ALU.mult))
                    c.then(nc.vector.tensor_reduce(outs[i], att[:, i].rearrange("p b (h d) -> p b h d", h=H), AX.X, ALU.add))
                c.done()

            end(begin(0, 0), 0)
            v.wait_ge(s_w, 48)

            def turn(n, slot, more):
                if more:
                    c = begin(n + 1, 1 - slot)
                if late(n, 1):
                    attend(n - 1, 1 - slot)
                if more:
                    end(c, 1 - slot)
            rounds(v, turn)
            attend(PAIRS - 1, 0)

        @block.tensor
        def _(pe):
            def transposes(n, slot):
                pe.wait_ge(s_ln, n * LN + LN)
                if late(n, 2):
                    pe.wait_ge(s_xt, n - 1)
                for b in range(2):
                    for k in range(KC):
                        last = nc.tensor.transpose(ps_t[slot][:, b, k, :], xn[:, slot, b, k * P:(k + 1) * P], g.ident[:])
                last.then_inc(s_t, 1)
            transposes(0, 0)
            pe.wait_ge(s_w, 48)

            def turn(n, slot, more):
                pe.wait_ge(s_xt, n + 1)
                if late(n, 2):
                    pe.wait_ge(s_hh, n - 1)
                for b in range(2):
                    for k in range(KC):
                        last = nc.tensor.matmul(ps_o[slot][:, b, :], xt[:, slot, k, b, :], w[:, k, :],
                                                start=(k == 0), stop=(k == KC - 1))
                last.then_inc(s_mm, 1)
                if more:
                    transposes(n + 1, 1 - slot)
            rounds(pe, turn)

        @block.scalar
        def _(act):
            def evac_xt(n, slot):
                act.wait_ge(s_t, n + 1)
                if late(n, 2):
                    act.wait_ge(s_mm, n - 1)
                nc.scalar.activation(xt[:, slot].rearrange("p k b n -> p b k n"), ps_t[slot][:], ACT.Copy).then_inc(s_xt, 1)
            evac_xt(0, 0)

            def turn(n, slot, more):
                act.wait_ge(s_mm, n + 1)
                if late(n, 2):
                    act.wait_ge(s_hst[slot], (n - slot) * 8)
                    act.wait_ge(s_a, n * 2 * AT - 2 * AT)
                nc.scalar.activation(hh[:, slot], ps_o[slot][:], ACT.Copy).then_inc(s_hh, 1)
                if more:
                    evac_xt(n + 1, 1 - slot)
            rounds(act, turn)


def graph2_out(nc, g, acc, logits):
    with Phase(nc, "out2") as m:
        w = m.sb("w", [P, KC, EXPERTS])
        vec = m.sb("vec", [P, 2, D])
        lin = m.sb("lin", [P, 2, 2, 2, D])
        rec = m.sb("rec", [P, 2, H])
        t = m.sb("t", [P, 2, 2, D])
        u = m.sb("u", [P, 2, D])
        z = m.sb("z", [P, 2, 2, D])
        low = m.sb("low", [P, 2, 2, D])
        el = m.sb("el", [P, 2, 2, D])
        lout = m.sb("lout", [P, 2, 2, 2, D])
        xt = m.sb("xt", [P, 2, KC, 2, P])
        stat = m.sb("stat", [P, 2, 20])
        ps_t = [m.ps(f"ps_t{i}", [P, 2, KC, P]) for i in range(2)]
        ps_l = [m.ps(f"ps_l{i}", [P, 2, EXPERTS]) for i in range(2)]
        s_w, s_a, s_c, s_var, s_rstd, s_var2, s_rstd2, s_t, s_xt, s_mm, s_log, s_low, s_el = (
            m.sem(k) for k in ("w", "a", "c", "var", "rstd", "var2", "rstd2", "t", "xt", "mm", "log", "low", "el"))
        s_norm, s_x2, s_st = ([m.sem(f"{k}{i}") for i in range(2)] for k in ("norm", "x2", "st"))
        block = m.block()
        PER_A, PER = 6 + LN_STEPS, 2 + LN_STEPS

        @block.sync
        def _(sp):
            sp.dma_start(w[:], g.router_t.rearrange("(k p) n -> p k n", p=P)).then_inc(s_w, 16)
            for i, a in enumerate((g.gamma, g.beta)):
                sp.dma_start(vec[:, i, :], spread(a, D)).then_inc(s_w, 16)

            def store(n, slot):
                sp.wait_ge(s_c, n * PER + PER)
                sp.dma_start(pair_rows(g.x3, n), lout[:, slot, 0]).then_inc(s_st[slot], 16)
                sp.dma_start(pair_rows(g.x3n, n), lout[:, slot, 1]).then_inc(s_st[slot], 16)

            def turn(n, slot, more):
                if more == 2:
                    sp.wait_ge(s_a, n * PER_A + PER_A)
                    load_norm(n + 2, slot)
                if late(n, 1):
                    store(n - 1, 1 - slot)
                if more:
                    load_x2(n + 1, 1 - slot)

            def load_norm(n, slot):
                sp.dma_start(lin[:, slot, 0], pair_rows(g.norm, n)).then_inc(s_norm[slot], 16)

            def load_x2(n, slot):
                sp.dma_start(lin[:, slot, 1], pair_rows(g.x2, n)).then_inc(s_x2[slot], 16)

            load_norm(0, 0)
            load_norm(1, 1)
            load_x2(0, 0)
            rounds(sp, turn)
            store(PAIRS - 1, 0)
            sp.wait_ge(s_st[0], 32 * (PAIRS // 2 + 1))
            sp.wait_ge(s_st[1], 32 * (PAIRS // 2))

        @block.gpsimd
        def _(pool):
            def turn(n, slot, more):
                if more:
                    root(n + 1, 0, s_var, s_rstd)
                root(n, 1, s_var2, s_rstd2)

            def root(n, k, variance, done):
                pool.wait_ge(variance, n + 1)
                nc.gpsimd.tensor_tensor(stat[:, k, 18:20], stat[:, k, 16:18], g.minus_half[:], ALU.pow).then_inc(done, 1)
            root(0, 0, s_var, s_rstd)
            rounds(pool, turn)

        @block.scalar
        def _(act):
            def exp(n, slot):
                act.wait_ge(s_low, n + 1)
                if late(n, 2):
                    act.wait_ge(s_c, n * PER - PER)
                nc.scalar.activation(el[:, slot], low[:, slot], ACT.Exp).then_inc(s_el, 1)
            exp(0, 0)

            def turn(n, slot, more):
                if more:
                    exp(n + 1, 1 - slot)
                act.wait_ge(s_t, n + 1)
                if late(n, 2):
                    act.wait_ge(s_mm, n - 1)
                nc.scalar.activation(xt[:, slot].rearrange("p k b n -> p b k n"), ps_t[slot][:], ACT.Copy).then_inc(s_xt, 1)
                act.wait_ge(s_mm, n + 1)
                nc.scalar.activation(logits[:, bass.ds(n * 2, 2), :], ps_l[slot][:], ACT.Copy).then_inc(s_log, 1)
            rounds(act, turn)

        @block.tensor
        def _(pe):
            pe.wait_ge(s_w, 48)

            def turn(n, slot, more):
                pe.wait_ge(s_c, n * PER + PER)
                if late(n, 2):
                    pe.wait_ge(s_xt, n - 1)
                for b in range(2):
                    for k in range(KC):
                        last = nc.tensor.transpose(ps_t[slot][:, b, k, :], lout[:, slot, 1, b, k * P:(k + 1) * P], g.ident[:])
                last.then_inc(s_t, 1)
                pe.wait_ge(s_xt, n + 1)
                if late(n, 2):
                    pe.wait_ge(s_log, n - 1)
                for b in range(2):
                    for k in range(KC):
                        last = nc.tensor.matmul(ps_l[slot][:, b, :], xt[:, slot, k, b, :], w[:, k, :],
                                                start=(k == 0), stop=(k == KC - 1))
                last.then_inc(s_mm, 1)
            rounds(pe, turn)

        @block.vector
        def _(v):
            v.wait_ge(s_w, 48)

            tt = nc.vector.tensor_tensor

            def a_begin(n, slot):
                c = Count(v, s_a, n, PER_A)
                a = acc[:, bass.ds(n * 2, 2), :]
                c.then(nc.vector.tensor_scalar(rec[:], a[:, :, D:AGG], 0.5, None, ALU.max))
                c.then(nc.vector.reciprocal(rec[:], rec[:]))
                c.then(tt(t[:, 0].rearrange("p b (h d) -> p b h d", h=H), a[:, :, 0:D].rearrange("p b (h d) -> p b h d", h=H),
                          rec[:].unsqueeze(3).to_broadcast([P, 2, H, HD]), ALU.mult))
                v.wait_ge(s_norm[slot], (n + (2 - slot)) * 8)
                c.then(tt(t[:, 0], t[:, 0], lin[:, slot, 0], ALU.add))
                norm_begin(nc, c, stat[:, 0], t[:, 0], s_var)
                return c

            def a_end(c, n, slot):
                norm_end(nc, c, stat[:, 0], u[:], t[:, 0], s_rstd, 0, 1)
                c.then(tt(u[:], u[:], wide(vec[:, 0, :]), ALU.mult))
                c.then(tt(z[:, slot], u[:], wide(vec[:, 1, :]), ALU.add))
                if late(n, 2):
                    v.wait_ge(s_el, n - 1)
                nc.vector.tensor_scalar(low[:, slot], z[:, slot], 0.0, None, ALU.min).then_inc(s_low, 1)
                c.done()

            def b_begin(n, slot):
                c = Count(v, s_c, n, PER)
                v.wait_ge(s_el, n + 1)
                c.then(nc.vector.scalar_tensor_tensor(t[:, 1].rearrange("p b d -> p (b d)"),
                                                      el[:, slot].rearrange("p b d -> p (b d)"), -1.0,
                                                      z[:, slot].rearrange("p b d -> p (b d)"), ALU.add, ALU.max))
                if late(n, 2):
                    v.wait_ge(s_st[slot], (n - slot) * 16)
                    v.wait_ge(s_t, n - 1)
                v.wait_ge(s_x2[slot], (n + (2 - slot)) * 8)
                c.then(tt(lout[:, slot, 0], t[:, 1], lin[:, slot, 1], ALU.add))
                norm_begin(nc, c, stat[:, 1], lout[:, slot, 0], s_var2)
                return c

            def b_end(c, slot):
                norm_end(nc, c, stat[:, 1], lout[:, slot, 1], lout[:, slot, 0], s_rstd2, 0, 1)
                c.done()

            a_end(a_begin(0, 0), 0, 0)

            def turn(n, slot, more):
                if more:
                    a = a_begin(n + 1, 1 - slot)
                b = b_begin(n, slot)
                if more:
                    a_end(a, n + 1, 1 - slot)
                b_end(b, slot)
            rounds(v, turn)
            v.wait_ge(s_log, PAIRS)


def route(nc, g, logits):
    with Phase(nc, "route") as m:
        B, X = BLOCKS, EXPERTS
        col = m.sb("col", [P, B, X])
        mx = m.sb("mx", [P, B])
        e = m.sb("e", [P, B, X])
        eq = m.sb("eq", [P, B, X])
        one = [m.sb(f"one{i}", [P, B, X]) for i in range(2)]
        pr = m.sb("pr", [P, 3, B])
        real = m.sb("real", [P, B])
        both = m.sb("both", [P, B, X])
        before = m.sb("before", [P, P])
        ones = m.sb("ones", [P, P])
        rank = m.sb("rank", [P, B, X])
        tot = m.sb("tot", [P, B, X])
        run = m.sb("run", [P, B + 1, X])
        zero = m.sb("zero", [P, B])
        cnt_i = m.sb("cnt_i", [P, X], I32)
        tiles = m.sb("tiles", [P, X])
        ends = m.sb("ends", [P, X + 1])
        base = m.sb("base", [P, X])
        tile_no = m.sb("tile_no", [P, MAX_TILES])
        over = m.sb("over", [P, MAX_TILES])
        tile_f = m.sb("tile_f", [P, MAX_TILES])
        pos = m.sb("pos", [P, 2, B])
        trash = m.sb("trash", [P, B])
        tmp = m.sb("tmp", [P, B, X])
        ps_r = m.ps("ps_r", [P, 512])
        ps_o = m.ps("ps_o", [P, 512])
        s_i, s_v, s_pe, s_m = (m.sem(x) for x in ("i", "v", "pe", "m"))
        block = m.block()

        @block.sync
        def _(sp):
            for e in range(EXPERTS):
                for i, t in enumerate((g.w1_t, g.w3_t)):
                    sp.dma_start(g.w13[:, e, :, i, :], t[e].rearrange("(k p) h -> p k h", p=P)).then_inc(g.s_experts, 16)
                full = (EC - 1) * P
                sp.dma_start(g.w2_sb[:, e, 0:EC - 1, :], g.w2_t[e, 0:full].rearrange("(c p) d -> p c d", p=P)).then_inc(g.s_experts, 16)
                sp.dma_start(g.w2_sb[0:EH - full, e, EC - 1, :], g.w2_t[e, full:EH]).then_inc(g.s_experts, 16)

        @block.gpsimd
        def _(pool):
            nc.gpsimd.iota(col[:], [[0, B], [1, X]], 0, 0, allow_small_or_imprecise_dtypes=True).then_inc(s_i, 1)
            nc.gpsimd.iota(tile_no[:], [[1, MAX_TILES]], 0, 0, allow_small_or_imprecise_dtypes=True).then_inc(s_i, 1)
            nc.gpsimd.memset(before[:], 1.0).then_inc(s_i, 1)
            pool.wait_ge(s_i, 3)
            nc.gpsimd.affine_select(out=before[:], in_=before[:], compare_op=ALU.is_gt, fill=0.0,
                                    base=0, pattern=[[1, P]], channel_multiplier=-1).then_inc(s_i, 1)

        @block.tensor
        def _(pe):
            pe.wait_ge(s_i, 4)
            pe.wait_ge(s_m, 1)
            flat = both[:].rearrange("p b x -> p (b x)")
            nc.tensor.matmul(ps_r[:, 0:B * X], before[:], flat, start=True, stop=True)
            nc.tensor.matmul(ps_o[:, 0:B * X], ones[:], flat, start=True, stop=True).then_inc(s_pe, 1)

        @block.vector
        def _(v):
            ch = Chain(v, s_v)
            ts, tt, red = nc.vector.tensor_scalar, nc.vector.tensor_tensor, nc.vector.tensor_reduce
            wide_x = lambda a: a.unsqueeze(2).to_broadcast([P, B, X])
            ch.after(nc.vector.memset(ones[:], 1.0))
            ch.after(nc.vector.memset(zero[:], 0.0))
            ch.after(nc.vector.memset(run[:], 0.0))
            ch.after(nc.vector.memset(ends[:], 0.0))
            ch.after(ts(real[:], g.node[:], float(N), None, ALU.is_lt))
            v.wait_ge(s_i, 4)
            ch.after(red(mx[:], logits[:], AX.X, ALU.max))
            ch.after(tt(e[:], logits[:], wide_x(mx[:]), ALU.subtract))
            v.sem_inc(g.s_exp, 1)
            v.wait_ge(g.s_exp, 2)
            ch.after(tt(e[:], g.exp_out[:], wide_x(real[:]), ALU.mult))
            ch.after(red(pr[:, 2], g.exp_out[:], AX.X, ALU.add))
            ch.after(nc.vector.reciprocal(pr[:, 2], pr[:, 2]))
            ch.after(tt(e[:], g.exp_out[:], wide_x(pr[:, 2]), ALU.mult))
            for i in range(2):
                ch.after(red(pr[:, i], e[:], AX.X, ALU.max))
                ch.after(tt(eq[:], e[:], wide_x(pr[:, i]), ALU.is_lt))
                ch.after(ts(eq[:], eq[:], float(X), None, ALU.mult))
                ch.after(tt(eq[:], eq[:], col[:], ALU.add))
                ch.after(red(mx[:], eq[:], AX.X, ALU.min))
                ch.after(tt(one[i][:], col[:], wide_x(mx[:]), ALU.is_equal))
                ch.after(ts(eq[:], one[i][:], -4.0, None, ALU.mult))
                ch.after(tt(e[:], e[:], eq[:], ALU.add))
                ch.after(tt(one[i][:], one[i][:], wide_x(real[:]), ALU.mult))
            ch.after(tt(pr[:, 2], pr[:, 0], pr[:, 1], ALU.add))
            ch.after(ts(pr[:, 2], pr[:, 2], 1e-9, None, ALU.add))
            ch.after(nc.vector.reciprocal(pr[:, 2], pr[:, 2]))
            for i in range(2):
                ch.after(tt(g.gate[:, i], pr[:, i], pr[:, 2], ALU.mult))
            tt(both[:], one[0][:], one[1][:], ALU.add).then_inc(s_m, 1)
            v.wait_ge(s_pe, 1)
            ch.after(nc.vector.tensor_copy(rank[:].rearrange("p b x -> p (b x)"), ps_r[:, 0:B * X]))
            ch.after(nc.vector.tensor_copy(tot[:].rearrange("p b x -> p (b x)"), ps_o[:, 0:B * X]))
            for x in range(X):
                ch.after(nc.vector.tensor_tensor_scan(run[:, 1:B + 1, x], zero[:], tot[:, :, x], 0.0, ALU.add, ALU.add))
            ch.after(ts(cnt_i[:], run[:, B, :], float(P - 1), None, ALU.add))
            ch.after(ts(cnt_i[:], cnt_i[:], 7, None, ALU.arith_shift_right))
            ch.after(nc.vector.tensor_copy(tiles[:], cnt_i[:]))
            ch.after(nc.vector.tensor_tensor_scan(ends[:, 1:X + 1], zero[:, 0:X], tiles[:], 0.0, ALU.add, ALU.add))
            ch.after(ts(base[:], ends[:, 0:X], float(P), None, ALU.mult))
            ch.after(tt(rank[:], rank[:], run[:, 0:B, :], ALU.add))
            ch.after(tt(rank[:], rank[:], base[:].unsqueeze(1).to_broadcast([P, B, X]), ALU.add))
            ch.after(ts(trash[:], g.node[:], float(SLOTS - N), None, ALU.add))
            ch.after(ts(real[:], real[:], -1.0, 1.0, ALU.mult, ALU.add))
            ch.after(tt(trash[:], trash[:], real[:], ALU.mult))
            for i in range(2):
                ch.after(tt(tmp[:], one[i][:], rank[:], ALU.mult))
                ch.after(red(pos[:, i], tmp[:], AX.X, ALU.add))
                ch.after(nc.vector.tensor_copy(g.from_slot[:, :, i], pos[:, i]))
                ch.after(tt(pos[:, i], pos[:, i], trash[:], ALU.add))
                if i == 1:
                    ch.after(ts(real[:], real[:], float(NPAD - N), None, ALU.mult))
                    ch.after(tt(pos[:, i], pos[:, i], real[:], ALU.add))
                ch.after(nc.vector.tensor_copy(g.to_slot[:, :, i], pos[:, i]))
            ch.after(nc.vector.memset(tile_f[:], 0.0))
            for x in range(1, X):
                ch.after(ts(over[:], tile_no[:], ends[:, x:x + 1], None, ALU.is_ge))
                ch.after(tt(tile_f[:], tile_f[:], over[:], ALU.add))
            ch.after(nc.vector.tensor_copy(g.tile_expert[0:1, 0:MAX_TILES], tile_f[0:1, :]))

        @block.scalar
        def _(act):
            act.wait_ge(g.s_exp, 1)
            nc.scalar.activation(g.exp_out[:], e[:], ACT.Exp).then_inc(g.s_exp, 1)


def scatter_tokens(nc, g):
    with Phase(nc, "scat") as m:
        x = m.sb("x", [P, 2, 2, D])
        idx = m.sb("idx", [P, 2, 2, 2], I32)
        s_idx = m.sem("idx")
        s_x = [m.sem(f"x{i}") for i in range(2)]
        s_st = m.sems_of_pool("st", 2)
        block = m.block()

        @block.sync
        def _(sp):
            def turn(n, slot, more):
                if late(n, 2):
                    sp.wait_ge(s_st[slot], (n - slot) * 32)
                sp.dma_start(x[:, slot], pair_rows(g.x3n, n)).then_inc(s_x[slot], 16)
            rounds(sp, turn)

        @block.vector
        def _(v):
            def turn(n, slot, more):
                if late(n, 2):
                    v.wait_ge(s_st[slot], (n - slot) * 32)
                nc.vector.tensor_copy(idx[:, slot], g.to_slot[:, bass.ds(n * 2, 2), :]).then_inc(s_idx, 1)
            rounds(v, turn)

        @block.gpsimd
        def _(pool):
            def turn(n, slot, more):
                pool.wait_ge(s_x[slot], (n + (2 - slot)) * 8)
                pool.wait_ge(s_idx, n + 1)
                pool.nop(nofuse=True)
                for b in range(2):
                    for i in range(2):
                        nc.gpsimd.indirect_dma_start(g.slot_rows, bass.IndirectOffsetOnAxis(idx[:, slot, b, i:i + 1], 0),
                                                     x[:, slot, b, :], None).then_inc(s_st[slot], 16)
            rounds(pool, turn)
            pool.wait_ge(s_st[0], 64 * (PAIRS // 2 + 1))
            pool.wait_ge(s_st[1], 64 * (PAIRS // 2))


def experts(nc, g):
    with Phase(nc, "moe") as m:
        w13, w2 = g.w13, g.w2_sb
        x = m.sb("x", [P, 2, D])
        xt = m.sb("xt", [P, 2, KC, P])
        act_ = m.sb("act", [P, EH])
        gl = m.sb("gl", [P, 2, EH])
        gt = m.sb("gt", [P, EC, P])
        y = m.sb("y", [P, 2, D])
        ps_x = m.ps("ps_x", [P, KC, P])
        ps_h = [m.ps(f"ps_h{i}", [P, 512]) for i in range(4)]
        ps_g = [m.ps(f"ps_g{i}", [P, 4, P]) for i in range(2)]
        ps_y = m.ps("ps_y", [P, D])
        s_xt, s_xtc, s_up, s_silu, s_mul, s_gt, s_gtc, s_y, s_yc = (
            m.sem(k) for k in ("xt", "xtc", "up", "silu", "mul", "gt", "gtc", "y", "yc"))
        s_x, s_st = ([m.sem(f"{k}{i}") for i in range(2)] for k in ("x", "st"))
        block = m.block()
        T = MAX_TILES
        tile_rows = lambda dram, n: dram[bass.ds(n * P, P), :]
        rest = EH - (EC - 1) * P

        @block.sync
        def _(sp):
            def load(n, slot):
                if late(n, 2):
                    sp.wait_ge(s_xt, n - 1)
                sp.dma_start(x[:, slot], tile_rows(g.slot_rows, n)).then_inc(s_x[slot], 16)
            load(0, 0)
            load(1, 1)

            def turn(n, slot, more):
                if late(n, 1) and more:
                    load(n + 1, 1 - slot)
                if late(n, 1):
                    sp.wait_ge(s_yc, n)
                    sp.dma_start(tile_rows(g.slot_y, n - 1), y[:, 1 - slot]).then_inc(s_st[1 - slot], 16)
            rounds(sp, turn, T)
            sp.wait_ge(s_yc, T)
            sp.dma_start(tile_rows(g.slot_y, T - 1), y[:, 0]).then_inc(s_st[0], 16)
            sp.wait_ge(s_st[0], 16 * (T // 2 + 1))
            sp.wait_ge(s_st[1], 16 * (T // 2))

        @block.tensor
        def _(pe):
            def expert_of(n):
                return nc.values_load_multi_w_load_instructions(
                    g.tile_expert[0:1, bass.ds(n, 1)], [mybir.EngineType.PE], min_val=0, max_val=EXPERTS - 1,
                    skip_runtime_bounds_check_because="made on the chip, at most EXPERTS - 1")[1][0]

            def transposes(n, slot):
                pe.wait_ge(s_x[slot], (n + (2 - slot)) * 8)
                if late(n, 1):
                    pe.wait_ge(s_xtc, n)
                for k in range(KC):
                    last = nc.tensor.transpose(ps_x[:, k, :], x[:, slot, k * P:(k + 1) * P], g.ident[:])
                last.then_inc(s_xt, 1)

            def down(n, slot):
                e = expert_of(n)
                if late(n, 1):
                    pe.wait_ge(s_yc, n)
                for c in range(EC):
                    if c % 4 == 0:
                        pe.wait_ge(s_gtc, n * 2 + c // 4 + 1)
                    size = P if c < EC - 1 else rest
                    last = nc.tensor.matmul(ps_y[:], gt[0:size, c, :], w2[0:size, :, c, :][:, bass.ds(e, 1), :].rearrange("p a d -> p (a d)"),
                                            start=(c == 0), stop=(c == EC - 1))
                last.then_inc(s_y, 1)

            transposes(0, 0)
            pe.wait_ge(g.s_experts, 16 * 4 * EXPERTS)

            def turn(n, slot, more):
                e = expert_of(n)
                pe.wait_ge(s_xtc, n + 1)
                for i in range(2):
                    for hf in range(2):
                        if late(n, 1):
                            pe.wait_ge(s_mul, n * 2 - 1 + hf)
                        for k in range(KC):
                            last = nc.tensor.matmul(ps_h[2 * i + hf][:, 0:EHALF], xt[:, slot, k, :],
                                                    w13[:, :, k, i, hf * EHALF:(hf + 1) * EHALF][:, bass.ds(e, 1), :].rearrange("p a h -> p (a h)"),
                                                    start=(k == 0), stop=(k == KC - 1))
                        last.then_inc(s_up, 1)
                if more:
                    transposes(n + 1, 1 - slot)
                if late(n, 1):
                    down(n - 1, 1 - slot)
                pe.wait_ge(s_mul, n * 2 + 2)
                for c in range(EC):
                    size = P if c < EC - 1 else rest
                    last = nc.tensor.transpose(ps_g[c // 4][0:size, c % 4, :], gl[:, slot, c * P:c * P + size], g.ident[:])
                    if c in (3, EC - 1):
                        last.then_inc(s_gt, 1)
            rounds(pe, turn, T)
            down(T - 1, 0)

        @block.scalar
        def _(act):
            def evac_xt(n, slot):
                act.wait_ge(s_xt, n + 1)
                nc.scalar.activation(xt[:, slot], ps_x[:], ACT.Copy).then_inc(s_xtc, 1)
            evac_xt(0, 0)

            def turn(n, slot, more):
                for hf in range(2):
                    act.wait_ge(s_up, n * 4 + hf + 1)
                    if late(n, 1):
                        act.wait_ge(s_mul, n * 2 - 1 + hf)
                    nc.scalar.activation(act_[:, hf * EHALF:(hf + 1) * EHALF], ps_h[hf][:, 0:EHALF], ACT.Silu).then_inc(s_silu, 1)
                if more:
                    evac_xt(n + 1, 1 - slot)
                if late(n, 1):
                    act.wait_ge(s_y, n)
                    if late(n, 3):
                        act.wait_ge(s_st[1 - slot], (n - 1 - (1 - slot)) * 8)
                    nc.scalar.activation(y[:, 1 - slot], ps_y[:], ACT.Copy).then_inc(s_yc, 1)
                for i in range(2):
                    act.wait_ge(s_gt, n * 2 + i + 1)
                    if i == 0:
                        nc.scalar.activation(gt[:, 0:4, :], ps_g[0][:], ACT.Copy).then_inc(s_gtc, 1)
                    else:
                        nc.scalar.activation(gt[:, 4:5, :], ps_g[1][:, 0:1, :], ACT.Copy)
                        nc.scalar.activation(gt[0:rest, 5:6, :], ps_g[1][0:rest, 1:2, :], ACT.Copy).then_inc(s_gtc, 1)
            rounds(act, turn, T)
            act.wait_ge(s_y, T)
            act.wait_ge(s_st[0], 16 * (T // 2))
            nc.scalar.activation(y[:, 0], ps_y[:], ACT.Copy).then_inc(s_yc, 1)

        @block.vector
        def _(v):
            def turn(n, slot, more):
                for hf in range(2):
                    v.wait_ge(s_silu, n * 2 + hf + 1)
                    v.wait_ge(s_up, n * 4 + hf + 3)
                    if late(n, 2):
                        v.wait_ge(s_gt, n * 2 - 2)
                    nc.vector.tensor_tensor(gl[:, slot, hf * EHALF:(hf + 1) * EHALF], ps_h[2 + hf][:, 0:EHALF],
                                            act_[:, hf * EHALF:(hf + 1) * EHALF], ALU.mult).then_inc(s_mul, 1)
            rounds(v, turn, T)


def combine(nc, g, out):
    with Phase(nc, "comb") as m:
        x = m.sb("x", [P, 2, 2, D])
        y = m.sb("y", [P, 2, 2, 2, D])
        o = m.sb("o", [P, 2, 2, D])
        t = m.sb("t", [P, 2, 2, D])
        idx = m.sb("idx", [P, 2, 2, 2], I32)
        s_idx, s_t, s_o = (m.sem(k) for k in ("idx", "t", "o"))
        s_x, s_st = ([m.sem(f"{k}{i}") for i in range(2)] for k in ("x", "st"))
        s_y = m.sems_of_pool("y", 2)
        block = m.block()

        @block.sync
        def _(sp):
            def turn(n, slot, more):
                if late(n, 2):
                    sp.wait_ge(s_o, n * 2 - 2)
                sp.dma_start(x[:, slot], pair_rows(g.x3, n)).then_inc(s_x[slot], 16)
                if late(n, 1):
                    sp.wait_ge(s_o, n * 2)
                    sp.dma_start(pair_rows(out, n - 1), o[:, 1 - slot]).then_inc(s_st[1 - slot], 16)
            rounds(sp, turn)
            sp.wait_ge(s_o, PAIRS * 2)
            sp.dma_start(pair_rows(out, PAIRS - 1), o[:, 0]).then_inc(s_st[0], 16)
            sp.wait_ge(s_st[0], 16 * (PAIRS // 2 + 1))
            sp.wait_ge(s_st[1], 16 * (PAIRS // 2))

        @block.scalar
        def _(act):
            def turn(n, slot, more):
                if late(n, 2):
                    act.wait_ge(s_o, n * 2 - 2)
                nc.scalar.activation(idx[:, slot], g.from_slot[:, bass.ds(n * 2, 2), :], ACT.Copy).then_inc(s_idx, 1)
            rounds(act, turn)

        @block.gpsimd
        def _(pool):
            def turn(n, slot, more):
                pool.wait_ge(s_idx, n + 1)
                pool.nop(nofuse=True)
                for b in range(2):
                    for i in range(2):
                        nc.gpsimd.indirect_dma_start(y[:, slot, b, i, :], None, g.slot_y,
                                                     bass.IndirectOffsetOnAxis(idx[:, slot, b, i:i + 1], 0)).then_inc(s_y[slot], 16)
            rounds(pool, turn)

        @block.vector
        def _(v):
            def turn(n, slot, more):
                v.wait_ge(s_x[slot], (n + (2 - slot)) * 8)
                v.wait_ge(s_y[slot], (n + (2 - slot)) * 32)
                for b in range(2):
                    if late(n, 2):
                        v.wait_ge(s_o, n * 2 - 2)
                    nc.vector.scalar_tensor_tensor(t[:, slot, b], y[:, slot, b, 0, :], g.gate[:, 0, bass.ds(n * 2 + b, 1)],
                                                   x[:, slot, b, :], ALU.mult, ALU.add).then_inc(s_t, 1)
                for b in range(2):
                    v.wait_ge(s_t, n * 2 + b + 1)
                    if late(n, 2):
                        v.wait_ge(s_st[slot], (n - slot) * 8)
                    nc.vector.scalar_tensor_tensor(o[:, slot, b], y[:, slot, b, 1, :], g.gate[:, 1, bass.ds(n * 2 + b, 1)],
                                                   t[:, slot, b], ALU.mult, ALU.add).then_inc(s_o, 1)
            rounds(v, turn)


class Plan:

    def __init__(self, ins):
        self.names = {}
        (self.x, self.src_rows, self.dst_rows, self.bias_rows,
         self.Wq, self.Wk, self.Wv, self.Wp, self.bp, self.ln1_g, self.ln1_b, self.ln2_g, self.ln2_b,
         self.W1, self.b1, self.W2, self.b2, self.wr, self.br, self.w1, self.fb1, self.w2, self.fb2,
         self.W, self.a_src, self.a_dst, self.gamma, self.beta,
         self.router_t, self.w1_t, self.w3_t, self.w2_t) = (ins[k] for k in INPUTS)

    def next_name(self, name):
        self.names[name] = self.names.get(name, 0) + 1
        return f"{name}{self.names[name]}"


def set_constants(nc, g):
    with Phase(nc, "const") as m:
        s_c, s_half = m.sem("c"), m.sem("half")
        block = m.block()

        @block.vector
        def _(v):
            nc.vector.memset(g.minus_half[:], -0.5).then_inc(s_half, 1)
            v.wait_ge(s_half, 1)

        @block.gpsimd
        def _(pool):
            nc.gpsimd.memset(g.ident[:], 0.0).then_inc(s_c, 1)
            pool.wait_ge(s_c, 1)
            nc.gpsimd.affine_select(out=g.ident[:], in_=g.ident[:], compare_op=ALU.not_equal, fill=1.0,
                                    base=0, pattern=[[-1, P]], channel_multiplier=1).then_inc(s_c, 1)
            nc.gpsimd.iota(g.lane[:], [[1, P]], 0, 0, allow_small_or_imprecise_dtypes=True).then_inc(s_c, 1)
            nc.gpsimd.iota(g.node[:], [[P, BLOCKS]], 0, 1, allow_small_or_imprecise_dtypes=True).then_inc(s_c, 1)
            pool.wait_ge(s_c, 4)


def clear(nc, g, acc):
    with Phase(nc, g.next_name("clear")) as m:
        s = m.sem("s")
        block = m.block()

        @block.vector
        def _(v):
            nc.vector.memset(acc[:], 0.0).then_inc(s, 1)
            v.wait_ge(s, 1)


INPUTS = {
    "x": (NPAD, D), "src_rows": (TILE_ROWS, P), "dst_rows": (TILE_ROWS, P), "bias_rows": (TILE_ROWS, P),
    "Wq": (D, D), "Wk": (D, D), "Wv": (D, D), "Wp": (D, D), "bp": (D,), "ln1_g": (D,), "ln1_b": (D,),
    "ln2_g": (D,), "ln2_b": (D,), "W1": (D, FF), "b1": (FF,), "W2": (FF, D), "b2": (D,),
    "wr": (D,), "br": (1,), "w1": (D, FF), "fb1": (FF,), "w2": (FF, D), "fb2": (D,),
    "W": (D, D), "a_src": (H, HD), "a_dst": (H, HD), "gamma": (D,), "beta": (D,),
    "router_t": (D, EXPERTS), "w1_t": (EXPERTS, D, EH), "w3_t": (EXPERTS, D, EH), "w2_t": (EXPERTS, EH, D),
}


def program(nc, ins, out):
    g = Plan(ins)

    def dram(name, shape):
        return nc.dram_tensor(name, shape, F32).ap()

    g.norm, g.k_rows, g.v_rows, g.hidden, g.resid, g.x1n, g.token_y, g.x2, g.x3, g.x3n = (
        dram(n, (NPAD, D)) for n in ("norm", "k_rows", "v_rows", "hidden", "resid", "x1n", "token_y", "x2", "x3", "x3n"))
    g.s_src = dram("s_src", (NPAD, H))
    g.slot_rows = dram("slot_rows", (SLOTS + 2 * (NPAD - N), D))
    g.slot_y = dram("slot_y", (SLOTS, D))

    with Phase(nc, "all") as top:
        g.ident, g.lane = top.sb("ident", [P, P]), top.sb("lane", [P, P])
        g.minus_half = top.sb("minus_half", [P, 2])
        g.node = top.sb("node", [P, BLOCKS])
        g.logits = top.sb("logits", [P, BLOCKS, EXPERTS])
        g.weight, g.keep = top.sb("weight", [P, BLOCKS]), top.sb("keep", [P, BLOCKS])
        g.step_dst, g.step_src = top.sb("step_dst", [P, STEPS]), top.sb("step_src", [P, STEPS], I32)
        g.step_block = top.sb("step_block", [1, STEPS], I32)
        g.run_bias, g.run_off, g.run_new = (top.sb("run_bias", [P, STEPS]), top.sb("run_off", [P, STEPS]),
                                            top.sb("run_new", [P, STEPS + 1]))
        set_constants(nc, g)
        step_tables(nc, g)

        with Phase(nc, "graph1") as m:
            scores = m.sb("scores", [P, STEPS, H])
            with Phase(nc, "q") as mq:
                q = mq.sb("q", [P, BLOCKS, D])
                project_qkv(nc, g, q)
                edge_scores(nc, g, scores, g.k_rows, D, q)
            edge_softmax(nc, g, scores, g.run_bias, float(HD) ** -0.5)
            with Phase(nc, "acc1") as ma:
                acc = ma.sb("acc", [P, BLOCKS, AGG])
                clear(nc, g, acc)
                aggregate(nc, g, acc, scores, g.v_rows)
                attention_out(nc, g, acc)
        ffn(nc, g, "ffn1", g.hidden, g.W1, g.b1, g.W2, ACT.Gelu, FF, [g.hidden, g.x], D, after_graph,
            8 + 2 * LN_STEPS, 2, [g.b2, g.ln2_g, g.ln2_b, g.wr], None, [g.resid, g.x1n])
        keep_top(nc, g)
        ffn(nc, g, "ffn2", g.x1n, g.w1, g.fb1, g.w2, ACT.Gelu_apprx_tanh, FF, [], D, weighted,
            2, 0, [g.fb2], None, [g.token_y])

        with Phase(nc, "graph2") as m:
            scores = m.sb("scores", [P, STEPS, H])
            s_dst = m.sb("s_dst", [P, BLOCKS, H])
            project_heads(nc, g, s_dst)
            edge_scores(nc, g, scores, g.s_src, H, s_dst)
            edge_softmax(nc, g, scores, g.run_off, 1.0)
            with Phase(nc, "acc2") as ma:
                acc = ma.sb("acc", [P, BLOCKS, AGG])
                clear(nc, g, acc)
                aggregate(nc, g, acc, scores, g.v_rows)
                graph2_out(nc, g, acc, g.logits)
        with Phase(nc, "experts") as m:
            g.gate = m.sb("gate", [P, 2, BLOCKS])
            g.from_slot, g.to_slot = m.sb("from_slot", [P, BLOCKS, 2], I32), m.sb("to_slot", [P, BLOCKS, 2], I32)
            g.tile_expert = m.sb("tile_expert", [1, MAX_TILES], I32)
            g.exp_out = m.sb("exp_out", [P, BLOCKS, EXPERTS])
            g.w13, g.w2_sb = m.sb("w13", [P, EXPERTS, KC, 2, EH]), m.sb("w2", [P, EXPERTS, EC, D])
            g.s_exp, g.s_experts = m.sem("exp"), m.sem("experts")
            route(nc, g, g.logits)
            scatter_tokens(nc, g)
            experts(nc, g)
            combine(nc, g, out)


def kernel(**inputs):
    import numpy as np
    import concourse.bacc as bacc
    from concourse.bass_utils import run_bass_kernel_spmd

    def rows(a, pad):
        flat = np.full((EPAD,), pad, a.dtype)
        flat[:E] = a.reshape(-1)
        return flat.reshape(TILE_ROWS, P)

    i = {k: np.asarray(v) for k, v in inputs.items()}
    x = np.zeros((NPAD, D), np.float32)
    x[:N] = i["x"]
    arrays = {"x": x, "src_rows": rows(i["src"], 0), "dst_rows": rows(i["dst"], DST_PAD),
              "bias_rows": rows(i["edge_weight1"], 0)}
    for k in ("Wq", "Wk", "Wv", "Wp", "bp", "ln1_g", "ln1_b", "ln2_g", "ln2_b", "W1", "b1", "W2", "b2"):
        arrays[k] = i["L0_gnn_" + k]
    arrays |= {"wr": i["L0_ffn_wr"].reshape(-1), "br": i["L0_ffn_br"], "w1": i["L0_ffn_w1"], "fb1": i["L0_ffn_b1"],
               "w2": i["L0_ffn_w2"], "fb2": i["L0_ffn_b2"]}
    for k in ("W", "a_src", "a_dst", "gamma", "beta"):
        arrays[k] = i["L1_gnn_" + k]
    arrays |= {"router_t": i["L1_ffn_router_w"].T, "w1_t": i["L1_ffn_w1"].transpose(0, 2, 1),
               "w3_t": i["L1_ffn_w3"].transpose(0, 2, 1), "w2_t": i["L1_ffn_w2"].transpose(0, 2, 1)}

    nc = bacc.Bacc("TRN2", target_bir_lowering=False, num_devices=1)
    ins, fed = {}, {}
    for k, shape in INPUTS.items():
        a = np.ascontiguousarray(arrays[k])
        assert a.shape == shape
        fed[f"in_{k}"] = a
        ins[k] = nc.dram_tensor(f"in_{k}", shape, mybir.dt.from_np(a.dtype), kind="ExternalInput").ap()
    out = nc.dram_tensor("out", (NPAD, D), F32, kind="ExternalOutput").ap()
    program(nc, ins, out)
    r = run_bass_kernel_spmd(nc, [fed], core_ids=[0])
    return r.results[0]["out"][:N]
```

```python
from contextlib import ExitStack

import concourse.bass as bass
from concourse import mybir

F32 = mybir.dt.float32
I32 = mybir.dt.int32
BF16 = mybir.dt.bfloat16
ALU = mybir.AluOpType
ACT = mybir.ActivationFunctionType
AX = mybir.AxisListType

P = 128
N = 6250
D = 256
H = 8
HD = D // H
FF = 4 * D
E = 106250
KC = D // P
BLOCKS = 50
NPAD = BLOCKS * P
LAST_BLOCK = (N - 1) // P
PAIRS = BLOCKS // 2
EDGE_TILES = -(-E // P)
TILE_ROWS = EDGE_TILES + 1
EPAD = TILE_ROWS * P
WINDOWS = 7
STEPS = P * WINDOWS
TGROUPS = WINDOWS
DST_PAD = 1 << 20
BIG = 1.0e30
NEG = -1.0e38
U = 8
HALVES = -(-(EDGE_TILES + LAST_BLOCK) // U)
RING = 4
AGG = D + H
LN_EPS = 1e-5
KEEP = 3124
KEPT_BLOCKS = 2 * -(-KEEP // (2 * P))
EXPERTS = 8
EH = 682
MAX_TILES = (2 * N) // P + EXPERTS
SLOTS = MAX_TILES * P
EC = -(-EH // P)
EHALF = EH // 2
assert STEPS >= HALVES * U >= EDGE_TILES + LAST_BLOCK and HALVES % 2 == 0 and KEEP == int(0.5 * N) - 1


class Phase:

    def __init__(self, nc, name):
        self.nc, self.name, self.ctx, self.sems = nc, name, ExitStack(), []

    def __enter__(self):
        return self

    def __exit__(self, *e):
        self.ctx.close()
        if self.sems:
            for first in (s for s in self.sems if s - 1 not in self.sems):
                self.nc.gpsimd.sem_clear(range(first, next(i for i in range(first, 257) if i not in self.sems)))
            self.nc.all_engine_barrier()

    def sb(self, name, shape, dt=F32):
        return self.ctx.enter_context(self.nc.sbuf_tensor(f"{self.name}_{name}", shape, dt))

    def ps(self, name, shape, dt=F32):
        return self.ctx.enter_context(self.nc.psum_tensor(f"{self.name}_{name}", shape, dt))

    def sem(self, name):
        sem = self.ctx.enter_context(self.nc.semaphore(f"{self.name}_{name}"))
        self.sems.append(sem.num)
        return sem

    def sems_of_pool(self, name, count):
        return [self.nc.alloc_semaphore(f"{self.name}_{name}{i}") for i in range(count)]

    def block(self):
        return self.ctx.enter_context(self.nc.Block())


class Chain:

    def __init__(self, eng, sem):
        self.eng, self.sem, self.n = eng, sem, 0

    def after(self, ins):
        self.n += 1
        ins.then_inc(self.sem, 1)
        self.eng.wait_ge(self.sem, self.n)
        return ins


def step_tables(nc, g):
    with Phase(nc, "tab") as m:
        last_dst = m.sb("last_dst", [P, TGROUPS], I32)
        last_blk = m.sb("last_blk", [P, TGROUPS], I32)
        ends = m.sb("ends", [P, TGROUPS])
        tile_no = m.sb("tile_no", [P, TGROUPS])
        beyond = m.sb("beyond", [P, TGROUPS])
        step_row = m.sb("step_row", [P, STEPS])
        step_pw = m.sb("step_pw", [P, WINDOWS])
        cmp = m.sb("cmp", [P, TGROUPS, STEPS])
        ones = m.sb("ones", [P, 1])
        tile_f = m.sb("tile_f", [P, WINDOWS])
        tile_idx = m.sb("tile_idx", [P, WINDOWS], I32)
        blk = m.sb("blk", [P, WINDOWS])
        e_row = m.sb("e_row", [1, STEPS])
        b_row = m.sb("b_row", [1, STEPS])
        dst_i = m.sb("dst_i", [P, WINDOWS, P], I32)
        src_i = m.sb("src_i", [P, WINDOWS, P], I32)
        dst_x = m.sb("dst_x", [P, STEPS + 2])
        src_f = m.sb("src_f", [P, WINDOWS, P])
        rel = m.sb("rel", [P, WINDOWS, P])
        over = m.sb("over", [P, WINDOWS, P])
        src_c = m.sb("src_c", [P, STEPS])
        ps_e = m.ps("ps_e", [P, 512])
        ps_r = [m.ps(f"ps_r{i}", [P, 512]) for i in range(2)]
        ps_t = [m.ps(f"ps_t{i}", [P, 512]) for i in range(3)]
        s_in, s_iota, s_set, s_cmp, s_pe, s_idx = (m.sem(x) for x in ("in", "iota", "set", "cmp", "pe", "idx"))
        s_v, s_cols, s_copied, s_side = (m.sem(x) for x in ("v", "cols", "copied", "side"))
        s_dst, s_src, s_bias = m.sems_of_pool("gathered", 3)
        block = m.block()
        dst_runs = dst_x[:, 1:STEPS + 1]

        @block.sync
        def _(sp):
            full = (TGROUPS - 1) * P
            sp.wait_ge(s_set, 1)
            with nc.allow_non_contiguous_dma(reason="one word of each edge tile"):
                sp.dma_start(last_dst[:, 0:TGROUPS - 1],
                             g.dst_rows[0:full, P - 1:P].rearrange("(k p) o -> p (k o)", p=P)).then_inc(s_in, 16)
                sp.dma_start(last_dst[0:TILE_ROWS - full, TGROUPS - 1:TGROUPS],
                             g.dst_rows[full:TILE_ROWS, P - 1:P]).then_inc(s_in, 16)
                sp.wait_ge(s_cols, 1)
                sp.dma_start(dst_x[1:P, 0:1], dst_x[0:P - 1, STEPS:STEPS + 1]).then_inc(s_side, 16)
                sp.dma_start(dst_x[0:P - 1, STEPS + 1:STEPS + 2], dst_x[1:P, 1:2]).then_inc(s_side, 16)
            sp.wait_ge(s_side, 32)

        @block.gpsimd
        def _(pool):
            nc.gpsimd.iota(step_row[:], [[1, STEPS]], 0, 0, allow_small_or_imprecise_dtypes=True).then_inc(s_iota, 1)
            nc.gpsimd.iota(tile_no[:], [[P, TGROUPS]], 0, 1, allow_small_or_imprecise_dtypes=True).then_inc(s_iota, 1)
            nc.gpsimd.iota(step_pw[:], [[1, WINDOWS]], 0, WINDOWS, allow_small_or_imprecise_dtypes=True).then_inc(s_iota, 1)
            pool.wait_ge(s_idx, 1)
            for w in range(WINDOWS):
                idx = bass.IndirectOffsetOnAxis(tile_idx[:, w:w + 1], 0)
                nc.gpsimd.indirect_dma_start(dst_i[:, w, :], None, g.dst_rows, idx).then_inc(s_dst, 16)
                nc.gpsimd.indirect_dma_start(src_i[:, w, :], None, g.src_rows, idx).then_inc(s_src, 16)
                nc.gpsimd.indirect_dma_start(g.run_bias[:, w * P:(w + 1) * P], None, g.bias_rows, idx).then_inc(s_bias, 16)
            pool.wait_ge(s_dst, 16 * WINDOWS)
            pool.wait_ge(s_src, 16 * WINDOWS)
            pool.wait_ge(s_bias, 16 * WINDOWS)

        @block.tensor
        def _(pe):
            by_w = cmp[:].rearrange("q k (p w) -> q k w p", w=WINDOWS)
            pe.wait_ge(s_cmp, TGROUPS)
            for w in range(WINDOWS):
                for k in range(TGROUPS):
                    last = nc.tensor.matmul(ps_e[:, w:w + 1], by_w[:, k, w, :], ones[:],
                                            start=(k == 0), stop=(k == TGROUPS - 1))
            last.then_inc(s_pe, 1)
            for i, (a, b) in enumerate(((0, 512), (512, STEPS))):
                for k in range(TGROUPS):
                    last = nc.tensor.matmul(ps_r[i][0:1, 0:b - a], ones[:], cmp[:, k, a:b],
                                            start=(k == 0), stop=(k == TGROUPS - 1))
            last.then_inc(s_pe, 1)
            pe.wait_ge(s_cols, 2)
            n = 0
            for rows in (rel, src_f):
                for w in range(WINDOWS):
                    if n >= 3:
                        pe.wait_ge(s_copied, n - 2)
                    nc.tensor.transpose(ps_t[n % 3][:, 0:P], rows[:, w, :], g.ident[:]).then_inc(s_pe, 1)
                    n += 1

        @block.vector
        def _(v):
            ch = Chain(v, s_v)
            nc.vector.memset(last_dst[:], DST_PAD).then_inc(s_set, 1)
            ch.after(nc.vector.memset(ones[:], 1.0))
            ch.after(nc.vector.memset(dst_x[:], -1.0))
            v.wait_ge(s_in, 32)
            ch.after(nc.vector.tensor_scalar(last_blk[:], last_dst[:], 7, None, ALU.arith_shift_right))
            ch.after(nc.vector.tensor_scalar(ends[:], last_blk[:], float(LAST_BLOCK), None, ALU.min))
            v.wait_ge(s_iota, 3)
            ch.after(nc.vector.tensor_tensor(ends[:], ends[:], tile_no[:], ALU.add))
            ch.after(nc.vector.tensor_scalar(beyond[:], tile_no[:], float(EDGE_TILES), BIG, ALU.is_ge, ALU.mult))
            ch.after(nc.vector.tensor_tensor(ends[:], ends[:], beyond[:], ALU.add))
            for k in range(TGROUPS):
                nc.vector.tensor_scalar(cmp[:, k, :], step_row[:], ends[:, k:k + 1], None, ALU.is_gt).then_inc(s_cmp, 1)
            v.wait_ge(s_pe, 1)
            nc.vector.tensor_copy(tile_idx[:], ps_e[:, 0:WINDOWS]).then_inc(s_idx, 1)
            ch.after(nc.vector.tensor_copy(tile_f[:], ps_e[:, 0:WINDOWS]))
            ch.after(nc.vector.tensor_tensor(blk[:], step_pw[:], tile_f[:], ALU.subtract))
            ch.after(nc.vector.tensor_scalar(blk[:], blk[:], float(LAST_BLOCK), float(-P), ALU.min, ALU.mult))
            v.wait_ge(s_pe, 2)
            nc.vector.tensor_copy(e_row[0:1, 0:512], ps_r[0][0:1, 0:512]).then_inc(s_v, 1)
            ch.n += 1
            ch.after(nc.vector.tensor_copy(e_row[0:1, 512:STEPS], ps_r[1][0:1, 0:STEPS - 512]))
            ch.after(nc.vector.tensor_tensor(b_row[:], step_row[0:1, :], e_row[:], ALU.subtract))
            ch.after(nc.vector.tensor_scalar(b_row[:], b_row[:], float(LAST_BLOCK), None, ALU.min))
            ch.after(nc.vector.tensor_copy(g.step_block[:], b_row[:]))
            v.wait_ge(s_dst, 16 * WINDOWS)
            nc.vector.tensor_copy(dst_runs, dst_i[:].rearrange("p w j -> p (w j)")).then_inc(s_cols, 1)
            v.wait_ge(s_src, 16 * WINDOWS)
            nc.vector.tensor_copy(src_f[:], src_i[:]).then_inc(s_v, 1)
            ch.n += 1
            v.wait_ge(s_cols, 1)
            ch.after(nc.vector.tensor_tensor(rel[:], dst_runs.rearrange("p (w j) -> p w j", w=WINDOWS),
                                             blk[:].unsqueeze(2).to_broadcast([P, WINDOWS, P]), ALU.add))
            v.sem_inc(s_cols, 1)
            ch.after(nc.vector.tensor_scalar(over[:], rel[:], float(P), NEG, ALU.is_ge, ALU.mult))
            ch.after(nc.vector.tensor_scalar(g.run_off[:].rearrange("p (w j) -> p w j", w=WINDOWS), rel[:],
                                             0.0, NEG, ALU.is_lt, ALU.mult))
            ch.after(nc.vector.tensor_tensor(g.run_off[:].rearrange("p (w j) -> p w j", w=WINDOWS),
                                             g.run_off[:].rearrange("p (w j) -> p w j", w=WINDOWS), over[:], ALU.add))
            v.wait_ge(s_bias, 16 * WINDOWS)
            ch.after(nc.vector.tensor_tensor(g.run_bias[:], g.run_bias[:], g.run_off[:], ALU.add))
            v.wait_ge(s_side, 32)
            ch.after(nc.vector.tensor_tensor(g.run_new[:], dst_x[:, 1:STEPS + 2], dst_x[:, 0:STEPS + 1], ALU.not_equal))
            ch.after(nc.vector.tensor_scalar(g.run_new[:], g.run_new[:], NEG, None, ALU.mult))
            by_w = [g.step_dst[:].rearrange("q (p w) -> q w p", w=WINDOWS),
                    g.step_src[:].rearrange("q (p w) -> q w p", w=WINDOWS)]
            n = 0
            for dest in by_w:
                for w in range(WINDOWS):
                    v.wait_ge(s_pe, 3 + n)
                    nc.vector.tensor_copy(dest[:, w, :], ps_t[n % 3][:, 0:P]).then_inc(s_copied, 1)
                    n += 1
            v.wait_ge(s_copied, n)


class Rows:

    def __init__(self, nc, g, m, rows, width):
        self.nc, self.g, self.rows = nc, g, rows
        self.ring = m.sb("ring", [P, RING, U, width])
        self.idx = m.sb("idx", [P, RING, U], I32)
        self.s_idx = m.sem("idx")
        self.landed = m.sems_of_pool("row", RING)

    def index(self, n, slot):
        self.nc.scalar.activation(self.idx[:, slot, :], self.g.step_src[:, bass.ds(n * U, U)],
                                  ACT.Copy).then_inc(self.s_idx, 1)

    def gather(self, n, slot, more=True):
        self.nc.gpsimd.wait_ge(self.s_idx, n + 1)
        self.nc.gpsimd.nop(nofuse=True)
        for u in range(U):
            self.nc.gpsimd.indirect_dma_start(self.ring[:, slot, u, :], None, self.rows,
                                              bass.IndirectOffsetOnAxis(self.idx[:, slot, u:u + 1], 0)
                                              ).then_inc(self.landed[slot], 16)

    def wait(self, eng, n, slot):
        eng.wait_ge(self.landed[slot], (n + (RING - slot)) * (16 * U // RING))


SOFT_EXP_AT = 52


def edge_softmax(nc, g, scores, runs_bias, scale, src):
    with Phase(nc, g.next_name("soft")) as m:
        val = m.sb("val", [P, H, STEPS])
        fwd = m.sb("fwd", [P, H, STEPS])
        bwd = m.sb("bwd", [P, H, STEPS])
        keep = m.sb("keep", [P, 2, H])
        tails = m.sb("tails", [P, 2, H])
        neg = m.sb("neg", [H, 2, P + 1])
        keep_t = m.sb("keep_t", [H, 2, P])
        tails_t = m.sb("tails_t", [H, 2, P])
        carry = m.sb("carry", [P, 2, H])
        ps = [m.ps(f"ps{i}", [P, 4, P]) for i in range(4)]
        ps_k = m.ps("ps_k", [H, 4, P])
        ps_c = m.ps("ps_c", [P, 2, H])
        s_v, s_tr, s_evac, s_tail, s_tailt, s_carry, s_back, s_exp, s_p, s_pevac = (
            m.sem(x) for x in ("v", "tr", "evac", "tail", "tailt", "carry", "back", "exp", "p", "pevac"))
        block = m.block()
        by_w = scores[:].rearrange("q (p w) h -> q w h p", w=WINDOWS)
        groups = [(h, w) for h in range(H) for w in (0, 4)]

        @block.tensor
        def _(pe):
            for n, (h, w0) in enumerate(groups):
                if n >= 4:
                    pe.wait_ge(s_evac, n - 3)
                for w in range(w0, min(w0 + 4, WINDOWS)):
                    last = nc.tensor.transpose(ps[n % 4][:, w - w0, :], by_w[:, w, h, :], g.ident[:])
                last.then_inc(s_tr, 1)
            pe.wait_ge(s_tail, 1)
            for i, t in enumerate((keep[:, 0], keep[:, 1], tails[:, 0], tails[:, 1])):
                last = nc.tensor.transpose(ps_k[:, i, :], t, g.ident[:])
            last.then_inc(s_tailt, 1)
            pe.wait_ge(s_carry, 1)
            nc.tensor.transpose(ps_c[:, 0, :], neg[:, 0, 0:P], g.ident[0:H, 0:H])
            nc.tensor.transpose(ps_c[:, 1, :], neg[:, 1, 1:P + 1], g.ident[0:H, 0:H]).then_inc(s_back, 1)
            for n, (h, w0) in enumerate(groups):
                if w0 == 0:
                    pe.wait_ge(s_exp, h + 1)
                if n >= 4:
                    pe.wait_ge(s_pevac, n - 3)
                for w in range(w0, min(w0 + 4, WINDOWS)):
                    last = nc.tensor.transpose(ps[n % 4][:, w - w0, :], val[:, h, w * P:(w + 1) * P], g.ident[:])
                last.then_inc(s_p, 1)

        @block.gpsimd
        def _(pool):
            for n in range(RING):
                src.gather(n, n)

        @block.scalar
        def _(act):
            for n in range(RING):
                src.index(n, n)
            for h in range(H):
                act.wait_ge(s_v, SOFT_EXP_AT + h)
                nc.scalar.activation(val[:, h, :], val[:, h, :], ACT.Exp).then_inc(s_exp, 1)

        @block.vector
        def _(v):
            ch = Chain(v, s_v)
            ch.after(nc.vector.memset(neg[:], NEG))
            for n, (h, w0) in enumerate(groups):
                v.wait_ge(s_tr, n + 1)
                w1 = min(w0 + 4, WINDOWS)
                nc.vector.scalar_tensor_tensor(val[:, h, w0 * P:w1 * P], ps[n % 4][:, 0:w1 - w0, :].rearrange("p a b -> p (a b)"),
                                               scale, runs_bias[:, w0 * P:w1 * P], ALU.mult, ALU.add).then_inc(s_evac, 1)
            v.wait_ge(s_evac, len(groups))
            start, end = g.run_new[:, 0:STEPS], g.run_new[:, 1:STEPS + 1]

            def scans(first):
                for h in range(H):
                    nc.vector.tensor_tensor_scan(fwd[:, h, :], start, val[:, h, :],
                                                 NEG if first else carry[:, 0, h:h + 1], ALU.add, ALU.max).then_inc(s_v, 1)
                    nc.vector.tensor_tensor_scan(bwd[:, h, ::-1], end[:, ::-1], val[:, h, ::-1],
                                                 NEG if first else carry[:, 1, h:h + 1], ALU.add, ALU.max).then_inc(s_v, 1)
                    ch.n += 2
                v.wait_ge(s_v, ch.n)

            scans(True)
            ch.after(nc.vector.tensor_reduce(keep[:, 0, 0:1], start, AX.X, ALU.min))
            ch.after(nc.vector.tensor_reduce(keep[:, 1, 0:1], end, AX.X, ALU.min))
            ch.after(nc.vector.tensor_copy(keep[:, :, 1:H], keep[:, :, 0:1].to_broadcast([P, 2, H - 1])))
            ch.after(nc.vector.tensor_copy(tails[:, 0, :], fwd[:, :, STEPS - 1]))
            ch.after(nc.vector.tensor_copy(tails[:, 1, :], bwd[:, :, 0]))
            v.sem_inc(s_tail, 1)
            v.wait_ge(s_tailt, 1)
            ch.after(nc.vector.tensor_copy(keep_t[:], ps_k[:, 0:2, :]))
            ch.after(nc.vector.tensor_copy(tails_t[:], ps_k[:, 2:4, :]))
            ch.after(nc.vector.tensor_tensor_scan(neg[:, 0, 1:P + 1], keep_t[:, 0, :], tails_t[:, 0, :], NEG, ALU.add, ALU.max))
            ch.after(nc.vector.tensor_tensor_scan(neg[:, 1, P - 1::-1], keep_t[:, 1, ::-1], tails_t[:, 1, ::-1], NEG, ALU.add, ALU.max))
            v.sem_inc(s_carry, 1)
            v.wait_ge(s_back, 1)
            ch.after(nc.vector.tensor_copy(carry[:], ps_c[:]))
            scans(False)
            for h in range(H):
                ch.after(nc.vector.tensor_tensor(fwd[:, h, :], fwd[:, h, :], bwd[:, h, :], ALU.max))
            assert ch.n + 1 == SOFT_EXP_AT, ch.n
            for h in range(H):
                nc.vector.tensor_tensor(val[:, h, :], val[:, h, :], fwd[:, h, :], ALU.subtract).then_inc(s_v, 1)
            for n, (h, w0) in enumerate(groups):
                v.wait_ge(s_p, n + 1)
                w1 = min(w0 + 4, WINDOWS)
                nc.vector.tensor_copy(by_w[:, w0:w1, h, :], ps[n % 4][:, 0:w1 - w0, :]).then_inc(s_pevac, 1)
            v.wait_ge(s_pevac, len(groups))


def turns(eng, body, first=0):
    for n in range(first, RING):
        body(n, n, True)
    with eng.Fori(1, HALVES // RING - 1) as it:
        for r in range(RING):
            body(it * RING + r, r, True)
    for n in range((HALVES // RING - 1) * RING, HALVES):
        body(n, n % RING, n + 1 < HALVES)


def step_blocks(nc, g, engine, n):
    return nc.values_load_multi_w_load_instructions(
        g.step_block[0:1, bass.ds(n * U, U)], [engine], min_val=0, max_val=LAST_BLOCK,
        skip_runtime_bounds_check_because="made on the chip and clamped")[1]


def pick(nc, g, out, n):
    return nc.vector.tensor_tensor(out, g.step_dst[:, bass.ds(n * U, U)].unsqueeze(2).to_broadcast([P, U, P]),
                                   g.lane[:].unsqueeze(1).to_broadcast([P, U, P]), ALU.is_equal)


def edge_scores(nc, g, scores, rows, width, node_vals):
    dots = width == D
    per_bank = 512 // D if dots else U
    banks = U // per_bank
    with Phase(nc, g.next_name("score")) as m:
        src = Rows(nc, g, m, rows, width)
        sel = m.sb("sel", [P, 2, U, P])
        sel_t = m.sb("sel_t", [P, 2, U, P])
        prod = m.sb("prod", [P, 2, U, width])
        ps_t = [m.ps(f"ps_t{i}", [P, 4, P]) for i in range(2)]
        ps_q = [m.ps(f"ps_q{i}", [P, per_bank, width]) for i in range(banks)]
        s_used, s_sel, s_selt, s_tpe, s_q, s_qfree, s_red = (
            m.sem(x) for x in ("used", "sel", "selt", "tpe", "q", "qfree", "red"))
        block = m.block()

        @block.gpsimd
        def _(pool):
            turns(pool, src.gather)

        @block.scalar
        def _(act):
            def index(n, slot):
                if late(n, RING):
                    act.wait_ge(s_used, n + (1 - RING))
                src.index(n, slot)

            def transposed(n, slot):
                for i in range(2):
                    act.wait_ge(s_tpe, n * 2 + i + 1)
                    nc.scalar.activation(sel_t[:, slot % 2, 4 * i:4 * i + 4, :], ps_t[i][:], ACT.Copy).then_inc(s_selt, 1)

            for n in range(RING - 1):
                index(n, n)
            transposed(0, 0)

            def half(n, slot, more):
                if not isinstance(n, int) or n < HALVES - RING + 1:
                    index(n + (RING - 1), (slot + RING - 1) % RING)
                if more:
                    if not isinstance(n, int) or n >= 1:
                        act.wait_ge(s_q, n * banks)
                    transposed(n + 1, slot + 1)
            turns(act, half)

        @block.tensor
        def _(pe):
            pe.sem_inc(s_qfree, banks)

            def transposes(n, slot):
                pe.wait_ge(s_sel, n + 1)
                if not isinstance(n, int) or n > 0:
                    pe.wait_ge(s_selt, n * 2)
                for u in range(U):
                    last = nc.tensor.transpose(ps_t[u // 4][:, u % 4, :], sel[:, slot % 2, u, :], g.ident[:])
                    if u % 4 == 3:
                        last.then_inc(s_tpe, 1)

            transposes(0, 0)

            def half(n, slot, more):
                blocks = step_blocks(nc, g, mybir.EngineType.PE, n)
                for u in range(U):
                    if u == U // 2 and more:
                        transposes(n + 1, slot + 1)
                    j = u // per_bank
                    if u % 4 == 0:
                        pe.wait_ge(s_selt, n * 2 + u // 4 + 1)
                    if u % per_bank == 0:
                        pe.wait_ge(s_qfree, n * banks + j + 1)
                    last = nc.tensor.matmul(ps_q[j][:, u % per_bank, :], sel_t[:, slot % 2, u, :],
                                            node_vals[:, bass.ds(blocks[u], 1), :].rearrange("p a d -> p (a d)"),
                                            start=True, stop=True)
                    if u % per_bank == per_bank - 1:
                        last.then_inc(s_q, 1)
            turns(pe, half)

        @block.vector
        def _(v):
            nc.vector.memset(scores[:, HALVES * U:, :], 0.0).then_inc(s_red, 1)
            pick(nc, g, sel[:, 0], 0).then_inc(s_sel, 1)

            def half(n, slot, more):
                par = slot % 2
                if more:
                    if not isinstance(n, int) or n >= 1:
                        v.wait_ge(s_tpe, n * 2)
                    pick(nc, g, sel[:, 1 - par], n + 1).then_inc(s_sel, 1)
                src.wait(v, n, slot)
                if late(n, 2):
                    v.wait_ge(s_red, n)
                for j in range(banks):
                    v.wait_ge(s_q, n * banks + j + 1)
                    nc.vector.tensor_tensor(prod[:, par, j * per_bank:(j + 1) * per_bank, :], ps_q[j][:],
                                            src.ring[:, slot, j * per_bank:(j + 1) * per_bank, :],
                                            ALU.mult if dots else ALU.add).then_inc(s_qfree, 1)
                v.wait_ge(s_qfree, n * banks + 2 * banks)
                v.sem_inc(s_used, 1)
                out = scores[:, bass.ds(n * U, U), :]
                if dots:
                    nc.vector.tensor_reduce(out.rearrange("p u h -> p (u h)"),
                                            prod[:, par].rearrange("p u (h d) -> p (u h) d", h=H),
                                            AX.X, ALU.add).then_inc(s_red, 1)
                else:
                    x = prod[:, par].rearrange("p u h -> p (u h)")
                    nc.vector.scalar_tensor_tensor(out.rearrange("p u h -> p (u h)"), x, 0.2, x,
                                                   ALU.mult, ALU.max).then_inc(s_red, 1)
            turns(v, half)
            v.wait_ge(s_red, HALVES + 1)


def aggregate(nc, g, acc, probs, src):
    with Phase(nc, g.next_name("agg")) as m:
        sel = m.sb("sel", [P, 2, U, P])
        msg = m.sb("msg", [P, 2, U, AGG])
        ps = [m.ps(f"ps{i}", [P, 512]) for i in range(U)]
        s_used, s_sel, s_pcol, s_msg, s_mm, s_add, s_zero = (
            m.sem(x) for x in ("used", "sel", "pcol", "msg", "mm", "add", "zero"))
        block = m.block()

        @block.gpsimd
        def _(pool):
            turns(pool, src.gather, RING)

        @block.scalar
        def _(act):
            def index(n, slot):
                if late(n, RING):
                    act.wait_ge(s_used, n + (1 - RING))
                src.index(n, slot)

            nc.scalar.activation(acc[:, 0:PAIRS, :], g.lane[:, 0:1].unsqueeze(2).to_broadcast([P, PAIRS, AGG]),
                                 ACT.Copy, scale=0.0).then_inc(s_zero, 1)

            def half(n, slot, more):
                if late(n, 1) and (not isinstance(n, int) or n < HALVES - RING + 1):
                    index(n + (RING - 1), (slot + RING - 1) % RING)
                if not isinstance(n, int) or n >= 2:
                    act.wait_ge(s_mm, n * U - U)
                nc.scalar.activation(msg[:, slot % 2, :, D:AGG], probs[:, bass.ds(n * U, U), :], ACT.Copy).then_inc(s_pcol, 1)
            turns(act, half)

        @block.tensor
        def _(pe):
            pe.sem_inc(s_add, U)

            def half(n, slot, more):
                pe.wait_ge(s_msg, n + 1)
                pe.wait_ge(s_pcol, n + 1)
                for u in range(U):
                    pe.wait_ge(s_add, n * U + u + 1)
                    nc.tensor.matmul(ps[u][:, 0:AGG], sel[:, slot % 2, u, :], msg[:, slot % 2, u, :],
                                     start=True, stop=True).then_inc(s_mm, 1)
            turns(pe, half)

        @block.vector
        def _(v):
            def message(n, slot, u):
                return nc.vector.tensor_tensor(msg[:, slot % 2, u, 0:D].rearrange("p (h d) -> p h d", h=H),
                                               src.ring[:, slot, u, :].rearrange("p (h d) -> p h d", h=H),
                                               probs[:, bass.ds(n * U + u, 1), :].rearrange("p a h -> p (a h)")
                                               .unsqueeze(2).to_broadcast([P, H, HD]), ALU.mult)

            def start(n, slot):
                pick(nc, g, sel[:, slot % 2], n).then_inc(s_sel, 1)
                src.wait(v, n, slot)

            def finish(n):
                v.wait_ge(s_sel, n * 2 + 2)
                v.sem_inc(s_used, 1)
                v.sem_inc(s_msg, 1)

            start(0, 0)
            for u in range(U):
                ins = message(0, 0, u)
            ins.then_inc(s_sel, 1)
            finish(0)
            nc.vector.memset(acc[:, PAIRS:BLOCKS, :], 0.0).then_inc(s_zero, 1)

            def half(n, slot, more):
                if more:
                    if not isinstance(n, int) or n >= 1:
                        v.wait_ge(s_mm, n * U)
                    start(n + 1, (slot + 1) % RING)
                blocks = step_blocks(nc, g, mybir.EngineType.DVE, n)
                for u in range(U):
                    if more:
                        ins = message(n + 1, (slot + 1) % RING, u)
                        if u == U - 1:
                            ins.then_inc(s_sel, 1)
                            finish(n + 1)
                    if u == 0 and isinstance(n, int) and n == 0:
                        v.wait_ge(s_zero, 2)
                    v.wait_ge(s_mm, n * U + u + 1)
                    v.wait_ge(s_add, n * U + u + U)
                    at = acc[:, bass.ds(blocks[u], 1), :].rearrange("p a d -> p (a d)")
                    nc.vector.tensor_tensor(at, at, ps[u][:, 0:AGG], ALU.add).then_inc(s_add, 1)
            turns(v, half)
            v.wait_ge(s_add, HALVES * U + U)


class Count:

    def __init__(self, eng, sem, n, per):
        self.eng, self.sem, self.n, self.per, self.i = eng, sem, n, per, 0

    def step(self, ins):
        self.i += 1
        return ins.then_inc(self.sem, 1)

    def here(self):
        self.eng.wait_ge(self.sem, self.n * self.per + self.i)

    def then(self, ins):
        self.step(ins)
        self.here()

    def done(self):
        assert self.i == self.per, self.i


def rounds(eng, body, count=PAIRS):
    assert count % 2 == 1
    body(0, 0, 2)
    body(1, 1, 2)
    with eng.Fori(1, count // 2 - 1) as it:
        body(it * 2, 0, 2)
        body(it * 2 + 1, 1, 2)
    for left in (2, 1, 0):
        body(count - 1 - left, left % 2, left)


def late(n, by):
    return not isinstance(n, int) or n >= by


def pair_rows(dram, n):
    return dram.rearrange("(b p) d -> p b d", p=P)[:, bass.ds(n * 2, 2), :]


LN_STEPS = 5


def norm_begin(nc, c, stat, x, s_var):
    for b in range(2):
        c.step(nc.vector.bn_stats(stat[:, 6 * b:6 * b + 6], x[:, b, :]))
    c.here()
    c.eng.nop(nofuse=True)
    for b in range(2):
        c.step(nc.vector.bn_aggr(stat[:, 12 + 2 * b:14 + 2 * b], stat[:, 6 * b:6 * b + 6]))
    c.here()
    nc.vector.tensor_scalar(stat[:, 16:18], stat[:, 12:16].rearrange("p (b s) -> p b s", b=2)[:, :, 1],
                            LN_EPS, None, ALU.add).then_inc(s_var, 1)


def norm_end(nc, c, stat, out, x, s_rstd, k, per):
    c.eng.wait_ge(s_rstd, c.n * per + k + 1)
    for b in range(2):
        ins = nc.vector.tensor_scalar(out[:, b, :], x[:, b, :], stat[:, 12 + 2 * b:13 + 2 * b], stat[:, 18 + b:19 + b],
                                      ALU.subtract, ALU.mult)
    c.then(ins)


def norm_pair(nc, g, c, stat, out, x, s_var, s_rstd, k, per):
    norm_begin(nc, c, stat, x, s_var)
    norm_end(nc, c, stat, out, x, s_rstd, k, per)


def spread(row, n):
    return row.rearrange("(a n) -> a n", a=1).to_broadcast([P, n])


def project_qkv(nc, g, q):
    with Phase(nc, "qkv") as m:
        w = m.sb("w", [P, KC, 3 * D])
        x = m.sb("x", [P, 2, 2, D])
        xn = m.sb("xn", [P, 2, 2, D])
        xt = m.sb("xt", [P, 2, KC, 2, P])
        kv = m.sb("kv", [P, 2, 2, 2 * D])
        stat = m.sb("stat", [P, 2, 20])
        ps_t = [m.ps(f"ps_t{i}", [P, 2, KC, P]) for i in range(2)]
        ps_kv = [[m.ps(f"ps_kv{i}{b}", [P, 2 * D]) for b in range(2)] for i in range(2)]
        ps_q = [m.ps(f"ps_q{i}", [P, 2, D]) for i in range(2)]
        s_w, s_ln, s_var, s_rstd, s_t, s_xt, s_mm, s_out = (
            m.sem(k) for k in ("w", "ln", "var", "rstd", "t", "xt", "mm", "out"))
        s_x, s_xnst, s_kvst = ([m.sem(f"{k}{i}") for i in range(2)] for k in ("x", "xnst", "kvst"))
        block = m.block()
        LN = LN_STEPS

        @block.sync
        def _(sp):
            def load(n, slot):
                sp.dma_start(x[:, slot], pair_rows(g.x, n)).then_inc(s_x[slot], 16)

            load(0, 0)
            load(1, 1)
            for i, t in enumerate((g.Wk, g.Wv, g.Wq)):
                sp.dma_start(w[:, :, i * D:(i + 1) * D], t.rearrange("(k p) n -> p k n", p=P)).then_inc(s_w, 16)

            def turn(n, slot, more):
                sp.wait_ge(s_ln, n * LN + LN)
                if more == 2:
                    load(n + 2, slot)
                sp.dma_start(pair_rows(g.norm, n), xn[:, slot]).then_inc(s_xnst[slot], 16)
                sp.wait_ge(s_out, n * 3 + 2)
                sp.dma_start(pair_rows(g.k_rows, n), kv[:, slot, :, 0:D]).then_inc(s_kvst[slot], 16)
                sp.dma_start(pair_rows(g.v_rows, n), kv[:, slot, :, D:2 * D]).then_inc(s_kvst[slot], 16)
            rounds(sp, turn)
            for i, turns_ in enumerate((PAIRS // 2 + 1, PAIRS // 2)):
                sp.wait_ge(s_xnst[i], 16 * turns_)
                sp.wait_ge(s_kvst[i], 32 * turns_)

        @block.gpsimd
        def _(pool):
            def turn(n, slot, more):
                pool.wait_ge(s_var, n + 1)
                nc.gpsimd.tensor_tensor(stat[:, slot, 18:20], stat[:, slot, 16:18], g.minus_half[:], ALU.pow).then_inc(s_rstd, 1)
            rounds(pool, turn)

        @block.vector
        def _(v):
            def turn(n, slot, more):
                c = Count(v, s_ln, n, LN)
                v.wait_ge(s_x[slot], (n + (2 - slot)) * 8)
                if late(n, 2):
                    v.wait_ge(s_xnst[slot], (n - slot) * 8)
                    v.wait_ge(s_t, n - 1)
                norm_pair(nc, g, c, stat[:, slot], xn[:, slot], x[:, slot], s_var, s_rstd, 0, 1)
                c.done()
            rounds(v, turn)

        @block.tensor
        def _(pe):
            def transposes(n, slot):
                pe.wait_ge(s_ln, n * LN + LN)
                if late(n, 2):
                    pe.wait_ge(s_xt, n - 1)
                for b in range(2):
                    for k in range(KC):
                        last = nc.tensor.transpose(ps_t[slot][:, b, k, :], xn[:, slot, b, k * P:(k + 1) * P], g.ident[:])
                last.then_inc(s_t, 1)

            transposes(0, 0)
            pe.wait_ge(s_w, 48)

            def turn(n, slot, more):
                pe.wait_ge(s_xt, n + 1)
                if late(n, 2):
                    pe.wait_ge(s_out, n * 3 - 3)
                for b in range(2):
                    for k in range(KC):
                        last = nc.tensor.matmul(ps_kv[slot][b][:], xt[:, slot, k, b, :], w[:, k, 0:2 * D],
                                                start=(k == 0), stop=(k == KC - 1))
                    last.then_inc(s_mm, 1)
                if more:
                    transposes(n + 1, 1 - slot)
                for b in range(2):
                    for k in range(KC):
                        last = nc.tensor.matmul(ps_q[slot][:, b, :], xt[:, slot, k, b, :], w[:, k, 2 * D:3 * D],
                                                start=(k == 0), stop=(k == KC - 1))
                last.then_inc(s_mm, 1)
            rounds(pe, turn)

        @block.scalar
        def _(act):
            def evac_xt(n, slot):
                act.wait_ge(s_t, n + 1)
                if late(n, 2):
                    act.wait_ge(s_mm, n * 3 - 3)
                nc.scalar.activation(xt[:, slot].rearrange("p k b n -> p b k n"), ps_t[slot][:], ACT.Copy).then_inc(s_xt, 1)

            evac_xt(0, 0)

            def turn(n, slot, more):
                if late(n, 2):
                    act.wait_ge(s_kvst[slot], (n - slot) * 16)
                for b in range(2):
                    act.wait_ge(s_mm, n * 3 + b + 1)
                    nc.scalar.activation(kv[:, slot, b, :], ps_kv[slot][b][:], ACT.Copy).then_inc(s_out, 1)
                if more:
                    evac_xt(n + 1, 1 - slot)
                act.wait_ge(s_mm, n * 3 + 3)
                nc.scalar.activation(q[:, bass.ds(n * 2, 2), :], ps_q[slot][:], ACT.Copy).then_inc(s_out, 1)
            rounds(act, turn)
            act.wait_ge(s_out, 3 * PAIRS)


def attention_out(nc, g, acc):
    with Phase(nc, "att") as m:
        w = m.sb("w", [P, KC, D])
        vec = m.sb("vec", [P, 3, D])
        h0 = m.sb("h0", [P, 2, 2, D])
        rec = m.sb("rec", [P, 2, 2, H])
        o = m.sb("o", [P, 2, 2, D])
        ot = m.sb("ot", [P, 2, KC, 2, P])
        t = m.sb("t", [P, 2, D])
        tn = m.sb("tn", [P, 2, D])
        h1 = m.sb("h1", [P, 2, 2, D])
        stat = m.sb("stat", [P, 20])
        ps_t = [m.ps(f"ps_t{i}", [P, 2, KC, P]) for i in range(2)]
        ps_o = [m.ps(f"ps_o{i}", [P, 2, D]) for i in range(2)]
        s_w, s_o, s_c, s_var, s_rstd, s_t, s_ot, s_mm = (
            m.sem(k) for k in ("w", "o", "c", "var", "rstd", "t", "ot", "mm"))
        s_x, s_st = ([m.sem(f"{k}{i}") for i in range(2)] for k in ("x", "st"))
        block = m.block()
        OPS, OUT = 3, 4 + LN_STEPS

        @block.sync
        def _(sp):
            sp.dma_start(w[:], g.Wp.rearrange("(k p) n -> p k n", p=P)).then_inc(s_w, 16)
            for i, r in enumerate((g.bp, g.ln1_g, g.ln1_b)):
                sp.dma_start(vec[:, i, :], spread(r, D)).then_inc(s_w, 16)

            def turn(n, slot, more):
                if late(n, 2):
                    sp.wait_ge(s_c, n * OUT - OUT)
                sp.dma_start(h0[:, slot], pair_rows(g.norm, n)).then_inc(s_x[slot], 16)
                if late(n, 1):
                    sp.wait_ge(s_c, n * OUT)
                    sp.dma_start(pair_rows(g.hidden, n - 1), h1[:, 1 - slot]).then_inc(s_st[1 - slot], 16)
            rounds(sp, turn)
            sp.wait_ge(s_c, PAIRS * OUT)
            sp.dma_start(pair_rows(g.hidden, PAIRS - 1), h1[:, 0]).then_inc(s_st[0], 16)
            sp.wait_ge(s_st[0], 16 * (PAIRS // 2 + 1))
            sp.wait_ge(s_st[1], 16 * (PAIRS // 2))

        @block.gpsimd
        def _(pool):
            def turn(n, slot, more):
                pool.wait_ge(s_var, n + 1)
                nc.gpsimd.tensor_tensor(stat[:, 18:20], stat[:, 16:18], g.minus_half[:], ALU.pow).then_inc(s_rstd, 1)
            rounds(pool, turn)

        @block.tensor
        def _(pe):
            pe.wait_ge(s_w, 64)

            def transposes(n, slot):
                pe.wait_ge(s_o, n * OPS + OPS)
                if late(n, 2):
                    pe.wait_ge(s_ot, n - 1)
                for b in range(2):
                    for k in range(KC):
                        last = nc.tensor.transpose(ps_t[slot][:, b, k, :], o[:, slot, b, k * P:(k + 1) * P], g.ident[:])
                last.then_inc(s_t, 1)
            transposes(0, 0)

            def turn(n, slot, more):
                pe.wait_ge(s_ot, n + 1)
                if late(n, 2):
                    pe.wait_ge(s_c, n * OUT - OUT)
                for b in range(2):
                    for k in range(KC):
                        last = nc.tensor.matmul(ps_o[slot][:, b, :], ot[:, slot, k, b, :], w[:, k, :],
                                                start=(k == 0), stop=(k == KC - 1))
                last.then_inc(s_mm, 1)
                if more:
                    transposes(n + 1, 1 - slot)
            rounds(pe, turn)

        @block.scalar
        def _(act):
            def turn(n, slot, more):
                act.wait_ge(s_t, n + 1)
                if late(n, 2):
                    act.wait_ge(s_mm, n - 1)
                nc.scalar.activation(ot[:, slot].rearrange("p k b n -> p b k n"), ps_t[slot][:], ACT.Copy).then_inc(s_ot, 1)
            rounds(act, turn)

        @block.vector
        def _(v):
            v.wait_ge(s_w, 64)

            def normalise(n, slot):
                c = Count(v, s_o, n, OPS)
                a = acc[:, bass.ds(n * 2, 2), :]
                c.then(nc.vector.tensor_scalar(rec[:, slot], a[:, :, D:AGG], 0.5, None, ALU.max))
                c.then(nc.vector.reciprocal(rec[:, slot], rec[:, slot]))
                if late(n, 2):
                    v.wait_ge(s_t, n - 1)
                c.step(nc.vector.tensor_tensor(o[:, slot].rearrange("p b (h d) -> p b h d", h=H),
                                               a[:, :, 0:D].rearrange("p b (h d) -> p b h d", h=H),
                                               rec[:, slot].unsqueeze(3).to_broadcast([P, 2, H, HD]), ALU.mult))
                c.done()
            normalise(0, 0)
            normalise(1, 1)

            def turn(n, slot, more):
                c = Count(v, s_c, n, OUT)
                wide = lambda i: vec[:, i, :].unsqueeze(1).to_broadcast([P, 2, D])
                v.wait_ge(s_mm, n + 1)
                v.wait_ge(s_x[slot], (n + (2 - slot)) * 8)
                c.then(nc.vector.tensor_tensor(t[:], ps_o[slot][:], wide(0), ALU.add))
                c.then(nc.vector.tensor_tensor(t[:], t[:], h0[:, slot], ALU.add))
                norm_begin(nc, c, stat, t, s_var)
                if more == 2:
                    normalise(n + 2, slot)
                norm_end(nc, c, stat, tn, t, s_rstd, 0, 1)
                c.then(nc.vector.tensor_tensor(tn[:], tn[:], wide(1), ALU.mult))
                if late(n, 2):
                    v.wait_ge(s_st[slot], (n - slot) * 8)
                c.then(nc.vector.tensor_tensor(h1[:, slot], tn[:], wide(2), ALU.add))
                c.done()
            rounds(v, turn)


def ffn(nc, g, name, rows, w1, b1, w2, func, loads, vectors, outs, epilogue, per, norms=0, tokens=None):
    chunks = FF // P
    count = PAIRS if tokens is None else tokens.shape[1] // 2
    x_step = 8 if tokens is None else 16
    with Phase(nc, name) as m:
        wa = m.sb("wa", [P, KC, FF])
        wb = m.sb("wb", [P, chunks, D])
        ba = m.sb("ba", [P, chunks])
        vec = m.sb("vec", [P, len(vectors), D])
        hx = m.sb("hx", [P, 2, 2, D])
        idx = m.sb("idx", [P, 2, 2], I32)
        xt = m.sb("xt", [P, 2, KC, 2 * P])
        ht = m.sb("ht", [P, 2, chunks, 2 * P])
        lin = m.sb("lin", [P, 2, max(1, len(loads)), 2, D])
        lout = m.sb("lout", [P, 2, len(outs), 2, D])
        tmp = m.sb("tmp", [P, 3, 2, D])
        stat = m.sb("stat", [P, max(1, norms), 20])
        ps_t = m.ps("ps_t", [P, KC, 2, P])
        ps_h = [m.ps(f"ps_h{i}", [P, 2 * P]) for i in range(4)]
        ps_y = [m.ps(f"ps_y{i}", [P, 2, D]) for i in range(2)]
        s_w, s_c, s_var, s_rstd, s_t, s_xt, s_up, s_act, s_y = (
            m.sem(k) for k in ("w", "c", "var", "rstd", "t", "xt", "up", "act", "y"))
        s_l, s_st = ([m.sem(f"{k}{i}") for i in range(2)] for k in ("l", "st"))
        s_x = [m.sem(f"x{i}") for i in range(2)] if tokens is None else m.sems_of_pool("x", 2)
        s_idx = m.sem("idx")
        block = m.block()
        nw = 3 + len(vectors)

        @block.sync
        def _(sp):
            def load(n, slot):
                if late(n, 2):
                    sp.wait_ge(s_t, n - 1)
                sp.dma_start(hx[:, slot], pair_rows(rows, n)).then_inc(s_x[slot], 16)
            if tokens is None:
                load(0, 0)
            sp.dma_start(wa[:], w1.rearrange("(k p) n -> p k n", p=P)).then_inc(s_w, 16)
            sp.dma_start(wb[:], w2.rearrange("(c p) n -> p c n", p=P)).then_inc(s_w, 16)
            with nc.allow_non_contiguous_dma(reason="a bias by partition"):
                sp.dma_start(ba[:], b1.rearrange("(c p) -> p c", p=P)).then_inc(s_w, 16)
            for i, r in enumerate(vectors):
                sp.dma_start(vec[:, i, :], spread(r, D)).then_inc(s_w, 16)

            def store(n, slot):
                sp.wait_ge(s_c, n * per + per)
                for i, r in enumerate(outs):
                    sp.dma_start(pair_rows(r, n), lout[:, slot, i]).then_inc(s_st[slot], 16)

            def turn(n, slot, more):
                if more and tokens is None:
                    load(n + 1, 1 - slot)
                if loads and late(n, 2):
                    sp.wait_ge(s_c, n * per - per)
                for i, r in enumerate(loads):
                    sp.dma_start(lin[:, slot, i], pair_rows(r, n)).then_inc(s_l[slot], 16)
                if late(n, 1):
                    store(n - 1, 1 - slot)
            rounds(sp, turn, count)
            store(count - 1, 0)
            sp.wait_ge(s_st[0], 16 * len(outs) * (count // 2 + 1))
            sp.wait_ge(s_st[1], 16 * len(outs) * (count // 2))

        @block.gpsimd
        def _(pool):
            def turn(n, slot, more):
                for k in range(norms):
                    pool.wait_ge(s_var, n * norms + k + 1)
                    nc.gpsimd.tensor_tensor(stat[:, k, 18:20], stat[:, k, 16:18], g.minus_half[:], ALU.pow).then_inc(s_rstd, 1)

            def gather(n, slot, more):
                if late(n, 2):
                    pool.wait_ge(s_t, n - 1)
                pool.wait_ge(s_idx, n + 1)
                pool.nop(nofuse=True)
                for b in range(2):
                    nc.gpsimd.indirect_dma_start(hx[:, slot, b, :], None, rows,
                                                 bass.IndirectOffsetOnAxis(idx[:, slot, b:b + 1], 0)).then_inc(s_x[slot], 16)
            if norms:
                rounds(pool, turn, count)
            if tokens is not None:
                rounds(pool, gather, count)

        @block.tensor
        def _(pe):
            def transposes(n, slot):
                pe.wait_ge(s_x[slot], (n + (2 - slot)) * x_step)
                if late(n, 1):
                    pe.wait_ge(s_xt, n)
                for b in range(2):
                    for k in range(KC):
                        last = nc.tensor.transpose(ps_t[:, k, b, :], hx[:, slot, b, k * P:(k + 1) * P], g.ident[:])
                last.then_inc(s_t, 1)
            transposes(0, 0)
            pe.wait_ge(s_w, 16 * nw)

            def turn(n, slot, more):
                pe.wait_ge(s_xt, n + 1)
                for c in range(chunks):
                    if late(n, 1) or c >= 4:
                        pe.wait_ge(s_act, n * chunks + c - 3)
                    for k in range(KC):
                        last = nc.tensor.matmul(ps_h[c % 4][:, :], wa[:, k, c * P:(c + 1) * P], xt[:, slot, k, :],
                                                start=(k == 0), stop=(k == KC - 1))
                    last.then_inc(s_up, 1)
                if more:
                    transposes(n + 1, 1 - slot)
                if late(n, 2):
                    pe.wait_ge(s_c, n * per - per)
                for b in range(2):
                    for c in range(chunks):
                        if b == 0:
                            pe.wait_ge(s_act, n * chunks + c + 1)
                        last = nc.tensor.matmul(ps_y[slot][:, b, :], ht[:, slot, c, b * P:(b + 1) * P],
                                                wb[:, c, :], start=(c == 0), stop=(c == chunks - 1))
                last.then_inc(s_y, 1)
            rounds(pe, turn, count)

        @block.scalar
        def _(act):
            act.wait_ge(s_w, 16 * nw)

            def evac_xt(n, slot):
                act.wait_ge(s_t, n + 1)
                nc.scalar.activation(xt[:, slot, :, :], ps_t[:].rearrange("p k b n -> p k (b n)"), ACT.Copy).then_inc(s_xt, 1)

            def index(n, slot):
                if late(n, 2):
                    act.wait_ge(s_x[slot], (n - slot) * x_step)
                nc.scalar.activation(idx[:, slot], tokens[:, bass.ds(n * 2, 2)], ACT.Copy).then_inc(s_idx, 1)
            if tokens is not None:
                index(0, 0)
                index(1, 1)
            evac_xt(0, 0)

            def turn(n, slot, more):
                if tokens is not None and more == 2:
                    index(n + 2, slot)
                if late(n, 2):
                    act.wait_ge(s_y, n - 1)
                for c in range(chunks):
                    act.wait_ge(s_up, n * chunks + c + 1)
                    nc.scalar.activation(ht[:, slot, c, :], ps_h[c % 4][:, :], func,
                                         bias=ba[:, c:c + 1]).then_inc(s_act, 1)
                if more:
                    evac_xt(n + 1, 1 - slot)
            rounds(act, turn, count)

        @block.vector
        def _(v):
            v.wait_ge(s_w, 16 * nw)

            def turn(n, slot, more):
                c = Count(v, s_c, n, per)
                v.wait_ge(s_y, n + 1)
                if loads:
                    v.wait_ge(s_l[slot], (n + (2 - slot)) * (8 * len(loads)))
                if late(n, 2):
                    v.wait_ge(s_st[slot], (n - slot) * (8 * len(outs)))
                epilogue(nc, g, c, n, ps_y[slot], [lin[:, slot, i] for i in range(len(loads))],
                         [vec[:, i, :] for i in range(len(vectors))], [tmp[:, i] for i in range(3)],
                         [lout[:, slot, i] for i in range(len(outs))], [stat[:, k] for k in range(norms)], s_var, s_rstd)
                c.done()
            rounds(v, turn, count)


def wide(row):
    return row.unsqueeze(1).to_broadcast([P, 2, D])


def after_graph(nc, g, c, n, y, loads, vecs, tmp, outs, stats, s_var, s_rstd):
    hid, x = loads
    b2, ln_g, ln_b, wr = vecs
    t, u, z = tmp
    c.then(nc.vector.tensor_tensor(t, y[:], wide(b2), ALU.add))
    c.then(nc.vector.tensor_tensor(t, t, hid, ALU.add))
    norm_pair(nc, g, c, stats[0], u, t, s_var, s_rstd, 0, 2)
    c.then(nc.vector.tensor_tensor(u, u, wide(ln_g), ALU.mult))
    c.then(nc.vector.tensor_tensor(u, u, wide(ln_b), ALU.add))
    c.then(nc.vector.tensor_tensor(z, u, x, ALU.add))
    norm_pair(nc, g, c, stats[1], outs[1], z, s_var, s_rstd, 1, 2)
    c.then(nc.vector.tensor_tensor(outs[0], z, outs[1], ALU.add))
    c.then(nc.vector.tensor_tensor(t, outs[1], wide(wr), ALU.mult))
    c.then(nc.vector.tensor_reduce(g.weight[:, bass.ds(n * 2, 2)], t, AX.X, ALU.add))


def biased(nc, g, c, n, y, loads, vecs, tmp, outs, stats, s_var, s_rstd):
    c.then(nc.vector.tensor_tensor(outs[0], y[:], wide(vecs[0]), ALU.add))


HALF_BITS = 16
DIGIT = 4
TRIES = (1 << DIGIT) - 1
assert NPAD < 1 << HALF_BITS


def keep_top(nc, g):
    with Phase(nc, "top") as m:
        br = m.sb("br", [P, 1])
        bits = m.sb("bits", [P, BLOCKS], I32)
        sign = m.sb("sign", [P, BLOCKS], I32)
        half_i = m.sb("half_i", [P, BLOCKS], I32)
        real = m.sb("real", [P, BLOCKS])
        high = m.sb("high", [P, BLOCKS])
        low = m.sb("low", [P, BLOCKS])
        t = m.sb("t", [P, BLOCKS])
        hit = m.sb("hit", [P, TRIES, BLOCKS])
        same = m.sb("same", [P, BLOCKS])
        cnt = m.sb("cnt", [P, TRIES])
        ones = m.sb("ones", [P, P])
        thr = m.sb("thr", [P, 3])
        tries = m.sb("tries", [P, TRIES])
        cand = m.sb("cand", [P, TRIES])
        passed = m.sb("passed", [P, TRIES])
        need = m.sb("need", [P, 1])
        digit = m.sb("digit", [P, 1])
        before = m.sb("before", [P, P])
        run = m.sb("run", [P, BLOCKS + 1])
        zero = m.sb("zero", [P, BLOCKS])
        ps = m.ps("ps", [P, 512])
        ps_r = m.ps("ps_r", [P, 2, BLOCKS])
        s_in, s_v, s_pe, s_cnt, s_pool = (m.sem(x) for x in ("in", "v", "pe", "cnt", "pool"))
        block = m.block()
        counts = 3 * (HALF_BITS // DIGIT) + 2

        @block.sync
        def _(sp):
            sp.dma_start(br[:], g.br.rearrange("(a n) -> a n", a=1).to_broadcast([P, 1])).then_inc(s_in, 16)

        @block.gpsimd
        def _(pool):
            nc.gpsimd.iota(tries[:], [[1, TRIES]], 1, 0, allow_small_or_imprecise_dtypes=True).then_inc(s_pool, 1)
            nc.gpsimd.memset(before[:], 1.0).then_inc(s_pool, 1)
            pool.wait_ge(s_pool, 2)
            nc.gpsimd.affine_select(out=before[:], in_=before[:], compare_op=ALU.is_gt, fill=0.0,
                                    base=0, pattern=[[1, P]], channel_multiplier=-1).then_inc(s_pool, 1)

        @block.tensor
        def _(pe):
            with pe.Fori(0, counts) as i:
                pe.wait_ge(s_cnt, i + 1)
                nc.tensor.matmul(ps[:, 0:TRIES], ones[:], cnt[:], start=True, stop=True).then_inc(s_pe, 1)
            pe.wait_ge(s_cnt, counts + 1)
            pe.wait_ge(s_pool, 3)
            nc.tensor.matmul(ps_r[:, 0, :], before[:], g.keep[:], start=True, stop=True)
            nc.tensor.matmul(ps_r[:, 1, :], ones[:], g.keep[:], start=True, stop=True).then_inc(s_pe, 1)

        @block.vector
        def _(v):
            ch = Chain(v, s_v)
            ts, tt = nc.vector.tensor_scalar, nc.vector.tensor_tensor
            ch.after(nc.vector.memset(ones[:], 1.0))
            ch.after(nc.vector.memset(thr[:], 0.0))
            v.wait_ge(s_in, 16)
            v.wait_ge(s_pool, 1)
            ch.after(ts(g.weight[:], g.weight[:], br[:, 0:1], None, ALU.add))
            ch.after(ts(real[:], g.node[:], float(N), None, ALU.is_lt))
            w = g.weight[:].bitcast(I32)
            ch.after(ts(sign[:], w, 31, None, ALU.arith_shift_right))
            ch.after(ts(sign[:], sign[:], -2147483648, None, ALU.bitwise_or))
            ch.after(tt(bits[:], w, sign[:], ALU.bitwise_xor))
            for half, op, by in ((high, ALU.logical_shift_right, 16), (low, ALU.bitwise_and, 0xFFFF)):
                ch.after(ts(half_i[:], bits[:], by, None, op))
                ch.after(ts(half[:], half_i[:], 1.0, None, ALU.add))
                ch.after(tt(half[:], half[:], real[:], ALU.mult))
                ch.after(ts(half[:], half[:], -1.0, None, ALU.add))
            ch.after(nc.vector.memset(need[:], float(KEEP)))
            done = [0]

            def total():
                nc.vector.tensor_reduce(cnt[:], hit[:], AX.X, ALU.add).then_inc(s_cnt, 1)
                done[0] += 1
                v.wait_ge(s_pe, done[0])

            def search(val, at, op, pred):
                for shift in range(HALF_BITS - DIGIT, -1, -DIGIT):
                    ch.after(ts(cand[:], tries[:], float(1 << shift), thr[:, at:at + 1], ALU.mult, ALU.add))
                    ch.after(tt(hit[:], val[:].unsqueeze(1).to_broadcast([P, TRIES, BLOCKS]),
                                cand[:].unsqueeze(2).to_broadcast([P, TRIES, BLOCKS]), op))
                    total()
                    ch.after(ts(passed[:], ps[:, 0:TRIES], need[:, 0:1], None, pred))
                    ch.after(nc.vector.tensor_reduce(digit[:], passed[:], AX.X, ALU.add))
                    ch.after(ts(digit[:], digit[:], float(1 << shift), None, ALU.mult))
                    ch.after(tt(thr[:, at:at + 1], thr[:, at:at + 1], digit[:], ALU.add))

            def above(val, at):
                ch.after(ts(hit[:, 0, :], val[:], thr[:, at:at + 1], None, ALU.is_gt))
                ch.after(tt(g.keep[:], g.keep[:], hit[:, 0, :], ALU.add))
                total()
                ch.after(tt(need[:], need[:], ps[:, 0:1], ALU.subtract))

            def among(val, at):
                ch.after(ts(t[:], val[:], thr[:, at:at + 1], None, ALU.is_equal))

            ch.after(nc.vector.memset(g.keep[:], 0.0))
            search(high, 0, ALU.is_ge, ALU.is_ge)
            above(high, 0)
            among(high, 0)
            ch.after(ts(low[:], low[:], 1.0, None, ALU.add))
            ch.after(tt(low[:], low[:], t[:], ALU.mult))
            ch.after(ts(low[:], low[:], -1.0, None, ALU.add))
            search(low, 1, ALU.is_ge, ALU.is_ge)
            above(low, 1)
            among(low, 1)
            ch.after(ts(same[:], t[:], -float(NPAD), float(NPAD), ALU.mult, ALU.add))
            ch.after(tt(same[:], same[:], g.node[:], ALU.add))
            search(same, 2, ALU.is_lt, ALU.is_lt)
            ch.after(ts(hit[:, 0, :], same[:], thr[:, 2:3], None, ALU.is_le))
            tt(g.keep[:], g.keep[:], hit[:, 0, :], ALU.add).then_inc(s_cnt, 1)
            assert done[0] == counts
            ch.after(nc.vector.memset(zero[:], 0.0))
            ch.after(nc.vector.memset(run[:], 0.0))
            v.wait_ge(s_pe, counts + 1)
            ch.after(nc.vector.tensor_tensor_scan(run[:, 1:BLOCKS + 1], zero[:], ps_r[:, 1, :], 0.0, ALU.add, ALU.add))
            ch.after(tt(t[:], run[:, 0:BLOCKS], ps_r[:, 0, :], ALU.add))
            ch.after(tt(g.kept_pos[:, 0], t[:], g.keep[:], ALU.mult))
            ch.after(nc.vector.tensor_copy(g.from_kept[:], g.kept_pos[:, 0]))
            ch.after(tt(g.kept_node[:], g.node[:], g.keep[:], ALU.mult))
            ch.after(tt(g.factor[:], g.weight[:], g.keep[:], ALU.mult))


def project_heads(nc, g, s_dst):
    with Phase(nc, "hds") as m:
        w = m.sb("w", [P, KC, D])
        vec = m.sb("vec", [P, 2, D])
        r = m.sb("r", [P, 2, 2, 2, D])
        x2 = m.sb("x2", [P, 2, 2, D])
        xn = m.sb("xn", [P, 2, 2, D])
        xt = m.sb("xt", [P, 2, KC, 2, P])
        hh = m.sb("hh", [P, 2, 2, D])
        att = m.sb("att", [P, 2, 2, D])
        src = m.sb("src", [P, 2, 2, H])
        stat = m.sb("stat", [P, 2, 20])
        idx = m.sb("idx", [P, 2, 2], I32)
        ps_t = [m.ps(f"ps_t{i}", [P, 2, KC, P]) for i in range(2)]
        ps_o = [m.ps(f"ps_o{i}", [P, 2, D]) for i in range(2)]
        s_w, s_ln, s_var, s_rstd, s_t, s_xt, s_mm, s_hh, s_a = (
            m.sem(k) for k in ("w", "ln", "var", "rstd", "t", "xt", "mm", "hh", "a"))
        s_idx, s_y = m.sem("idx"), m.sems_of_pool("y", 2)
        s_x, s_xnst, s_hst, s_sst = ([m.sem(f"{k}{i}") for i in range(2)] for k in ("x", "xnst", "hst", "sst"))
        block = m.block()
        LN, AT = 1 + LN_STEPS, 2

        @block.sync
        def _(sp):
            def load(n, slot):
                sp.dma_start(r[:, slot, 0], pair_rows(g.resid, n)).then_inc(s_x[slot], 16)
            load(0, 0)
            load(1, 1)
            sp.dma_start(w[:], g.W.rearrange("(k p) n -> p k n", p=P)).then_inc(s_w, 16)
            for i, a in enumerate((g.a_src, g.a_dst)):
                sp.dma_start(vec[:, i, :], spread(a.rearrange("h d -> (h d)"), D)).then_inc(s_w, 16)

            def turn(n, slot, more):
                sp.wait_ge(s_ln, n * LN + LN)
                if more == 2:
                    load(n + 2, slot)
                sp.dma_start(pair_rows(g.norm, n), xn[:, slot]).then_inc(s_xnst[slot], 16)
                sp.dma_start(pair_rows(g.x2, n), x2[:, slot]).then_inc(s_xnst[slot], 16)
                sp.wait_ge(s_hh, n + 1)
                sp.dma_start(pair_rows(g.v_rows, n), hh[:, slot]).then_inc(s_hst[slot], 16)
                if late(n, 1):
                    store_src(n - 1, 1 - slot)

            def store_src(n, slot):
                sp.wait_ge(s_a, n * AT * 2 + 2)
                sp.dma_start(pair_rows(g.s_src, n), src[:, slot]).then_inc(s_sst[slot], 16)
            rounds(sp, turn)
            store_src(PAIRS - 1, 0)
            for i, k in enumerate((PAIRS // 2 + 1, PAIRS // 2)):
                sp.wait_ge(s_xnst[i], 32 * k)
                sp.wait_ge(s_hst[i], 16 * k)
                sp.wait_ge(s_sst[i], 16 * k)

        @block.gpsimd
        def _(pool):
            def gather(n, slot):
                if late(n, 2):
                    pool.wait_ge(s_ln, n * LN - LN)
                pool.wait_ge(s_idx, n + 1)
                pool.nop(nofuse=True)
                for b in range(2):
                    nc.gpsimd.indirect_dma_start(r[:, slot, 1, b, :], None, g.kept_y,
                                                 bass.IndirectOffsetOnAxis(idx[:, slot, b:b + 1], 0)).then_inc(s_y[slot], 16)
            gather(0, 0)
            gather(1, 1)

            def turn(n, slot, more):
                pool.wait_ge(s_var, n + 1)
                nc.gpsimd.tensor_tensor(stat[:, slot, 18:20], stat[:, slot, 16:18], g.minus_half[:], ALU.pow).then_inc(s_rstd, 1)
                if more == 2:
                    gather(n + 2, slot)
            rounds(pool, turn)

        @block.vector
        def _(v):
            def begin(n, slot):
                c = Count(v, s_ln, n, LN)
                v.wait_ge(s_x[slot], (n + (2 - slot)) * 8)
                v.wait_ge(s_y[slot], (n + (2 - slot)) * 16)
                if late(n, 2):
                    v.wait_ge(s_xnst[slot], (n - slot) * 16)
                    v.wait_ge(s_t, n - 1)
                for b in range(2):
                    ins = nc.vector.scalar_tensor_tensor(x2[:, slot, b, :], r[:, slot, 1, b, :],
                                                         g.factor[:, bass.ds(n * 2 + b, 1)], r[:, slot, 0, b, :],
                                                         ALU.mult, ALU.add)
                c.then(ins)
                norm_begin(nc, c, stat[:, slot], x2[:, slot], s_var)
                return c

            def end(c, slot):
                norm_end(nc, c, stat[:, slot], xn[:, slot], x2[:, slot], s_rstd, 0, 1)
                c.done()

            def attend(n, slot):
                v.wait_ge(s_hh, n + 1)
                c = Count(v, s_a, n, 2 * AT)
                if late(n, 2):
                    v.wait_ge(s_sst[slot], (n - slot) * 8)
                outs = (src[:, slot], s_dst[:, bass.ds(n * 2, 2), :])
                for i in range(2):
                    c.then(nc.vector.tensor_tensor(att[:, i], hh[:, slot], wide(vec[:, i, :]), ALU.mult))
                    c.then(nc.vector.tensor_reduce(outs[i], att[:, i].rearrange("p b (h d) -> p b h d", h=H), AX.X, ALU.add))
                c.done()

            end(begin(0, 0), 0)
            v.wait_ge(s_w, 48)

            def turn(n, slot, more):
                if more:
                    c = begin(n + 1, 1 - slot)
                if late(n, 1):
                    attend(n - 1, 1 - slot)
                if more:
                    end(c, 1 - slot)
            rounds(v, turn)
            attend(PAIRS - 1, 0)

        @block.tensor
        def _(pe):
            def transposes(n, slot):
                pe.wait_ge(s_ln, n * LN + LN)
                if late(n, 2):
                    pe.wait_ge(s_xt, n - 1)
                for b in range(2):
                    for k in range(KC):
                        last = nc.tensor.transpose(ps_t[slot][:, b, k, :], xn[:, slot, b, k * P:(k + 1) * P], g.ident[:])
                last.then_inc(s_t, 1)
            transposes(0, 0)
            pe.wait_ge(s_w, 48)

            def turn(n, slot, more):
                pe.wait_ge(s_xt, n + 1)
                if late(n, 2):
                    pe.wait_ge(s_hh, n - 1)
                for b in range(2):
                    for k in range(KC):
                        last = nc.tensor.matmul(ps_o[slot][:, b, :], xt[:, slot, k, b, :], w[:, k, :],
                                                start=(k == 0), stop=(k == KC - 1))
                last.then_inc(s_mm, 1)
                if more:
                    transposes(n + 1, 1 - slot)
            rounds(pe, turn)

        @block.scalar
        def _(act):
            def evac_xt(n, slot):
                act.wait_ge(s_t, n + 1)
                if late(n, 2):
                    act.wait_ge(s_mm, n - 1)
                nc.scalar.activation(xt[:, slot].rearrange("p k b n -> p b k n"), ps_t[slot][:], ACT.Copy).then_inc(s_xt, 1)

            def index(n, slot):
                if late(n, 2):
                    act.wait_ge(s_y[slot], (n - slot) * 16)
                nc.scalar.activation(idx[:, slot], g.from_kept[:, bass.ds(n * 2, 2)], ACT.Copy).then_inc(s_idx, 1)
            index(0, 0)
            index(1, 1)
            evac_xt(0, 0)

            def turn(n, slot, more):
                if more == 2:
                    index(n + 2, slot)
                act.wait_ge(s_mm, n + 1)
                if late(n, 2):
                    act.wait_ge(s_hst[slot], (n - slot) * 8)
                    act.wait_ge(s_a, n * 2 * AT - 2 * AT)
                nc.scalar.activation(hh[:, slot], ps_o[slot][:], ACT.Copy).then_inc(s_hh, 1)
                if more:
                    evac_xt(n + 1, 1 - slot)
            rounds(act, turn)


def graph2_out(nc, g, acc, logits):
    with Phase(nc, "out2") as m:
        w = m.sb("w", [P, KC, EXPERTS])
        vec = m.sb("vec", [P, 2, D])
        lin = m.sb("lin", [P, 2, 2, 2, D])
        rec = m.sb("rec", [P, 2, H])
        t = m.sb("t", [P, 2, 2, D])
        u = m.sb("u", [P, 2, D])
        z = m.sb("z", [P, 2, 2, D])
        low = m.sb("low", [P, 2, 2, D])
        el = m.sb("el", [P, 2, 2, D])
        lout = m.sb("lout", [P, 2, 2, 2, D])
        xt = m.sb("xt", [P, 2, KC, 2, P])
        stat = m.sb("stat", [P, 2, 20])
        ps_t = [m.ps(f"ps_t{i}", [P, 2, KC, P]) for i in range(2)]
        ps_l = [m.ps(f"ps_l{i}", [P, 2, EXPERTS]) for i in range(2)]
        s_w, s_a, s_c, s_var, s_rstd, s_var2, s_rstd2, s_t, s_xt, s_mm, s_log, s_low, s_el = (
            m.sem(k) for k in ("w", "a", "c", "var", "rstd", "var2", "rstd2", "t", "xt", "mm", "log", "low", "el"))
        s_norm, s_x2, s_st = ([m.sem(f"{k}{i}") for i in range(2)] for k in ("norm", "x2", "st"))
        block = m.block()
        PER_A, PER = 6 + LN_STEPS, 2 + LN_STEPS

        @block.sync
        def _(sp):
            sp.dma_start(w[:], g.router_t.rearrange("(k p) n -> p k n", p=P)).then_inc(s_w, 16)
            for i, a in enumerate((g.gamma, g.beta)):
                sp.dma_start(vec[:, i, :], spread(a, D)).then_inc(s_w, 16)

            def store(n, slot):
                sp.wait_ge(s_c, n * PER + PER)
                sp.dma_start(pair_rows(g.x3, n), lout[:, slot, 0]).then_inc(s_st[slot], 16)
                sp.dma_start(pair_rows(g.x3n, n), lout[:, slot, 1]).then_inc(s_st[slot], 16)

            def turn(n, slot, more):
                if more == 2:
                    sp.wait_ge(s_a, n * PER_A + PER_A)
                    load_norm(n + 2, slot)
                if late(n, 1):
                    store(n - 1, 1 - slot)
                if more:
                    load_x2(n + 1, 1 - slot)

            def load_norm(n, slot):
                sp.dma_start(lin[:, slot, 0], pair_rows(g.norm, n)).then_inc(s_norm[slot], 16)

            def load_x2(n, slot):
                sp.dma_start(lin[:, slot, 1], pair_rows(g.x2, n)).then_inc(s_x2[slot], 16)

            load_norm(0, 0)
            load_norm(1, 1)
            load_x2(0, 0)
            rounds(sp, turn)
            store(PAIRS - 1, 0)
            sp.wait_ge(s_st[0], 32 * (PAIRS // 2 + 1))
            sp.wait_ge(s_st[1], 32 * (PAIRS // 2))

        @block.gpsimd
        def _(pool):
            def turn(n, slot, more):
                if more:
                    root(n + 1, 0, s_var, s_rstd)
                root(n, 1, s_var2, s_rstd2)

            def root(n, k, variance, done):
                pool.wait_ge(variance, n + 1)
                nc.gpsimd.tensor_tensor(stat[:, k, 18:20], stat[:, k, 16:18], g.minus_half[:], ALU.pow).then_inc(done, 1)
            root(0, 0, s_var, s_rstd)
            rounds(pool, turn)

        @block.scalar
        def _(act):
            def exp(n, slot):
                act.wait_ge(s_low, n + 1)
                if late(n, 2):
                    act.wait_ge(s_c, n * PER - PER)
                nc.scalar.activation(el[:, slot], low[:, slot], ACT.Exp).then_inc(s_el, 1)
            exp(0, 0)

            def turn(n, slot, more):
                if more:
                    exp(n + 1, 1 - slot)
                act.wait_ge(s_t, n + 1)
                if late(n, 2):
                    act.wait_ge(s_mm, n - 1)
                nc.scalar.activation(xt[:, slot].rearrange("p k b n -> p b k n"), ps_t[slot][:], ACT.Copy).then_inc(s_xt, 1)
                act.wait_ge(s_mm, n + 1)
                nc.scalar.activation(logits[:, bass.ds(n * 2, 2), :], ps_l[slot][:], ACT.Copy).then_inc(s_log, 1)
            rounds(act, turn)

        @block.tensor
        def _(pe):
            pe.wait_ge(s_w, 48)

            def turn(n, slot, more):
                pe.wait_ge(s_c, n * PER + PER)
                if late(n, 2):
                    pe.wait_ge(s_xt, n - 1)
                for b in range(2):
                    for k in range(KC):
                        last = nc.tensor.transpose(ps_t[slot][:, b, k, :], lout[:, slot, 1, b, k * P:(k + 1) * P], g.ident[:])
                last.then_inc(s_t, 1)
                pe.wait_ge(s_xt, n + 1)
                if late(n, 2):
                    pe.wait_ge(s_log, n - 1)
                for b in range(2):
                    for k in range(KC):
                        last = nc.tensor.matmul(ps_l[slot][:, b, :], xt[:, slot, k, b, :], w[:, k, :],
                                                start=(k == 0), stop=(k == KC - 1))
                last.then_inc(s_mm, 1)
            rounds(pe, turn)

        @block.vector
        def _(v):
            v.wait_ge(s_w, 48)

            tt = nc.vector.tensor_tensor

            def a_begin(n, slot):
                c = Count(v, s_a, n, PER_A)
                a = acc[:, bass.ds(n * 2, 2), :]
                c.then(nc.vector.tensor_scalar(rec[:], a[:, :, D:AGG], 0.5, None, ALU.max))
                c.then(nc.vector.reciprocal(rec[:], rec[:]))
                c.then(tt(t[:, 0].rearrange("p b (h d) -> p b h d", h=H), a[:, :, 0:D].rearrange("p b (h d) -> p b h d", h=H),
                          rec[:].unsqueeze(3).to_broadcast([P, 2, H, HD]), ALU.mult))
                v.wait_ge(s_norm[slot], (n + (2 - slot)) * 8)
                c.then(tt(t[:, 0], t[:, 0], lin[:, slot, 0], ALU.add))
                norm_begin(nc, c, stat[:, 0], t[:, 0], s_var)
                return c

            def a_end(c, n, slot):
                norm_end(nc, c, stat[:, 0], u[:], t[:, 0], s_rstd, 0, 1)
                c.then(tt(u[:], u[:], wide(vec[:, 0, :]), ALU.mult))
                c.then(tt(z[:, slot], u[:], wide(vec[:, 1, :]), ALU.add))
                if late(n, 2):
                    v.wait_ge(s_el, n - 1)
                nc.vector.tensor_scalar(low[:, slot], z[:, slot], 0.0, None, ALU.min).then_inc(s_low, 1)
                c.done()

            def b_begin(n, slot):
                c = Count(v, s_c, n, PER)
                v.wait_ge(s_el, n + 1)
                c.then(nc.vector.scalar_tensor_tensor(t[:, 1].rearrange("p b d -> p (b d)"),
                                                      el[:, slot].rearrange("p b d -> p (b d)"), -1.0,
                                                      z[:, slot].rearrange("p b d -> p (b d)"), ALU.add, ALU.max))
                if late(n, 2):
                    v.wait_ge(s_st[slot], (n - slot) * 16)
                    v.wait_ge(s_t, n - 1)
                v.wait_ge(s_x2[slot], (n + (2 - slot)) * 8)
                c.then(tt(lout[:, slot, 0], t[:, 1], lin[:, slot, 1], ALU.add))
                norm_begin(nc, c, stat[:, 1], lout[:, slot, 0], s_var2)
                return c

            def b_end(c, slot):
                norm_end(nc, c, stat[:, 1], lout[:, slot, 1], lout[:, slot, 0], s_rstd2, 0, 1)
                c.done()

            a_end(a_begin(0, 0), 0, 0)

            def turn(n, slot, more):
                if more:
                    a = a_begin(n + 1, 1 - slot)
                b = b_begin(n, slot)
                if more:
                    a_end(a, n + 1, 1 - slot)
                b_end(b, slot)
            rounds(v, turn)
            v.wait_ge(s_log, PAIRS)


def route(nc, g, logits):
    with Phase(nc, "route") as m:
        B, X = BLOCKS, EXPERTS
        col = m.sb("col", [P, B, X])
        mx = m.sb("mx", [P, B])
        e = m.sb("e", [P, B, X])
        eq = m.sb("eq", [P, B, X])
        one = [m.sb(f"one{i}", [P, B, X]) for i in range(2)]
        pr = m.sb("pr", [P, 3, B])
        real = m.sb("real", [P, B])
        both = m.sb("both", [P, B, X])
        before = m.sb("before", [P, P])
        ones = m.sb("ones", [P, P])
        rank = m.sb("rank", [P, B, X])
        tot = m.sb("tot", [P, B, X])
        run = m.sb("run", [P, B + 1, X])
        zero = m.sb("zero", [P, B])
        cnt_i = m.sb("cnt_i", [P, X], I32)
        tiles = m.sb("tiles", [P, X])
        ends = m.sb("ends", [P, X + 1])
        base = m.sb("base", [P, X])
        tile_no = m.sb("tile_no", [P, MAX_TILES])
        over = m.sb("over", [P, MAX_TILES])
        tile_f = m.sb("tile_f", [P, MAX_TILES])
        tmp = m.sb("tmp", [P, B, X])
        ps_r = m.ps("ps_r", [P, 512])
        ps_o = m.ps("ps_o", [P, 512])
        s_i, s_v, s_pe, s_m = (m.sem(x) for x in ("i", "v", "pe", "m"))
        block = m.block()

        @block.sync
        def _(sp):
            for e in range(EXPERTS):
                for i, t in enumerate((g.w1_t, g.w3_t)):
                    sp.dma_start(g.w13[:, e, :, i, :], t[e].rearrange("(k p) h -> p k h", p=P)).then_inc(g.s_experts, 16)
                full = (EC - 1) * P
                sp.dma_start(g.w2_sb[:, e, 0:EC - 1, :], g.w2_t[e, 0:full].rearrange("(c p) d -> p c d", p=P)).then_inc(g.s_experts, 16)
                sp.dma_start(g.w2_sb[0:EH - full, e, EC - 1, :], g.w2_t[e, full:EH]).then_inc(g.s_experts, 16)

        @block.gpsimd
        def _(pool):
            nc.gpsimd.iota(col[:], [[0, B], [1, X]], 0, 0, allow_small_or_imprecise_dtypes=True).then_inc(s_i, 1)
            nc.gpsimd.iota(tile_no[:], [[1, MAX_TILES]], 0, 0, allow_small_or_imprecise_dtypes=True).then_inc(s_i, 1)
            nc.gpsimd.memset(before[:], 1.0).then_inc(s_i, 1)
            pool.wait_ge(s_i, 3)
            nc.gpsimd.affine_select(out=before[:], in_=before[:], compare_op=ALU.is_gt, fill=0.0,
                                    base=0, pattern=[[1, P]], channel_multiplier=-1).then_inc(s_i, 1)

        @block.tensor
        def _(pe):
            pe.wait_ge(s_i, 4)
            pe.wait_ge(s_m, 1)
            flat = both[:].rearrange("p b x -> p (b x)")
            nc.tensor.matmul(ps_r[:, 0:B * X], before[:], flat, start=True, stop=True)
            nc.tensor.matmul(ps_o[:, 0:B * X], ones[:], flat, start=True, stop=True).then_inc(s_pe, 1)

        @block.vector
        def _(v):
            ch = Chain(v, s_v)
            ts, tt, red = nc.vector.tensor_scalar, nc.vector.tensor_tensor, nc.vector.tensor_reduce
            wide_x = lambda a: a.unsqueeze(2).to_broadcast([P, B, X])
            ch.after(nc.vector.memset(ones[:], 1.0))
            ch.after(nc.vector.memset(zero[:], 0.0))
            ch.after(nc.vector.memset(run[:], 0.0))
            ch.after(nc.vector.memset(ends[:], 0.0))
            ch.after(ts(real[:], g.node[:], float(N), None, ALU.is_lt))
            v.wait_ge(s_i, 4)
            ch.after(red(mx[:], logits[:], AX.X, ALU.max))
            ch.after(tt(e[:], logits[:], wide_x(mx[:]), ALU.subtract))
            v.sem_inc(g.s_exp, 1)
            v.wait_ge(g.s_exp, 2)
            ch.after(tt(e[:], g.exp_out[:], wide_x(real[:]), ALU.mult))
            ch.after(red(pr[:, 2], g.exp_out[:], AX.X, ALU.add))
            ch.after(nc.vector.reciprocal(pr[:, 2], pr[:, 2]))
            ch.after(tt(e[:], g.exp_out[:], wide_x(pr[:, 2]), ALU.mult))
            for i in range(2):
                ch.after(red(pr[:, i], e[:], AX.X, ALU.max))
                ch.after(tt(eq[:], e[:], wide_x(pr[:, i]), ALU.is_lt))
                ch.after(ts(eq[:], eq[:], float(X), None, ALU.mult))
                ch.after(tt(eq[:], eq[:], col[:], ALU.add))
                ch.after(red(mx[:], eq[:], AX.X, ALU.min))
                ch.after(tt(one[i][:], col[:], wide_x(mx[:]), ALU.is_equal))
                ch.after(ts(eq[:], one[i][:], -4.0, None, ALU.mult))
                ch.after(tt(e[:], e[:], eq[:], ALU.add))
                ch.after(tt(one[i][:], one[i][:], wide_x(real[:]), ALU.mult))
            ch.after(tt(pr[:, 2], pr[:, 0], pr[:, 1], ALU.add))
            ch.after(ts(pr[:, 2], pr[:, 2], 1e-9, None, ALU.add))
            ch.after(nc.vector.reciprocal(pr[:, 2], pr[:, 2]))
            for i in range(2):
                ch.after(tt(g.gate[:, i], pr[:, i], pr[:, 2], ALU.mult))
            tt(both[:], one[0][:], one[1][:], ALU.add).then_inc(s_m, 1)
            v.wait_ge(s_pe, 1)
            ch.after(nc.vector.tensor_copy(rank[:].rearrange("p b x -> p (b x)"), ps_r[:, 0:B * X]))
            ch.after(nc.vector.tensor_copy(tot[:].rearrange("p b x -> p (b x)"), ps_o[:, 0:B * X]))
            for x in range(X):
                ch.after(nc.vector.tensor_tensor_scan(run[:, 1:B + 1, x], zero[:], tot[:, :, x], 0.0, ALU.add, ALU.add))
            ch.after(ts(cnt_i[:], run[:, B, :], float(P - 1), None, ALU.add))
            ch.after(ts(cnt_i[:], cnt_i[:], 7, None, ALU.arith_shift_right))
            ch.after(nc.vector.tensor_copy(tiles[:], cnt_i[:]))
            ch.after(nc.vector.tensor_tensor_scan(ends[:, 1:X + 1], zero[:, 0:X], tiles[:], 0.0, ALU.add, ALU.add))
            ch.after(ts(base[:], ends[:, 0:X], float(P), None, ALU.mult))
            ch.after(tt(rank[:], rank[:], run[:, 0:B, :], ALU.add))
            ch.after(tt(rank[:], rank[:], base[:].unsqueeze(1).to_broadcast([P, B, X]), ALU.add))
            ch.after(tt(g.real_node[:], g.node[:], real[:], ALU.mult))
            for i in range(2):
                ch.after(tt(tmp[:], one[i][:], rank[:], ALU.mult))
                ch.after(red(g.pos[:, i], tmp[:], AX.X, ALU.add))
                ch.after(nc.vector.tensor_copy(g.from_slot[:, :, i], g.pos[:, i]))
            ch.after(nc.vector.memset(tile_f[:], 0.0))
            for x in range(1, X):
                ch.after(ts(over[:], tile_no[:], ends[:, x:x + 1], None, ALU.is_ge))
                ch.after(tt(tile_f[:], tile_f[:], over[:], ALU.add))
            ch.after(nc.vector.tensor_copy(g.tile_expert[0:1, 0:MAX_TILES], tile_f[0:1, :]))

        @block.scalar
        def _(act):
            act.wait_ge(g.s_exp, 1)
            nc.scalar.activation(g.exp_out[:], e[:], ACT.Exp).then_inc(g.s_exp, 1)


def invert(nc, g, pos, value, tiles, out):
    lists, part = pos.shape[1], 10
    parts = lists * BLOCKS // part
    assert BLOCKS % part == 0
    with Phase(nc, g.next_name("inv")) as m:
        pos_i = m.sb("pos_i", [P, lists, BLOCKS], I32)
        piece_i = m.sb("piece_i", [P, 2, lists, BLOCKS], I32)
        piece = m.sb("piece", [P, 2, lists, BLOCKS])
        tile_no = m.sb("tile_no", [P, tiles])
        lanes = m.sb("lanes", [P, 2, part, P])
        marks = m.sb("marks", [P, 2, part, tiles])
        ps = m.ps("ps", [P, 512])
        s_i, s_v, s_ready, s_mm = (m.sem(k) for k in ("i", "v", "ready", "mm"))
        block = m.block()

        @block.gpsimd
        def _(pool):
            nc.gpsimd.iota(tile_no[:], [[1, tiles]], 0, 0, allow_small_or_imprecise_dtypes=True).then_inc(s_i, 1)

        @block.tensor
        def _(pe):
            for n in range(parts):
                pe.wait_ge(s_ready, 2 * n + 2)
                for b in range(part):
                    last = nc.tensor.matmul(ps[:, 0:tiles], lanes[:, n % 2, b, :], marks[:, n % 2, b, :],
                                            start=(n == 0 and b == 0), stop=(n == parts - 1 and b == part - 1))
                last.then_inc(s_mm, 1)

        @block.vector
        def _(v):
            ch = Chain(v, s_v)
            ch.after(nc.vector.tensor_copy(pos_i[:], pos[:]))
            ch.after(nc.vector.tensor_scalar(piece_i[:, 0], pos_i[:], P - 1, None, ALU.bitwise_and))
            ch.after(nc.vector.tensor_scalar(piece_i[:, 1], pos_i[:], 7, None, ALU.arith_shift_right))
            ch.after(nc.vector.tensor_copy(piece[:], piece_i[:]))
            v.wait_ge(s_i, 1)
            for n in range(parts):
                k, b0 = n * part // BLOCKS, n * part % BLOCKS
                each = lambda a, width: a.unsqueeze(2).to_broadcast([P, part, width])
                row = lambda a, width: a.unsqueeze(1).to_broadcast([P, part, width])
                if n >= 2:
                    v.wait_ge(s_mm, n - 1)
                nc.vector.tensor_tensor(lanes[:, n % 2], each(piece[:, 0, k, b0:b0 + part], P), row(g.lane[:], P),
                                        ALU.is_equal).then_inc(s_ready, 1)
                ch.after(nc.vector.tensor_tensor(marks[:, n % 2], each(piece[:, 1, k, b0:b0 + part], tiles),
                                                 row(tile_no[:], tiles), ALU.is_equal))
                nc.vector.tensor_tensor(marks[:, n % 2], marks[:, n % 2], each(value[:, b0:b0 + part], tiles),
                                        ALU.mult).then_inc(s_ready, 1)
            v.wait_ge(s_mm, parts)
            ch.after(nc.vector.tensor_copy(out[:], ps[:, 0:tiles]))


def experts(nc, g):
    with Phase(nc, "moe") as m:
        w13, w2 = g.w13, g.w2_sb
        x = m.sb("x", [P, 2, D])
        idx = m.sb("idx", [P, 2], I32)
        xt = m.sb("xt", [P, 2, KC, P])
        act_ = m.sb("act", [P, EH])
        gl = m.sb("gl", [P, 2, EH])
        gt = m.sb("gt", [P, EC, P])
        y = m.sb("y", [P, 2, D])
        ps_x = m.ps("ps_x", [P, KC, P])
        ps_h = [m.ps(f"ps_h{i}", [P, 512]) for i in range(4)]
        ps_g = [m.ps(f"ps_g{i}", [P, 4, P]) for i in range(2)]
        ps_y = m.ps("ps_y", [P, D])
        s_xt, s_xtc, s_up, s_silu, s_mul, s_gt, s_gtc, s_y, s_yc = (
            m.sem(k) for k in ("xt", "xtc", "up", "silu", "mul", "gt", "gtc", "y", "yc"))
        s_idx = m.sem("idx")
        s_x = m.sems_of_pool("x", 2)
        s_st = [m.sem(f"st{i}") for i in range(2)]
        block = m.block()
        T = MAX_TILES
        tile_rows = lambda dram, n: dram[bass.ds(n * P, P), :]
        rest = EH - (EC - 1) * P

        @block.sync
        def _(sp):
            def turn(n, slot, more):
                if late(n, 1):
                    sp.wait_ge(s_yc, n)
                    sp.dma_start(tile_rows(g.slot_y, n - 1), y[:, 1 - slot]).then_inc(s_st[1 - slot], 16)
            rounds(sp, turn, T)
            sp.wait_ge(s_yc, T)
            sp.dma_start(tile_rows(g.slot_y, T - 1), y[:, 0]).then_inc(s_st[0], 16)
            sp.wait_ge(s_st[0], 16 * (T // 2 + 1))
            sp.wait_ge(s_st[1], 16 * (T // 2))

        @block.gpsimd
        def _(pool):
            def turn(n, slot, more):
                if late(n, 2):
                    pool.wait_ge(s_xt, n - 1)
                pool.wait_ge(s_idx, n + 1)
                pool.nop(nofuse=True)
                nc.gpsimd.indirect_dma_start(x[:, slot], None, g.x3n,
                                             bass.IndirectOffsetOnAxis(idx[:, slot:slot + 1], 0)).then_inc(s_x[slot], 16)
            rounds(pool, turn, T)

        @block.tensor
        def _(pe):
            def expert_of(n):
                return nc.values_load_multi_w_load_instructions(
                    g.tile_expert[0:1, bass.ds(n, 1)], [mybir.EngineType.PE], min_val=0, max_val=EXPERTS - 1,
                    skip_runtime_bounds_check_because="made on the chip, at most EXPERTS - 1")[1][0]

            def transposes(n, slot):
                pe.wait_ge(s_x[slot], (n + (2 - slot)) * 8)
                if late(n, 1):
                    pe.wait_ge(s_xtc, n)
                for k in range(KC):
                    last = nc.tensor.transpose(ps_x[:, k, :], x[:, slot, k * P:(k + 1) * P], g.ident[:])
                last.then_inc(s_xt, 1)

            def down(n, slot):
                e = expert_of(n)
                if late(n, 1):
                    pe.wait_ge(s_yc, n)
                for c in range(EC):
                    if c % 4 == 0:
                        pe.wait_ge(s_gtc, n * 2 + c // 4 + 1)
                    size = P if c < EC - 1 else rest
                    last = nc.tensor.matmul(ps_y[:], gt[0:size, c, :], w2[0:size, :, c, :][:, bass.ds(e, 1), :].rearrange("p a d -> p (a d)"),
                                            start=(c == 0), stop=(c == EC - 1))
                last.then_inc(s_y, 1)

            transposes(0, 0)
            pe.wait_ge(g.s_experts, 16 * 4 * EXPERTS)

            def turn(n, slot, more):
                e = expert_of(n)
                pe.wait_ge(s_xtc, n + 1)
                for i in range(2):
                    for hf in range(2):
                        if late(n, 1):
                            pe.wait_ge(s_mul, n * 2 - 1 + hf)
                        for k in range(KC):
                            last = nc.tensor.matmul(ps_h[2 * i + hf][:, 0:EHALF], xt[:, slot, k, :],
                                                    w13[:, :, k, i, hf * EHALF:(hf + 1) * EHALF][:, bass.ds(e, 1), :].rearrange("p a h -> p (a h)"),
                                                    start=(k == 0), stop=(k == KC - 1))
                        last.then_inc(s_up, 1)
                if more:
                    transposes(n + 1, 1 - slot)
                if late(n, 1):
                    down(n - 1, 1 - slot)
                pe.wait_ge(s_mul, n * 2 + 2)
                for c in range(EC):
                    size = P if c < EC - 1 else rest
                    last = nc.tensor.transpose(ps_g[c // 4][0:size, c % 4, :], gl[:, slot, c * P:c * P + size], g.ident[:])
                    if c in (3, EC - 1):
                        last.then_inc(s_gt, 1)
            rounds(pe, turn, T)
            down(T - 1, 0)

        @block.scalar
        def _(act):
            def index(n, slot):
                if late(n, 2):
                    act.wait_ge(s_x[slot], (n - slot) * 8)
                nc.scalar.activation(idx[:, slot:slot + 1], g.tile_tokens[:, bass.ds(n, 1)], ACT.Copy).then_inc(s_idx, 1)
            index(0, 0)
            index(1, 1)

            def evac_xt(n, slot):
                act.wait_ge(s_xt, n + 1)
                nc.scalar.activation(xt[:, slot], ps_x[:], ACT.Copy).then_inc(s_xtc, 1)
            evac_xt(0, 0)

            def turn(n, slot, more):
                if more == 2:
                    index(n + 2, slot)
                for hf in range(2):
                    act.wait_ge(s_up, n * 4 + hf + 1)
                    if late(n, 1):
                        act.wait_ge(s_mul, n * 2 - 1 + hf)
                    nc.scalar.activation(act_[:, hf * EHALF:(hf + 1) * EHALF], ps_h[hf][:, 0:EHALF], ACT.Silu).then_inc(s_silu, 1)
                if more:
                    evac_xt(n + 1, 1 - slot)
                if late(n, 1):
                    act.wait_ge(s_y, n)
                    if late(n, 3):
                        act.wait_ge(s_st[1 - slot], (n - 1 - (1 - slot)) * 8)
                    nc.scalar.activation(y[:, 1 - slot], ps_y[:], ACT.Copy).then_inc(s_yc, 1)
                for i in range(2):
                    act.wait_ge(s_gt, n * 2 + i + 1)
                    if i == 0:
                        nc.scalar.activation(gt[:, 0:4, :], ps_g[0][:], ACT.Copy).then_inc(s_gtc, 1)
                    else:
                        nc.scalar.activation(gt[:, 4:5, :], ps_g[1][:, 0:1, :], ACT.Copy)
                        nc.scalar.activation(gt[0:rest, 5:6, :], ps_g[1][0:rest, 1:2, :], ACT.Copy).then_inc(s_gtc, 1)
            rounds(act, turn, T)
            act.wait_ge(s_y, T)
            act.wait_ge(s_st[0], 16 * (T // 2))
            nc.scalar.activation(y[:, 0], ps_y[:], ACT.Copy).then_inc(s_yc, 1)

        @block.vector
        def _(v):
            def turn(n, slot, more):
                for hf in range(2):
                    v.wait_ge(s_silu, n * 2 + hf + 1)
                    v.wait_ge(s_up, n * 4 + hf + 3)
                    if late(n, 2):
                        v.wait_ge(s_gt, n * 2 - 2)
                    nc.vector.tensor_tensor(gl[:, slot, hf * EHALF:(hf + 1) * EHALF], ps_h[2 + hf][:, 0:EHALF],
                                            act_[:, hf * EHALF:(hf + 1) * EHALF], ALU.mult).then_inc(s_mul, 1)
            rounds(v, turn, T)


def combine(nc, g, out):
    with Phase(nc, "comb") as m:
        x = m.sb("x", [P, 2, 2, D])
        y = m.sb("y", [P, 2, 2, 2, D])
        o = m.sb("o", [P, 2, 2, D])
        t = m.sb("t", [P, 2, 2, D])
        idx = m.sb("idx", [P, 2, 2, 2], I32)
        s_idx, s_t, s_o = (m.sem(k) for k in ("idx", "t", "o"))
        s_x, s_st = ([m.sem(f"{k}{i}") for i in range(2)] for k in ("x", "st"))
        s_y = m.sems_of_pool("y", 2)
        block = m.block()

        @block.sync
        def _(sp):
            def turn(n, slot, more):
                if late(n, 2):
                    sp.wait_ge(s_o, n * 2 - 2)
                sp.dma_start(x[:, slot], pair_rows(g.x3, n)).then_inc(s_x[slot], 16)
                if late(n, 1):
                    sp.wait_ge(s_o, n * 2)
                    sp.dma_start(pair_rows(out, n - 1), o[:, 1 - slot]).then_inc(s_st[1 - slot], 16)
            rounds(sp, turn)
            sp.wait_ge(s_o, PAIRS * 2)
            sp.dma_start(pair_rows(out, PAIRS - 1), o[:, 0]).then_inc(s_st[0], 16)
            sp.wait_ge(s_st[0], 16 * (PAIRS // 2 + 1))
            sp.wait_ge(s_st[1], 16 * (PAIRS // 2))

        @block.scalar
        def _(act):
            def turn(n, slot, more):
                if late(n, 2):
                    act.wait_ge(s_o, n * 2 - 2)
                nc.scalar.activation(idx[:, slot], g.from_slot[:, bass.ds(n * 2, 2), :], ACT.Copy).then_inc(s_idx, 1)
            rounds(act, turn)

        @block.gpsimd
        def _(pool):
            def turn(n, slot, more):
                pool.wait_ge(s_idx, n + 1)
                pool.nop(nofuse=True)
                for b in range(2):
                    for i in range(2):
                        nc.gpsimd.indirect_dma_start(y[:, slot, b, i, :], None, g.slot_y,
                                                     bass.IndirectOffsetOnAxis(idx[:, slot, b, i:i + 1], 0)).then_inc(s_y[slot], 16)
            rounds(pool, turn)

        @block.vector
        def _(v):
            def turn(n, slot, more):
                v.wait_ge(s_x[slot], (n + (2 - slot)) * 8)
                v.wait_ge(s_y[slot], (n + (2 - slot)) * 32)
                for b in range(2):
                    if late(n, 2):
                        v.wait_ge(s_o, n * 2 - 2)
                    nc.vector.scalar_tensor_tensor(t[:, slot, b], y[:, slot, b, 0, :], g.gate[:, 0, bass.ds(n * 2 + b, 1)],
                                                   x[:, slot, b, :], ALU.mult, ALU.add).then_inc(s_t, 1)
                for b in range(2):
                    v.wait_ge(s_t, n * 2 + b + 1)
                    if late(n, 2):
                        v.wait_ge(s_st[slot], (n - slot) * 8)
                    nc.vector.scalar_tensor_tensor(o[:, slot, b], y[:, slot, b, 1, :], g.gate[:, 1, bass.ds(n * 2 + b, 1)],
                                                   t[:, slot, b], ALU.mult, ALU.add).then_inc(s_o, 1)
            rounds(v, turn)


class Plan:

    def __init__(self, ins):
        self.names = {}
        (self.x, self.src_rows, self.dst_rows, self.bias_rows,
         self.Wq, self.Wk, self.Wv, self.Wp, self.bp, self.ln1_g, self.ln1_b, self.ln2_g, self.ln2_b,
         self.W1, self.b1, self.W2, self.b2, self.wr, self.br, self.w1, self.fb1, self.w2, self.fb2,
         self.W, self.a_src, self.a_dst, self.gamma, self.beta,
         self.router_t, self.w1_t, self.w3_t, self.w2_t) = (ins[k] for k in INPUTS)

    def next_name(self, name):
        self.names[name] = self.names.get(name, 0) + 1
        return f"{name}{self.names[name]}"


def set_constants(nc, g):
    with Phase(nc, "const") as m:
        s_c, s_half = m.sem("c"), m.sem("half")
        block = m.block()

        @block.vector
        def _(v):
            nc.vector.memset(g.minus_half[:], -0.5).then_inc(s_half, 1)
            v.wait_ge(s_half, 1)

        @block.gpsimd
        def _(pool):
            nc.gpsimd.memset(g.ident[:], 0.0).then_inc(s_c, 1)
            pool.wait_ge(s_c, 1)
            nc.gpsimd.affine_select(out=g.ident[:], in_=g.ident[:], compare_op=ALU.not_equal, fill=1.0,
                                    base=0, pattern=[[-1, P]], channel_multiplier=1).then_inc(s_c, 1)
            nc.gpsimd.iota(g.lane[:], [[1, P]], 0, 0, allow_small_or_imprecise_dtypes=True).then_inc(s_c, 1)
            nc.gpsimd.iota(g.node[:], [[P, BLOCKS]], 0, 1, allow_small_or_imprecise_dtypes=True).then_inc(s_c, 1)
            pool.wait_ge(s_c, 4)


INPUTS = {
    "x": (NPAD, D), "src_rows": (TILE_ROWS, P), "dst_rows": (TILE_ROWS, P), "bias_rows": (TILE_ROWS, P),
    "Wq": (D, D), "Wk": (D, D), "Wv": (D, D), "Wp": (D, D), "bp": (D,), "ln1_g": (D,), "ln1_b": (D,),
    "ln2_g": (D,), "ln2_b": (D,), "W1": (D, FF), "b1": (FF,), "W2": (FF, D), "b2": (D,),
    "wr": (D,), "br": (1,), "w1": (D, FF), "fb1": (FF,), "w2": (FF, D), "fb2": (D,),
    "W": (D, D), "a_src": (H, HD), "a_dst": (H, HD), "gamma": (D,), "beta": (D,),
    "router_t": (D, EXPERTS), "w1_t": (EXPERTS, D, EH), "w3_t": (EXPERTS, D, EH), "w2_t": (EXPERTS, EH, D),
}


def program(nc, ins, out):
    g = Plan(ins)

    def dram(name, shape):
        return nc.dram_tensor(name, shape, F32).ap()

    g.norm, g.k_rows, g.v_rows, g.hidden, g.resid, g.x1n, g.x2, g.x3, g.x3n = (
        dram(n, (NPAD, D)) for n in ("norm", "k_rows", "v_rows", "hidden", "resid", "x1n", "x2", "x3", "x3n"))
    g.s_src = dram("s_src", (NPAD, H))
    g.kept_y = dram("kept_y", (KEPT_BLOCKS * P, D))
    g.slot_y = dram("slot_y", (SLOTS, D))

    with Phase(nc, "all") as top:
        g.ident, g.lane = top.sb("ident", [P, P]), top.sb("lane", [P, P])
        g.minus_half = top.sb("minus_half", [P, 2])
        g.node = top.sb("node", [P, BLOCKS])
        g.logits = top.sb("logits", [P, BLOCKS, EXPERTS])
        g.weight, g.keep = top.sb("weight", [P, BLOCKS]), top.sb("keep", [P, BLOCKS])
        g.factor = top.sb("factor", [P, BLOCKS])
        g.kept_pos, g.kept_node = top.sb("kept_pos", [P, 1, BLOCKS]), top.sb("kept_node", [P, BLOCKS])
        g.from_kept, g.kept_tokens = top.sb("from_kept", [P, BLOCKS], I32), top.sb("kept_tokens", [P, KEPT_BLOCKS], I32)
        g.step_dst, g.step_src = top.sb("step_dst", [P, STEPS]), top.sb("step_src", [P, STEPS], I32)
        g.step_block = top.sb("step_block", [1, STEPS], I32)
        g.run_bias, g.run_off, g.run_new = (top.sb("run_bias", [P, STEPS]), top.sb("run_off", [P, STEPS]),
                                            top.sb("run_new", [P, STEPS + 1]))
        set_constants(nc, g)
        step_tables(nc, g)

        with Phase(nc, "graph1") as m:
            scores = m.sb("scores", [P, STEPS, H])
            with Phase(nc, "q") as mq:
                q = mq.sb("q", [P, BLOCKS, D])
                project_qkv(nc, g, q)
                edge_scores(nc, g, scores, g.k_rows, D, q)
            with Phase(nc, "values1") as mv:
                src = Rows(nc, g, mv, g.v_rows, D)
                edge_softmax(nc, g, scores, g.run_bias, float(HD) ** -0.5, src)
                acc = mv.sb("acc", [P, BLOCKS, AGG])
                aggregate(nc, g, acc, scores, src)
                attention_out(nc, g, acc)
        ffn(nc, g, "ffn1", g.hidden, g.W1, g.b1, g.W2, ACT.Gelu, [g.hidden, g.x], [g.b2, g.ln2_g, g.ln2_b, g.wr],
            [g.resid, g.x1n], after_graph, 8 + 2 * LN_STEPS, 2)
        keep_top(nc, g)
        invert(nc, g, g.kept_pos, g.kept_node, KEPT_BLOCKS, g.kept_tokens)
        ffn(nc, g, "ffn2", g.x1n, g.w1, g.fb1, g.w2, ACT.Gelu_apprx_tanh, [], [g.fb2],
            [g.kept_y], biased, 1, tokens=g.kept_tokens)

        with Phase(nc, "graph2") as m:
            scores = m.sb("scores", [P, STEPS, H])
            s_dst = m.sb("s_dst", [P, BLOCKS, H])
            project_heads(nc, g, s_dst)
            edge_scores(nc, g, scores, g.s_src, H, s_dst)
            with Phase(nc, "values2") as mv:
                src = Rows(nc, g, mv, g.v_rows, D)
                edge_softmax(nc, g, scores, g.run_off, 1.0, src)
                acc = mv.sb("acc", [P, BLOCKS, AGG])
                aggregate(nc, g, acc, scores, src)
                graph2_out(nc, g, acc, g.logits)
        with Phase(nc, "experts") as m:
            g.gate = m.sb("gate", [P, 2, BLOCKS])
            g.pos, g.real_node = m.sb("pos", [P, 2, BLOCKS]), m.sb("real_node", [P, BLOCKS])
            g.from_slot = m.sb("from_slot", [P, BLOCKS, 2], I32)
            g.tile_tokens = m.sb("tile_tokens", [P, MAX_TILES], I32)
            g.tile_expert = m.sb("tile_expert", [1, MAX_TILES], I32)
            g.exp_out = m.sb("exp_out", [P, BLOCKS, EXPERTS])
            g.w13, g.w2_sb = m.sb("w13", [P, EXPERTS, KC, 2, EH]), m.sb("w2", [P, EXPERTS, EC, D])
            g.s_exp, g.s_experts = m.sem("exp"), m.sem("experts")
            route(nc, g, g.logits)
            invert(nc, g, g.pos, g.real_node, MAX_TILES, g.tile_tokens)
            experts(nc, g)
            combine(nc, g, out)


def kernel(**inputs):
    import numpy as np
    import concourse.bacc as bacc
    from concourse.bass_utils import run_bass_kernel_spmd

    def rows(a, pad):
        flat = np.full((EPAD,), pad, a.dtype)
        flat[:E] = a.reshape(-1)
        return flat.reshape(TILE_ROWS, P)

    i = {k: np.asarray(v) for k, v in inputs.items()}
    x = np.zeros((NPAD, D), np.float32)
    x[:N] = i["x"]
    arrays = {"x": x, "src_rows": rows(i["src"], 0), "dst_rows": rows(i["dst"], DST_PAD),
              "bias_rows": rows(i["edge_weight1"], 0)}
    for k in ("Wq", "Wk", "Wv", "Wp", "bp", "ln1_g", "ln1_b", "ln2_g", "ln2_b", "W1", "b1", "W2", "b2"):
        arrays[k] = i["L0_gnn_" + k]
    arrays |= {"wr": i["L0_ffn_wr"].reshape(-1), "br": i["L0_ffn_br"], "w1": i["L0_ffn_w1"], "fb1": i["L0_ffn_b1"],
               "w2": i["L0_ffn_w2"], "fb2": i["L0_ffn_b2"]}
    for k in ("W", "a_src", "a_dst", "gamma", "beta"):
        arrays[k] = i["L1_gnn_" + k]
    arrays |= {"router_t": i["L1_ffn_router_w"].T, "w1_t": i["L1_ffn_w1"].transpose(0, 2, 1),
               "w3_t": i["L1_ffn_w3"].transpose(0, 2, 1), "w2_t": i["L1_ffn_w2"].transpose(0, 2, 1)}

    nc = bacc.Bacc("TRN2", target_bir_lowering=False, num_devices=1)
    ins, fed = {}, {}
    for k, shape in INPUTS.items():
        a = np.ascontiguousarray(arrays[k])
        assert a.shape == shape
        fed[f"in_{k}"] = a
        ins[k] = nc.dram_tensor(f"in_{k}", shape, mybir.dt.from_np(a.dtype), kind="ExternalInput").ap()
    out = nc.dram_tensor("out", (NPAD, D), F32, kind="ExternalOutput").ap()
    program(nc, ins, out)
    r = run_bass_kernel_spmd(nc, [fed], core_ids=[0])
    return r.results[0]["out"][:N]
```

```python
from contextlib import ExitStack

import concourse.bass as bass
from concourse import mybir

F32 = mybir.dt.float32
I32 = mybir.dt.int32
BF16 = mybir.dt.bfloat16
ALU = mybir.AluOpType
ACT = mybir.ActivationFunctionType
AX = mybir.AxisListType

P = 128
N = 6250
D = 256
H = 8
HD = D // H
FF = 4 * D
E = 106250
KC = D // P
BLOCKS = 50
NPAD = BLOCKS * P
LAST_BLOCK = (N - 1) // P
PAIRS = BLOCKS // 2
EDGE_TILES = -(-E // P)
TILE_ROWS = EDGE_TILES + 1
EPAD = TILE_ROWS * P
WINDOWS = 7
STEPS = P * WINDOWS
TGROUPS = WINDOWS
DST_PAD = 1 << 20
BIG = 1.0e30
NEG = -1.0e38
U = 8
HALVES = -(-(EDGE_TILES + LAST_BLOCK) // U)
RING = 4
AGG = D + H
LN_EPS = 1e-5
KEEP = 3124
KEPT_BLOCKS = 2 * -(-KEEP // (2 * P))
EXPERTS = 8
EH = 682
MAX_TILES = (2 * N) // P + EXPERTS
EC = -(-EH // P)
EHALF = EH // 2
assert NPAD - N >= P and STEPS >= HALVES * U >= EDGE_TILES + LAST_BLOCK and HALVES % 2 == 0 and KEEP == int(0.5 * N) - 1


class Phase:

    def __init__(self, nc, name):
        self.nc, self.name, self.ctx, self.sems = nc, name, ExitStack(), []

    def __enter__(self):
        return self

    def __exit__(self, *e):
        self.ctx.close()
        if self.sems:
            for first in (s for s in self.sems if s - 1 not in self.sems):
                self.nc.gpsimd.sem_clear(range(first, next(i for i in range(first, 257) if i not in self.sems)))
            self.nc.all_engine_barrier()

    def sb(self, name, shape, dt=F32):
        return self.ctx.enter_context(self.nc.sbuf_tensor(f"{self.name}_{name}", shape, dt))

    def ps(self, name, shape, dt=F32):
        return self.ctx.enter_context(self.nc.psum_tensor(f"{self.name}_{name}", shape, dt))

    def sem(self, name):
        sem = self.ctx.enter_context(self.nc.semaphore(f"{self.name}_{name}"))
        self.sems.append(sem.num)
        return sem

    def sems_of_pool(self, name, count):
        return [self.nc.alloc_semaphore(f"{self.name}_{name}{i}") for i in range(count)]

    def block(self):
        return self.ctx.enter_context(self.nc.Block())


class Chain:

    def __init__(self, eng, sem):
        self.eng, self.sem, self.n = eng, sem, 0

    def after(self, ins):
        self.n += 1
        ins.then_inc(self.sem, 1)
        self.eng.wait_ge(self.sem, self.n)
        return ins


def step_tables(nc, g):
    with Phase(nc, "tab") as m:
        last_dst = m.sb("last_dst", [P, TGROUPS], I32)
        last_blk = m.sb("last_blk", [P, TGROUPS], I32)
        ends = m.sb("ends", [P, TGROUPS])
        tile_no = m.sb("tile_no", [P, TGROUPS])
        beyond = m.sb("beyond", [P, TGROUPS])
        step_row = m.sb("step_row", [P, STEPS])
        step_pw = m.sb("step_pw", [P, WINDOWS])
        cmp = m.sb("cmp", [P, TGROUPS, STEPS])
        ones = m.sb("ones", [P, 1])
        tile_f = m.sb("tile_f", [P, WINDOWS])
        tile_idx = m.sb("tile_idx", [P, WINDOWS], I32)
        blk = m.sb("blk", [P, WINDOWS])
        e_row = m.sb("e_row", [1, STEPS])
        b_row = m.sb("b_row", [1, STEPS])
        dst_i = m.sb("dst_i", [P, WINDOWS, P], I32)
        src_i = m.sb("src_i", [P, WINDOWS, P], I32)
        dst_x = m.sb("dst_x", [P, STEPS + 2])
        src_f = m.sb("src_f", [P, WINDOWS, P])
        rel = m.sb("rel", [P, WINDOWS, P])
        over = m.sb("over", [P, WINDOWS, P])
        src_part = m.sb("src_part", [P, 2, STEPS], I32)
        rows_b = m.sb("rows_b", [P, 3, STEPS], BF16)
        ps_e = m.ps("ps_e", [P, 512])
        ps_r = [m.ps(f"ps_r{i}", [P, 512]) for i in range(2)]
        ps_t = [m.ps(f"ps_t{i}", [P, 512]) for i in range(3)]
        s_in, s_iota, s_set, s_cmp, s_pe, s_idx = (m.sem(x) for x in ("in", "iota", "set", "cmp", "pe", "idx"))
        s_v, s_cols, s_copied, s_side, s_part, s_rows, s_stored = (
            m.sem(x) for x in ("v", "cols", "copied", "side", "part", "rows", "stored"))
        s_dst, s_src, s_bias = m.sems_of_pool("gathered", 3)
        block = m.block()
        dst_runs = dst_x[:, 1:STEPS + 1]

        @block.sync
        def _(sp):
            full = (TGROUPS - 1) * P
            sp.wait_ge(s_set, 1)
            with nc.allow_non_contiguous_dma(reason="one word of each edge tile"):
                sp.dma_start(last_dst[:, 0:TGROUPS - 1],
                             g.dst_rows[0:full, P - 1:P].rearrange("(k p) o -> p (k o)", p=P)).then_inc(s_in, 16)
                sp.dma_start(last_dst[0:TILE_ROWS - full, TGROUPS - 1:TGROUPS],
                             g.dst_rows[full:TILE_ROWS, P - 1:P]).then_inc(s_in, 16)
                sp.wait_ge(s_cols, 1)
                sp.dma_start(dst_x[1:P, 0:1], dst_x[0:P - 1, STEPS:STEPS + 1]).then_inc(s_side, 16)
                sp.dma_start(dst_x[0:P - 1, STEPS + 1:STEPS + 2], dst_x[1:P, 1:2]).then_inc(s_side, 16)
            sp.wait_ge(s_side, 32)
            for i, r in enumerate((g.dst_lane_rows, g.src_lane_rows, g.src_block_rows)):
                sp.wait_ge(s_rows, i + 1)
                sp.dma_start(r.rearrange("(p w) e -> p (w e)", w=WINDOWS), rows_b[:, i]).then_inc(s_stored, 16)
            sp.wait_ge(s_stored, 48)

        @block.gpsimd
        def _(pool):
            nc.gpsimd.iota(step_row[:], [[1, STEPS]], 0, 0, allow_small_or_imprecise_dtypes=True).then_inc(s_iota, 1)
            nc.gpsimd.iota(tile_no[:], [[P, TGROUPS]], 0, 1, allow_small_or_imprecise_dtypes=True).then_inc(s_iota, 1)
            nc.gpsimd.iota(step_pw[:], [[1, WINDOWS]], 0, WINDOWS, allow_small_or_imprecise_dtypes=True).then_inc(s_iota, 1)
            pool.wait_ge(s_idx, 1)
            for w in range(WINDOWS):
                idx = bass.IndirectOffsetOnAxis(tile_idx[:, w:w + 1], 0)
                nc.gpsimd.indirect_dma_start(dst_i[:, w, :], None, g.dst_rows, idx).then_inc(s_dst, 16)
                nc.gpsimd.indirect_dma_start(src_i[:, w, :], None, g.src_rows, idx).then_inc(s_src, 16)
                nc.gpsimd.indirect_dma_start(g.run_bias[:, w * P:(w + 1) * P], None, g.bias_rows, idx).then_inc(s_bias, 16)
            pool.wait_ge(s_dst, 16 * WINDOWS)
            pool.wait_ge(s_src, 16 * WINDOWS)
            pool.wait_ge(s_bias, 16 * WINDOWS)

        @block.tensor
        def _(pe):
            by_w = cmp[:].rearrange("q k (p w) -> q k w p", w=WINDOWS)
            pe.wait_ge(s_cmp, TGROUPS)
            for w in range(WINDOWS):
                for k in range(TGROUPS):
                    last = nc.tensor.matmul(ps_e[:, w:w + 1], by_w[:, k, w, :], ones[:],
                                            start=(k == 0), stop=(k == TGROUPS - 1))
            last.then_inc(s_pe, 1)
            for i, (a, b) in enumerate(((0, 512), (512, STEPS))):
                for k in range(TGROUPS):
                    last = nc.tensor.matmul(ps_r[i][0:1, 0:b - a], ones[:], cmp[:, k, a:b],
                                            start=(k == 0), stop=(k == TGROUPS - 1))
            last.then_inc(s_pe, 1)
            pe.wait_ge(s_cols, 2)
            n = 0
            for rows in (rel, src_f):
                for w in range(WINDOWS):
                    if n >= 3:
                        pe.wait_ge(s_copied, n - 2)
                    nc.tensor.transpose(ps_t[n % 3][:, 0:P], rows[:, w, :], g.ident[:]).then_inc(s_pe, 1)
                    n += 1

        @block.vector
        def _(v):
            ch = Chain(v, s_v)
            nc.vector.memset(last_dst[:], DST_PAD).then_inc(s_set, 1)
            ch.after(nc.vector.memset(ones[:], 1.0))
            ch.after(nc.vector.memset(dst_x[:], -1.0))
            v.wait_ge(s_in, 32)
            ch.after(nc.vector.tensor_scalar(last_blk[:], last_dst[:], 7, None, ALU.arith_shift_right))
            ch.after(nc.vector.tensor_scalar(ends[:], last_blk[:], float(LAST_BLOCK), None, ALU.min))
            v.wait_ge(s_iota, 3)
            ch.after(nc.vector.tensor_tensor(ends[:], ends[:], tile_no[:], ALU.add))
            ch.after(nc.vector.tensor_scalar(beyond[:], tile_no[:], float(EDGE_TILES), BIG, ALU.is_ge, ALU.mult))
            ch.after(nc.vector.tensor_tensor(ends[:], ends[:], beyond[:], ALU.add))
            for k in range(TGROUPS):
                nc.vector.tensor_scalar(cmp[:, k, :], step_row[:], ends[:, k:k + 1], None, ALU.is_gt).then_inc(s_cmp, 1)
            v.wait_ge(s_pe, 1)
            nc.vector.tensor_copy(tile_idx[:], ps_e[:, 0:WINDOWS]).then_inc(s_idx, 1)
            ch.after(nc.vector.tensor_copy(tile_f[:], ps_e[:, 0:WINDOWS]))
            ch.after(nc.vector.tensor_tensor(blk[:], step_pw[:], tile_f[:], ALU.subtract))
            ch.after(nc.vector.tensor_scalar(blk[:], blk[:], float(LAST_BLOCK), float(-P), ALU.min, ALU.mult))
            v.wait_ge(s_pe, 2)
            nc.vector.tensor_copy(e_row[0:1, 0:512], ps_r[0][0:1, 0:512]).then_inc(s_v, 1)
            ch.n += 1
            ch.after(nc.vector.tensor_copy(e_row[0:1, 512:STEPS], ps_r[1][0:1, 0:STEPS - 512]))
            ch.after(nc.vector.tensor_tensor(b_row[:], step_row[0:1, :], e_row[:], ALU.subtract))
            ch.after(nc.vector.tensor_scalar(b_row[:], b_row[:], float(LAST_BLOCK), None, ALU.min))
            ch.after(nc.vector.tensor_copy(g.step_block[:], b_row[:]))
            v.wait_ge(s_dst, 16 * WINDOWS)
            nc.vector.tensor_copy(dst_runs, dst_i[:].rearrange("p w j -> p (w j)")).then_inc(s_cols, 1)
            v.wait_ge(s_src, 16 * WINDOWS)
            nc.vector.tensor_copy(src_f[:], src_i[:]).then_inc(s_v, 1)
            ch.n += 1
            v.wait_ge(s_cols, 1)
            ch.after(nc.vector.tensor_tensor(rel[:], dst_runs.rearrange("p (w j) -> p w j", w=WINDOWS),
                                             blk[:].unsqueeze(2).to_broadcast([P, WINDOWS, P]), ALU.add))
            v.sem_inc(s_cols, 1)
            src_row = src_i[:].rearrange("p w j -> p (w j)")
            nc.vector.tensor_copy(rows_b[:, 0], rel[:].rearrange("p w j -> p (w j)")).then_inc(s_rows, 1)
            nc.vector.tensor_scalar(src_part[:, 0], src_row, P - 1, None, ALU.bitwise_and).then_inc(s_part, 1)
            nc.vector.tensor_scalar(src_part[:, 1], src_row, 7, None, ALU.arith_shift_right).then_inc(s_part, 1)
            for i in range(2):
                v.wait_ge(s_part, i + 1)
                nc.vector.tensor_copy(rows_b[:, 1 + i], src_part[:, i]).then_inc(s_rows, 1)
            ch.after(nc.vector.tensor_scalar(over[:], rel[:], float(P), NEG, ALU.is_ge, ALU.mult))
            ch.after(nc.vector.tensor_scalar(g.run_off[:].rearrange("p (w j) -> p w j", w=WINDOWS), rel[:],
                                             0.0, NEG, ALU.is_lt, ALU.mult))
            ch.after(nc.vector.tensor_tensor(g.run_off[:].rearrange("p (w j) -> p w j", w=WINDOWS),
                                             g.run_off[:].rearrange("p (w j) -> p w j", w=WINDOWS), over[:], ALU.add))
            v.wait_ge(s_bias, 16 * WINDOWS)
            ch.after(nc.vector.tensor_tensor(g.run_bias[:], g.run_bias[:], g.run_off[:], ALU.add))
            v.wait_ge(s_side, 32)
            ch.after(nc.vector.tensor_tensor(g.run_new[:], dst_x[:, 1:STEPS + 2], dst_x[:, 0:STEPS + 1], ALU.not_equal))
            ch.after(nc.vector.tensor_scalar(g.run_new[:], g.run_new[:], NEG, None, ALU.mult))
            by_w = [g.step_dst[:].rearrange("q (p w) -> q w p", w=WINDOWS),
                    g.step_src[:].rearrange("q (p w) -> q w p", w=WINDOWS)]
            n = 0
            for dest in by_w:
                for w in range(WINDOWS):
                    v.wait_ge(s_pe, 3 + n)
                    nc.vector.tensor_copy(dest[:, w, :], ps_t[n % 3][:, 0:P]).then_inc(s_copied, 1)
                    n += 1
            v.wait_ge(s_copied, n)


class Rows:

    def __init__(self, nc, g, m, rows, width, steps=U):
        self.nc, self.g, self.rows, self.steps = nc, g, rows, steps
        self.ring = m.sb("ring", [P, RING, steps, width])
        self.idx = m.sb("idx", [P, RING, steps], I32)
        self.s_idx = m.sem("idx")
        self.landed = m.sems_of_pool("row", RING)

    def index(self, n, slot):
        self.nc.scalar.activation(self.idx[:, slot, :], self.g.step_src[:, bass.ds(n * U, self.steps)],
                                  ACT.Copy).then_inc(self.s_idx, 1)

    def gather(self, n, slot, more=True):
        self.nc.gpsimd.wait_ge(self.s_idx, n + 1)
        self.nc.gpsimd.nop(nofuse=True)
        for u in range(self.steps):
            self.nc.gpsimd.indirect_dma_start(self.ring[:, slot, u, :], None, self.rows,
                                              bass.IndirectOffsetOnAxis(self.idx[:, slot, u:u + 1], 0)
                                              ).then_inc(self.landed[slot], 16)

    def wait(self, eng, n, slot):
        eng.wait_ge(self.landed[slot], (n + (RING - slot)) * (16 * self.steps // RING))


SOFT_EXP_AT = 44


def edge_softmax(nc, g, scores, runs_bias, scale, src):
    with Phase(nc, g.next_name("soft")) as m:
        val = m.sb("val", [P, H, STEPS])
        fwd = m.sb("fwd", [P, H, STEPS])
        bwd = m.sb("bwd", [P, H, STEPS])
        keep = m.sb("keep", [P, 2, H])
        tails = m.sb("tails", [P, 2, H])
        neg = m.sb("neg", [H, 2, P + 1])
        keep_t = m.sb("keep_t", [H, 2, P])
        tails_t = m.sb("tails_t", [H, 2, P])
        carry = m.sb("carry", [P, 2, H])
        ps = [m.ps(f"ps{i}", [P, 4, P]) for i in range(4)]
        ps_k = m.ps("ps_k", [H, 4, P])
        ps_c = m.ps("ps_c", [P, 2, H])
        s_v, s_tr, s_evac, s_tail, s_tailt, s_carry, s_back, s_exp, s_p = (
            m.sem(x) for x in ("v", "tr", "evac", "tail", "tailt", "carry", "back", "exp", "p"))
        s_out = [m.sem(f"out{i}") for i in range(2)]
        block = m.block()
        by_w = scores[:].rearrange("q (p w) h -> q w h p", w=WINDOWS)
        groups = [(h, w) for h in range(H) for w in (0, 4)]

        @block.tensor
        def _(pe):
            for n, (h, w0) in enumerate(groups):
                if n >= 4:
                    pe.wait_ge(s_evac, n - 3)
                for w in range(w0, min(w0 + 4, WINDOWS)):
                    last = nc.tensor.transpose(ps[n % 4][:, w - w0, :], by_w[:, w, h, :], g.ident[:])
                last.then_inc(s_tr, 1)
            pe.wait_ge(s_tail, 1)
            for i, t in enumerate((keep[:, 0], keep[:, 1], tails[:, 0], tails[:, 1])):
                last = nc.tensor.transpose(ps_k[:, i, :], t, g.ident[:])
            last.then_inc(s_tailt, 1)
            pe.wait_ge(s_carry, 1)
            nc.tensor.transpose(ps_c[:, 0, :], neg[:, 0, 0:P], g.ident[0:H, 0:H])
            nc.tensor.transpose(ps_c[:, 1, :], neg[:, 1, 1:P + 1], g.ident[0:H, 0:H]).then_inc(s_back, 1)
            for n, (h, w0) in enumerate(groups):
                if w0 == 0:
                    pe.wait_ge(s_exp, h + 1)
                if n >= 4:
                    pe.wait_ge(s_out[n % 2], (n - 4) // 2 + 1)
                for w in range(w0, min(w0 + 4, WINDOWS)):
                    last = nc.tensor.transpose(ps[n % 4][:, w - w0, :], val[:, h, w * P:(w + 1) * P], g.ident[:])
                last.then_inc(s_p, 1)

        @block.gpsimd
        def _(pool):
            for n in range(RING):
                src.gather(n, n)

        @block.scalar
        def _(act):
            for n in range(RING):
                src.index(n, n)
            for h in range(H):
                act.wait_ge(s_v, SOFT_EXP_AT + h)
                nc.scalar.activation(val[:, h, :], val[:, h, :], ACT.Exp).then_inc(s_exp, 1)
            for n, (h, w0) in list(enumerate(groups))[1::2]:
                act.wait_ge(s_p, n + 1)
                w1 = min(w0 + 4, WINDOWS)
                nc.scalar.activation(by_w[:, w0:w1, h, :], ps[n % 4][:, 0:w1 - w0, :], ACT.Copy).then_inc(s_out[1], 1)
            act.wait_ge(s_out[1], len(groups) // 2)

        @block.vector
        def _(v):
            ch = Chain(v, s_v)
            ch.after(nc.vector.memset(neg[:], NEG))
            for n, (h, w0) in enumerate(groups):
                v.wait_ge(s_tr, n + 1)
                w1 = min(w0 + 4, WINDOWS)
                nc.vector.scalar_tensor_tensor(val[:, h, w0 * P:w1 * P], ps[n % 4][:, 0:w1 - w0, :].rearrange("p a b -> p (a b)"),
                                               scale, runs_bias[:, w0 * P:w1 * P], ALU.mult, ALU.add).then_inc(s_evac, 1)
            v.wait_ge(s_evac, len(groups))
            start, end = g.run_new[:, 0:STEPS], g.run_new[:, 1:STEPS + 1]

            def forward(first):
                for h in range(H):
                    nc.vector.tensor_tensor_scan(fwd[:, h, :], start, val[:, h, :], first(h), ALU.add, ALU.max).then_inc(s_v, 1)
                ch.n += H
                v.wait_ge(s_v, ch.n)

            def backward(rows, first):
                for h in range(H):
                    nc.vector.tensor_tensor_scan(bwd[:, h, ::-1], end[:, ::-1], rows[:, h, ::-1], first(h),
                                                 ALU.add, ALU.max).then_inc(s_v, 1)
                ch.n += H
                v.wait_ge(s_v, ch.n)

            forward(lambda h: NEG)
            backward(val, lambda h: NEG)
            ch.after(nc.vector.tensor_reduce(keep[:, 0, 0:1], start, AX.X, ALU.min))
            ch.after(nc.vector.tensor_reduce(keep[:, 1, 0:1], end, AX.X, ALU.min))
            ch.after(nc.vector.tensor_copy(keep[:, :, 1:H], keep[:, :, 0:1].to_broadcast([P, 2, H - 1])))
            ch.after(nc.vector.tensor_copy(tails[:, 0, :], fwd[:, :, STEPS - 1]))
            ch.after(nc.vector.tensor_copy(tails[:, 1, :], bwd[:, :, 0]))
            v.sem_inc(s_tail, 1)
            v.wait_ge(s_tailt, 1)
            ch.after(nc.vector.tensor_copy(keep_t[:], ps_k[:, 0:2, :]))
            ch.after(nc.vector.tensor_copy(tails_t[:], ps_k[:, 2:4, :]))
            ch.after(nc.vector.tensor_tensor_scan(neg[:, 0, 1:P + 1], keep_t[:, 0, :], tails_t[:, 0, :], NEG, ALU.add, ALU.max))
            ch.after(nc.vector.tensor_tensor_scan(neg[:, 1, P - 1::-1], keep_t[:, 1, ::-1], tails_t[:, 1, ::-1], NEG, ALU.add, ALU.max))
            v.sem_inc(s_carry, 1)
            v.wait_ge(s_back, 1)
            ch.after(nc.vector.tensor_copy(carry[:], ps_c[:]))
            forward(lambda h: carry[:, 0, h:h + 1])
            backward(fwd, lambda h: carry[:, 1, h:h + 1])
            assert ch.n + 1 == SOFT_EXP_AT, ch.n
            for h in range(H):
                nc.vector.tensor_tensor(val[:, h, :], val[:, h, :], bwd[:, h, :], ALU.subtract).then_inc(s_v, 1)
            for n, (h, w0) in list(enumerate(groups))[0::2]:
                v.wait_ge(s_p, n + 1)
                w1 = min(w0 + 4, WINDOWS)
                nc.vector.tensor_copy(by_w[:, w0:w1, h, :], ps[n % 4][:, 0:w1 - w0, :]).then_inc(s_out[0], 1)
            v.wait_ge(s_out[0], len(groups) // 2)


def late(n, by):
    return not isinstance(n, int) or n >= by


def early(n):
    return not isinstance(n, int) or n < HALVES - RING + 1


def turns(eng, body, first=0):
    for n in range(first, RING):
        body(n, n, True)
    with eng.Fori(1, HALVES // RING - 1) as it:
        for r in range(RING):
            body(it * RING + r, r, True)
    for n in range((HALVES // RING - 1) * RING, HALVES):
        body(n, n % RING, n + 1 < HALVES)


def step_blocks(nc, g, engine, n):
    return nc.values_load_multi_w_load_instructions(
        g.step_block[0:1, bass.ds(n * U, U)], [engine], min_val=0, max_val=LAST_BLOCK,
        skip_runtime_bounds_check_because="made on the chip and clamped")[1]


def pick(nc, g, out, n):
    return nc.vector.tensor_tensor(out, g.step_dst[:, bass.ds(n * U, U)].unsqueeze(2).to_broadcast([P, U, P]),
                                   g.lane[:].unsqueeze(1).to_broadcast([P, U, P]), ALU.is_equal)


def dot_scores(nc, g, scores, rows, node_vals):
    width, per_bank = D, 512 // D
    banks = U // per_bank
    with Phase(nc, g.next_name("score")) as m:
        src = Rows(nc, g, m, rows, width)
        sel = m.sb("sel", [P, 2, U, P])
        sel_t = m.sb("sel_t", [P, 2, U, P])
        prod = m.sb("prod", [P, 2, U, width])
        ps_t = [m.ps(f"ps_t{i}", [P, 4, P]) for i in range(2)]
        ps_q = [m.ps(f"ps_q{i}", [P, per_bank, width]) for i in range(banks)]
        s_used, s_sel, s_selt, s_tpe, s_q, s_qfree, s_red = (
            m.sem(x) for x in ("used", "sel", "selt", "tpe", "q", "qfree", "red"))
        block = m.block()

        @block.gpsimd
        def _(pool):
            turns(pool, src.gather)

        @block.scalar
        def _(act):
            def index(n, slot):
                if late(n, RING):
                    act.wait_ge(s_used, n + (1 - RING))
                src.index(n, slot)

            def transposed(n, slot):
                for i in range(2):
                    act.wait_ge(s_tpe, n * 2 + i + 1)
                    nc.scalar.activation(sel_t[:, slot % 2, 4 * i:4 * i + 4, :], ps_t[i][:], ACT.Copy).then_inc(s_selt, 1)

            for n in range(RING - 1):
                index(n, n)
            transposed(0, 0)

            def half(n, slot, more):
                if early(n):
                    index(n + (RING - 1), (slot + RING - 1) % RING)
                if more:
                    if late(n, 1):
                        act.wait_ge(s_q, n * banks)
                    transposed(n + 1, slot + 1)
            turns(act, half)

        @block.tensor
        def _(pe):
            pe.sem_inc(s_qfree, banks)

            def transposes(n, slot):
                pe.wait_ge(s_sel, n + 1)
                if late(n, 1):
                    pe.wait_ge(s_selt, n * 2)
                for u in range(U):
                    last = nc.tensor.transpose(ps_t[u // 4][:, u % 4, :], sel[:, slot % 2, u, :], g.ident[:])
                    if u % 4 == 3:
                        last.then_inc(s_tpe, 1)

            transposes(0, 0)

            def half(n, slot, more):
                blocks = step_blocks(nc, g, mybir.EngineType.PE, n)
                for u in range(U):
                    if u == U // 2 and more:
                        transposes(n + 1, slot + 1)
                    j = u // per_bank
                    if u % 4 == 0:
                        pe.wait_ge(s_selt, n * 2 + u // 4 + 1)
                    if u % per_bank == 0:
                        pe.wait_ge(s_qfree, n * banks + j + 1)
                    last = nc.tensor.matmul(ps_q[j][:, u % per_bank, :], sel_t[:, slot % 2, u, :],
                                            node_vals[:, bass.ds(blocks[u], 1), :].rearrange("p a d -> p (a d)"),
                                            start=True, stop=True)
                    if u % per_bank == per_bank - 1:
                        last.then_inc(s_q, 1)
            turns(pe, half)

        @block.vector
        def _(v):
            nc.vector.memset(scores[:, HALVES * U:, :], 0.0).then_inc(s_red, 1)
            pick(nc, g, sel[:, 0], 0).then_inc(s_sel, 1)

            def half(n, slot, more):
                par = slot % 2
                if more:
                    if late(n, 1):
                        v.wait_ge(s_tpe, n * 2)
                    pick(nc, g, sel[:, 1 - par], n + 1).then_inc(s_sel, 1)
                src.wait(v, n, slot)
                if late(n, 2):
                    v.wait_ge(s_red, n)
                for j in range(banks):
                    v.wait_ge(s_q, n * banks + j + 1)
                    nc.vector.tensor_tensor(prod[:, par, j * per_bank:(j + 1) * per_bank, :], ps_q[j][:],
                                            src.ring[:, slot, j * per_bank:(j + 1) * per_bank, :],
                                            ALU.mult).then_inc(s_qfree, 1)
                v.wait_ge(s_qfree, n * banks + 2 * banks)
                v.sem_inc(s_used, 1)
                out = scores[:, bass.ds(n * U, U), :]
                nc.vector.tensor_reduce(out.rearrange("p u h -> p (u h)"),
                                        prod[:, par].rearrange("p u (h d) -> p (u h) d", h=H),
                                        AX.X, ALU.add).then_inc(s_red, 1)
            turns(v, half)
            v.wait_ge(s_red, HALVES + 1)


FOUND = 2
GATHERED = U - FOUND
CHUNK = P // H
CHUNKS = -(-BLOCKS // CHUNK)
PARTS = 3
assert FOUND * P <= 512 and CHUNKS == 4


def sum_scores(nc, g, scores, rows, src_vals, dst_vals):
    src_cols = src_vals[:].rearrange("p b h -> p (b h)")
    width = FOUND * P
    with Phase(nc, g.next_name("sum")) as m:
        src = Rows(nc, g, m, rows, H, GATHERED)
        dst_row = m.sb("dst_row", [P, RING, U * P], BF16)
        lane_row = m.sb("lane_row", [P, RING, width], BF16)
        block_row = m.sb("block_row", [P, RING, width], BF16)
        dst_sel = m.sb("dst_sel", [P, RING, U, P], BF16)
        dst_parts = m.sb("dst_parts", [P, BLOCKS, PARTS, H], BF16)
        rest = m.sb("rest", [P, BLOCKS, H])
        lane_sel = m.sb("lane_sel", [P, 2, width])
        kept = m.sb("kept", [P, CHUNKS, width])
        found = m.sb("found", [P, 2, width])
        part = m.sb("part", [P, 1])
        part_i = m.sb("part_i", [P, 2], I32)
        chunk_block = m.sb("chunk_block", [P, CHUNKS])
        part_head = m.sb("part_head", [P, 1])
        head_sel = m.sb("head_sel", [P, H])
        total = m.sb("total", [P, 2, U, H])
        ps_all = [m.ps(f"ps_all{c}", [P, 512]) for c in range(CHUNKS)]
        ps_sum = [m.ps(f"ps_sum{i}", [P, U, H]) for i in range(2)]
        s_iota, s_setup, s_set, s_sel, s_all, s_kept, s_sum, s_fin = (
            m.sem(k) for k in ("iota", "setup", "set", "sel", "all", "kept", "sum", "fin"))
        s_chunks = m.sem("chunks")
        s_rows = [m.sem(f"rows{i}") for i in range(RING)]
        block = m.block()
        of_chunk = lambda c: min(P, BLOCKS * H - c * P)

        @block.sync
        def _(sp):
            def load(n, slot, more):
                if late(n, RING):
                    sp.wait_ge(s_kept, (n - RING + 1) * CHUNKS)
                for dest, r, u0 in ((dst_row, g.dst_lane_rows, 0), (lane_row, g.src_lane_rows, GATHERED),
                                    (block_row, g.src_block_rows, GATHERED)):
                    sp.dma_start(dest[:, slot], r[bass.ds(n * U + u0, U - u0), :].rearrange("s e -> (s e)")
                                 .rearrange("(a n) -> a n", a=1).to_broadcast([P, (U - u0) * P])).then_inc(s_rows[slot], 16)
            turns(sp, load)

        @block.gpsimd
        def _(pool):
            nc.gpsimd.iota(part_i[:], [[0, 2]], 0, 1).then_inc(s_iota, 1)
            turns(pool, src.gather)

        @block.scalar
        def _(act):
            for n in range(RING - 1):
                src.index(n, n)

            def half(n, slot, more):
                if early(n):
                    if late(n, 1):
                        act.wait_ge(s_fin, n * 3)
                    src.index(n + (RING - 1), (slot + RING - 1) % RING)
            turns(act, half)

        @block.tensor
        def _(pe):
            def search(n, slot):
                pe.wait_ge(s_sel, n * 2 + 2)
                for c in range(CHUNKS):
                    if late(n, 1):
                        pe.wait_ge(s_kept, (n - 1) * CHUNKS + c + 1)
                    nc.tensor.matmul(ps_all[c][0:of_chunk(c), 0:width], src_cols[:, c * P:c * P + of_chunk(c)],
                                     lane_sel[:, slot % 2, :], start=True, stop=True).then_inc(s_all, 1)

            def sums(n, slot):
                blocks = step_blocks(nc, g, mybir.EngineType.PE, n)
                pe.wait_ge(s_chunks, n * 3 + 3)
                if late(n, 2):
                    pe.wait_ge(s_fin, n * 3 - 3)
                for u in range(U):
                    k = u - GATHERED
                    for p in range(PARTS):
                        last = nc.tensor.matmul(ps_sum[slot % 2][:, u, :], dst_sel[:, slot, u, :],
                                                dst_parts[:, bass.ds(blocks[u], 1), p, :].rearrange("p a h -> p (a h)"),
                                                start=(p == 0), stop=(k < 0 and p == PARTS - 1))
                    if k >= 0:
                        last = nc.tensor.matmul(ps_sum[slot % 2][:, u, :], found[:, slot % 2, k * P:(k + 1) * P],
                                                head_sel[:], start=False, stop=True)
                last.then_inc(s_sum, 1)

            pe.wait_ge(s_set, 1)
            search(0, 0)

            def half(n, slot, more):
                if more:
                    search(n + 1, (slot + 1) % RING)
                sums(n, slot)
            turns(pe, half)

        @block.vector
        def _(v):
            ch = Chain(v, s_setup)
            ch.after(nc.vector.memset(scores[:, HALVES * U:, :], 0.0))
            ch.after(nc.vector.tensor_copy(rest[:], dst_vals[:]))
            for p in range(PARTS):
                ch.after(nc.vector.tensor_copy(dst_parts[:, :, p, :], rest[:]))
                if p < PARTS - 1:
                    ch.after(nc.vector.tensor_tensor(rest[:], rest[:], dst_parts[:, :, p, :], ALU.subtract))
            v.wait_ge(s_iota, 1)
            ch.after(nc.vector.tensor_copy(part[:], part_i[:, 0:1]))
            ch.after(nc.vector.tensor_scalar(part_i[:, 1:2], part_i[:, 0:1], H - 1, None, ALU.bitwise_and))
            ch.after(nc.vector.tensor_copy(part_head[:], part_i[:, 1:2]))
            ch.after(nc.vector.tensor_scalar(part_i[:, 1:2], part_i[:, 0:1], H.bit_length() - 1, None, ALU.arith_shift_right))
            for c in range(CHUNKS):
                ch.after(nc.vector.tensor_scalar(chunk_block[:, c:c + 1], part_i[:, 1:2], float(CHUNK * c), None, ALU.add))
            nc.vector.tensor_scalar(head_sel[:], g.lane[:, 0:H], part_head[:, 0:1], None, ALU.is_equal).then_inc(s_set, 1)

            def matrices(n, slot):
                v.wait_ge(s_rows[slot], (n + (RING - slot)) * (48 // RING))
                nc.vector.tensor_scalar(dst_sel[:, slot].rearrange("p u e -> p (u e)"), dst_row[:, slot], part[:, 0:1],
                                        None, ALU.is_equal).then_inc(s_sel, 1)
                nc.vector.tensor_scalar(lane_sel[:, slot % 2], lane_row[:, slot], part[:, 0:1], None, ALU.is_equal).then_inc(s_sel, 1)

            def finish(n, slot):
                v.wait_ge(s_sum, n + 1)
                src.wait(v, n, slot)
                par = slot % 2
                if late(n, 2):
                    v.wait_ge(s_fin, n * 3 - 3)
                nc.vector.tensor_tensor(total[:, par, 0:GATHERED], ps_sum[par][:, 0:GATHERED, :], src.ring[:, slot],
                                        ALU.add).then_inc(s_fin, 1)
                nc.vector.tensor_copy(total[:, par, GATHERED:U], ps_sum[par][:, GATHERED:U, :]).then_inc(s_fin, 1)
                v.wait_ge(s_fin, n * 3 + 2)
                x = total[:, par].rearrange("p u h -> p (u h)")
                nc.vector.scalar_tensor_tensor(scores[:, bass.ds(n * U, U), :].rearrange("p u h -> p (u h)"), x, 0.2, x,
                                               ALU.mult, ALU.max).then_inc(s_fin, 1)

            matrices(0, 0)

            def half(n, slot, more):
                if more:
                    if late(n, 1):
                        v.wait_ge(s_all, n * CHUNKS)
                    if late(n, 3):
                        v.wait_ge(s_sum, n - 2)
                    matrices(n + 1, (slot + 1) % RING)
                if late(n, 1):
                    v.wait_ge(s_chunks, n * 3)
                for c in range(CHUNKS):
                    v.wait_ge(s_all, n * CHUNKS + c + 1)
                    at = slice(0, of_chunk(c))
                    nc.vector.scalar_tensor_tensor(kept[at, c, :], block_row[at, slot], chunk_block[at, c:c + 1],
                                                   ps_all[c][at, 0:width], ALU.is_equal, ALU.mult).then_inc(s_kept, 1)
                add = lambda out, a, b: nc.vector.tensor_tensor(out, a, b, ALU.add).then_inc(s_chunks, 1)
                last = slice(0, of_chunk(CHUNKS - 1))
                v.wait_ge(s_kept, n * CHUNKS + CHUNKS)
                add(kept[:, 0], kept[:, 0], kept[:, 1])
                add(kept[last, 2], kept[last, 2], kept[last, 3])
                if late(n, 2):
                    v.wait_ge(s_sum, n - 1)
                v.wait_ge(s_chunks, n * 3 + 2)
                add(found[:, slot % 2], kept[:, 0], kept[:, 2])
                if late(n, 1):
                    finish(n - 1, (slot - 1) % RING)
            turns(v, half)
            finish(HALVES - 1, (HALVES - 1) % RING)
            v.wait_ge(s_fin, HALVES * 3)


def aggregate(nc, g, acc, probs, src):
    with Phase(nc, g.next_name("agg")) as m:
        sel = m.sb("sel", [P, 2, U, P])
        msg = m.sb("msg", [P, 2, U, AGG])
        ps = [m.ps(f"ps{i}", [P, 512]) for i in range(U)]
        s_used, s_sel, s_pcol, s_msg, s_mm, s_add, s_zero = (
            m.sem(x) for x in ("used", "sel", "pcol", "msg", "mm", "add", "zero"))
        block = m.block()

        @block.gpsimd
        def _(pool):
            turns(pool, src.gather, RING)

        @block.scalar
        def _(act):
            def index(n, slot):
                if late(n, RING):
                    act.wait_ge(s_used, n + (1 - RING))
                src.index(n, slot)

            nc.scalar.activation(acc[:, 0:PAIRS, :], g.lane[:, 0:1].unsqueeze(2).to_broadcast([P, PAIRS, AGG]),
                                 ACT.Copy, scale=0.0).then_inc(s_zero, 1)

            def half(n, slot, more):
                if late(n, 1) and early(n):
                    index(n + (RING - 1), (slot + RING - 1) % RING)
                if late(n, 2):
                    act.wait_ge(s_mm, n * U - U)
                nc.scalar.activation(msg[:, slot % 2, :, D:AGG], probs[:, bass.ds(n * U, U), :], ACT.Copy).then_inc(s_pcol, 1)
            turns(act, half)

        @block.tensor
        def _(pe):
            pe.sem_inc(s_add, U)

            def half(n, slot, more):
                pe.wait_ge(s_msg, n + 1)
                pe.wait_ge(s_pcol, n + 1)
                for u in range(U):
                    pe.wait_ge(s_add, n * U + u + 1)
                    nc.tensor.matmul(ps[u][:, 0:AGG], sel[:, slot % 2, u, :], msg[:, slot % 2, u, :],
                                     start=True, stop=True).then_inc(s_mm, 1)
            turns(pe, half)

        @block.vector
        def _(v):
            def message(n, slot, u):
                return nc.vector.tensor_tensor(msg[:, slot % 2, u, 0:D].rearrange("p (h d) -> p h d", h=H),
                                               src.ring[:, slot, u, :].rearrange("p (h d) -> p h d", h=H),
                                               probs[:, bass.ds(n * U + u, 1), :].rearrange("p a h -> p (a h)")
                                               .unsqueeze(2).to_broadcast([P, H, HD]), ALU.mult)

            def start(n, slot):
                pick(nc, g, sel[:, slot % 2], n).then_inc(s_sel, 1)
                src.wait(v, n, slot)

            def finish(n):
                v.wait_ge(s_sel, n * 2 + 2)
                v.sem_inc(s_used, 1)
                v.sem_inc(s_msg, 1)

            start(0, 0)
            for u in range(U):
                ins = message(0, 0, u)
            ins.then_inc(s_sel, 1)
            finish(0)
            nc.vector.memset(acc[:, PAIRS:BLOCKS, :], 0.0).then_inc(s_zero, 1)

            def half(n, slot, more):
                if more:
                    if late(n, 1):
                        v.wait_ge(s_mm, n * U)
                    start(n + 1, (slot + 1) % RING)
                blocks = step_blocks(nc, g, mybir.EngineType.DVE, n)
                for u in range(U):
                    if more:
                        ins = message(n + 1, (slot + 1) % RING, u)
                        if u == U - 1:
                            ins.then_inc(s_sel, 1)
                            finish(n + 1)
                    if u == 0 and isinstance(n, int) and n == 0:
                        v.wait_ge(s_zero, 2)
                    v.wait_ge(s_mm, n * U + u + 1)
                    v.wait_ge(s_add, n * U + u + U)
                    at = acc[:, bass.ds(blocks[u], 1), :].rearrange("p a d -> p (a d)")
                    nc.vector.tensor_tensor(at, at, ps[u][:, 0:AGG], ALU.add).then_inc(s_add, 1)
            turns(v, half)
            v.wait_ge(s_add, HALVES * U + U)


class Count:

    def __init__(self, eng, sem, n, per):
        self.eng, self.sem, self.n, self.per, self.i = eng, sem, n, per, 0

    def step(self, ins):
        self.i += 1
        return ins.then_inc(self.sem, 1)

    def here(self):
        self.eng.wait_ge(self.sem, self.n * self.per + self.i)

    def then(self, ins):
        self.step(ins)
        self.here()

    def done(self):
        assert self.i == self.per, self.i


def rounds(eng, body, count=PAIRS, first=2):
    assert count % 2 == 1 and first % 2 == 0
    for n in range(first):
        body(n, n % 2, 2)
    with eng.Fori(first // 2, count // 2 - 1) as it:
        body(it * 2, 0, 2)
        body(it * 2 + 1, 1, 2)
    for left in (2, 1, 0):
        body(count - 1 - left, left % 2, left)


def pair_rows(dram, n):
    return dram.rearrange("(b p) d -> p b d", p=P)[:, bass.ds(n * 2, 2), :]


LN_STEPS = 5


def norm_begin(nc, c, stat, x, s_var):
    for b in range(2):
        c.step(nc.vector.bn_stats(stat[:, 6 * b:6 * b + 6], x[:, b, :]))
    c.here()
    c.eng.nop(nofuse=True)
    for b in range(2):
        c.step(nc.vector.bn_aggr(stat[:, 12 + 2 * b:14 + 2 * b], stat[:, 6 * b:6 * b + 6]))
    c.here()
    nc.vector.tensor_scalar(stat[:, 16:18], stat[:, 12:16].rearrange("p (b s) -> p b s", b=2)[:, :, 1],
                            LN_EPS, None, ALU.add).then_inc(s_var, 1)


def norm_end(nc, c, stat, out, x, s_rstd, k, per):
    c.eng.wait_ge(s_rstd, c.n * per + k + 1)
    for b in range(2):
        ins = nc.vector.tensor_scalar(out[:, b, :], x[:, b, :], stat[:, 12 + 2 * b:13 + 2 * b], stat[:, 18 + b:19 + b],
                                      ALU.subtract, ALU.mult)
    c.then(ins)


def norm_pair(nc, c, stat, out, x, s_var, s_rstd, k, per):
    norm_begin(nc, c, stat, x, s_var)
    norm_end(nc, c, stat, out, x, s_rstd, k, per)


def spread(row, n):
    return row.rearrange("(a n) -> a n", a=1).to_broadcast([P, n])


def project_qkv(nc, g, q):
    with Phase(nc, "qkv") as m:
        w = m.sb("w", [P, KC, 3 * D])
        x = m.sb("x", [P, 2, 2, D])
        xn = m.sb("xn", [P, 2, 2, D])
        xt = m.sb("xt", [P, 2, KC, 2, P])
        kv = m.sb("kv", [P, 2, 2, 2 * D])
        stat = m.sb("stat", [P, 2, 20])
        ps_t = [m.ps(f"ps_t{i}", [P, 2, KC, P]) for i in range(2)]
        ps_kv = [[m.ps(f"ps_kv{i}{b}", [P, 2 * D]) for b in range(2)] for i in range(2)]
        ps_q = [m.ps(f"ps_q{i}", [P, 2, D]) for i in range(2)]
        s_w, s_ln, s_var, s_rstd, s_t, s_xt, s_mm, s_out = (
            m.sem(k) for k in ("w", "ln", "var", "rstd", "t", "xt", "mm", "out"))
        s_x, s_xnst, s_kvst = ([m.sem(f"{k}{i}") for i in range(2)] for k in ("x", "xnst", "kvst"))
        block = m.block()
        LN = LN_STEPS

        @block.sync
        def _(sp):
            def load(n, slot):
                sp.dma_start(x[:, slot], pair_rows(g.x, n)).then_inc(s_x[slot], 16)

            load(0, 0)
            load(1, 1)
            for i, t in enumerate((g.Wk, g.Wv, g.Wq)):
                sp.dma_start(w[:, :, i * D:(i + 1) * D], t.rearrange("(k p) n -> p k n", p=P)).then_inc(s_w, 16)

            def turn(n, slot, more):
                sp.wait_ge(s_ln, n * LN + LN)
                if more == 2:
                    load(n + 2, slot)
                sp.dma_start(pair_rows(g.norm, n), xn[:, slot]).then_inc(s_xnst[slot], 16)
                sp.wait_ge(s_out, n * 3 + 2)
                sp.dma_start(pair_rows(g.k_rows, n), kv[:, slot, :, 0:D]).then_inc(s_kvst[slot], 16)
                sp.dma_start(pair_rows(g.v_rows, n), kv[:, slot, :, D:2 * D]).then_inc(s_kvst[slot], 16)
            rounds(sp, turn)
            for i, turns_ in enumerate((PAIRS // 2 + 1, PAIRS // 2)):
                sp.wait_ge(s_xnst[i], 16 * turns_)
                sp.wait_ge(s_kvst[i], 32 * turns_)

        @block.gpsimd
        def _(pool):
            def turn(n, slot, more):
                pool.wait_ge(s_var, n + 1)
                nc.gpsimd.tensor_tensor(stat[:, slot, 18:20], stat[:, slot, 16:18], g.minus_half[:], ALU.pow).then_inc(s_rstd, 1)
            rounds(pool, turn)

        @block.vector
        def _(v):
            def turn(n, slot, more):
                c = Count(v, s_ln, n, LN)
                v.wait_ge(s_x[slot], (n + (2 - slot)) * 8)
                if late(n, 2):
                    v.wait_ge(s_xnst[slot], (n - slot) * 8)
                    v.wait_ge(s_t, n - 1)
                norm_pair(nc, c, stat[:, slot], xn[:, slot], x[:, slot], s_var, s_rstd, 0, 1)
                c.done()
            rounds(v, turn)

        @block.tensor
        def _(pe):
            def transposes(n, slot):
                pe.wait_ge(s_ln, n * LN + LN)
                if late(n, 2):
                    pe.wait_ge(s_xt, n - 1)
                for b in range(2):
                    for k in range(KC):
                        last = nc.tensor.transpose(ps_t[slot][:, b, k, :], xn[:, slot, b, k * P:(k + 1) * P], g.ident[:])
                last.then_inc(s_t, 1)

            transposes(0, 0)
            pe.wait_ge(s_w, 48)

            def turn(n, slot, more):
                pe.wait_ge(s_xt, n + 1)
                if late(n, 2):
                    pe.wait_ge(s_out, n * 3 - 3)
                for b in range(2):
                    for k in range(KC):
                        last = nc.tensor.matmul(ps_kv[slot][b][:], xt[:, slot, k, b, :], w[:, k, 0:2 * D],
                                                start=(k == 0), stop=(k == KC - 1))
                    last.then_inc(s_mm, 1)
                if more:
                    transposes(n + 1, 1 - slot)
                for b in range(2):
                    for k in range(KC):
                        last = nc.tensor.matmul(ps_q[slot][:, b, :], xt[:, slot, k, b, :], w[:, k, 2 * D:3 * D],
                                                start=(k == 0), stop=(k == KC - 1))
                last.then_inc(s_mm, 1)
            rounds(pe, turn)

        @block.scalar
        def _(act):
            def evac_xt(n, slot):
                act.wait_ge(s_t, n + 1)
                if late(n, 2):
                    act.wait_ge(s_mm, n * 3 - 3)
                nc.scalar.activation(xt[:, slot].rearrange("p k b n -> p b k n"), ps_t[slot][:], ACT.Copy).then_inc(s_xt, 1)

            evac_xt(0, 0)

            def turn(n, slot, more):
                if late(n, 2):
                    act.wait_ge(s_kvst[slot], (n - slot) * 16)
                for b in range(2):
                    act.wait_ge(s_mm, n * 3 + b + 1)
                    nc.scalar.activation(kv[:, slot, b, :], ps_kv[slot][b][:], ACT.Copy).then_inc(s_out, 1)
                if more:
                    evac_xt(n + 1, 1 - slot)
                act.wait_ge(s_mm, n * 3 + 3)
                nc.scalar.activation(q[:, bass.ds(n * 2, 2), :], ps_q[slot][:], ACT.Copy).then_inc(s_out, 1)
            rounds(act, turn)
            act.wait_ge(s_out, 3 * PAIRS)


def inverse(nc, v, rec, acc, s_rec):
    nc.vector.tensor_scalar(rec[:], acc[:, :, D:AGG], 0.5, None, ALU.max).then_inc(s_rec, 1)
    v.wait_ge(s_rec, 1)
    nc.vector.reciprocal(rec[:], rec[:]).then_inc(s_rec, 1)
    v.wait_ge(s_rec, 2)


def attention_out(nc, g, acc):
    with Phase(nc, "att") as m:
        w = m.sb("w", [P, KC, D])
        vec = m.sb("vec", [P, 3, D])
        h0 = m.sb("h0", [P, 2, 2, D])
        rec = m.sb("rec", [P, BLOCKS, H])
        o = m.sb("o", [P, 2, 2, D])
        ot = m.sb("ot", [P, 2, KC, 2, P])
        t = m.sb("t", [P, 2, D])
        tn = m.sb("tn", [P, 2, D])
        h1 = m.sb("h1", [P, 2, 2, D])
        stat = m.sb("stat", [P, 20])
        ps_t = [m.ps(f"ps_t{i}", [P, 2, KC, P]) for i in range(2)]
        ps_o = [m.ps(f"ps_o{i}", [P, 2, D]) for i in range(2)]
        s_rec = m.sem("rec")
        s_w, s_o, s_c, s_var, s_rstd, s_t, s_ot, s_mm = (
            m.sem(k) for k in ("w", "o", "c", "var", "rstd", "t", "ot", "mm"))
        s_x, s_st = ([m.sem(f"{k}{i}") for i in range(2)] for k in ("x", "st"))
        block = m.block()
        OPS, OUT = 1, 4 + LN_STEPS

        @block.sync
        def _(sp):
            sp.dma_start(w[:], g.Wp.rearrange("(k p) n -> p k n", p=P)).then_inc(s_w, 16)
            for i, r in enumerate((g.bp, g.ln1_g, g.ln1_b)):
                sp.dma_start(vec[:, i, :], spread(r, D)).then_inc(s_w, 16)

            def turn(n, slot, more):
                if late(n, 2):
                    sp.wait_ge(s_c, n * OUT - OUT)
                sp.dma_start(h0[:, slot], pair_rows(g.norm, n)).then_inc(s_x[slot], 16)
                if late(n, 1):
                    sp.wait_ge(s_c, n * OUT)
                    sp.dma_start(pair_rows(g.hidden, n - 1), h1[:, 1 - slot]).then_inc(s_st[1 - slot], 16)
            rounds(sp, turn)
            sp.wait_ge(s_c, PAIRS * OUT)
            sp.dma_start(pair_rows(g.hidden, PAIRS - 1), h1[:, 0]).then_inc(s_st[0], 16)
            sp.wait_ge(s_st[0], 16 * (PAIRS // 2 + 1))
            sp.wait_ge(s_st[1], 16 * (PAIRS // 2))

        @block.gpsimd
        def _(pool):
            def turn(n, slot, more):
                pool.wait_ge(s_var, n + 1)
                nc.gpsimd.tensor_tensor(stat[:, 18:20], stat[:, 16:18], g.minus_half[:], ALU.pow).then_inc(s_rstd, 1)
            rounds(pool, turn)

        @block.tensor
        def _(pe):
            pe.wait_ge(s_w, 64)

            def transposes(n, slot):
                pe.wait_ge(s_o, n * OPS + OPS)
                if late(n, 2):
                    pe.wait_ge(s_ot, n - 1)
                for b in range(2):
                    for k in range(KC):
                        last = nc.tensor.transpose(ps_t[slot][:, b, k, :], o[:, slot, b, k * P:(k + 1) * P], g.ident[:])
                last.then_inc(s_t, 1)
            transposes(0, 0)

            def turn(n, slot, more):
                pe.wait_ge(s_ot, n + 1)
                if late(n, 2):
                    pe.wait_ge(s_c, n * OUT - OUT)
                for b in range(2):
                    for k in range(KC):
                        last = nc.tensor.matmul(ps_o[slot][:, b, :], ot[:, slot, k, b, :], w[:, k, :],
                                                start=(k == 0), stop=(k == KC - 1))
                last.then_inc(s_mm, 1)
                if more:
                    transposes(n + 1, 1 - slot)
            rounds(pe, turn)

        @block.scalar
        def _(act):
            def turn(n, slot, more):
                act.wait_ge(s_t, n + 1)
                if late(n, 2):
                    act.wait_ge(s_mm, n - 1)
                nc.scalar.activation(ot[:, slot].rearrange("p k b n -> p b k n"), ps_t[slot][:], ACT.Copy).then_inc(s_ot, 1)
            rounds(act, turn)

        @block.vector
        def _(v):
            v.wait_ge(s_w, 64)
            inverse(nc, v, rec, acc, s_rec)

            def normalise(n, slot):
                c = Count(v, s_o, n, OPS)
                a = acc[:, bass.ds(n * 2, 2), :]
                if late(n, 2):
                    v.wait_ge(s_t, n - 1)
                c.step(nc.vector.tensor_tensor(o[:, slot].rearrange("p b (h d) -> p b h d", h=H),
                                               a[:, :, 0:D].rearrange("p b (h d) -> p b h d", h=H),
                                               rec[:, bass.ds(n * 2, 2), :].unsqueeze(3).to_broadcast([P, 2, H, HD]), ALU.mult))
                c.done()
            normalise(0, 0)
            normalise(1, 1)

            def turn(n, slot, more):
                c = Count(v, s_c, n, OUT)
                wide = lambda i: vec[:, i, :].unsqueeze(1).to_broadcast([P, 2, D])
                v.wait_ge(s_mm, n + 1)
                v.wait_ge(s_x[slot], (n + (2 - slot)) * 8)
                c.then(nc.vector.tensor_tensor(t[:], ps_o[slot][:], wide(0), ALU.add))
                c.then(nc.vector.tensor_tensor(t[:], t[:], h0[:, slot], ALU.add))
                norm_begin(nc, c, stat, t, s_var)
                if more == 2:
                    normalise(n + 2, slot)
                norm_end(nc, c, stat, tn, t, s_rstd, 0, 1)
                c.then(nc.vector.tensor_tensor(tn[:], tn[:], wide(1), ALU.mult))
                if late(n, 2):
                    v.wait_ge(s_st[slot], (n - slot) * 8)
                c.then(nc.vector.tensor_tensor(h1[:, slot], tn[:], wide(2), ALU.add))
                c.done()
            rounds(v, turn)


def ffn(nc, g, name, rows, w1, b1, w2, func, loads, vectors, outs, epilogue, per, norms=0, tokens=None):
    chunks = FF // P
    count = PAIRS if tokens is None else tokens.shape[1] // 2
    x_step = 8 if tokens is None else 16
    with Phase(nc, name) as m:
        wa = m.sb("wa", [P, KC, FF])
        wb = m.sb("wb", [P, chunks, D])
        ba = m.sb("ba", [P, chunks])
        vec = m.sb("vec", [P, len(vectors), D])
        hx = m.sb("hx", [P, 2, 2, D])
        idx = m.sb("idx", [P, 2, 2], I32)
        xt = m.sb("xt", [P, 2, KC, 2 * P])
        ht = m.sb("ht", [P, 2, chunks, 2 * P])
        lin = m.sb("lin", [P, 2, max(1, len(loads)), 2, D])
        lout = m.sb("lout", [P, 2, len(outs), 2, D])
        tmp = m.sb("tmp", [P, 3, 2, D])
        stat = m.sb("stat", [P, max(1, norms), 20])
        ps_t = m.ps("ps_t", [P, KC, 2, P])
        ps_h = [m.ps(f"ps_h{i}", [P, 2 * P]) for i in range(4)]
        ps_y = [m.ps(f"ps_y{i}", [P, 2, D]) for i in range(2)]
        s_w, s_c, s_var, s_rstd, s_t, s_xt, s_up, s_act, s_y = (
            m.sem(k) for k in ("w", "c", "var", "rstd", "t", "xt", "up", "act", "y"))
        s_l, s_st = ([m.sem(f"{k}{i}") for i in range(2)] for k in ("l", "st"))
        s_x = [m.sem(f"x{i}") for i in range(2)] if tokens is None else m.sems_of_pool("x", 2)
        s_idx = m.sem("idx")
        block = m.block()
        nw = 3 + len(vectors)

        @block.sync
        def _(sp):
            def load(n, slot):
                if late(n, 2):
                    sp.wait_ge(s_t, n - 1)
                sp.dma_start(hx[:, slot], pair_rows(rows, n)).then_inc(s_x[slot], 16)
            if tokens is None:
                load(0, 0)
            sp.dma_start(wa[:], w1.rearrange("(k p) n -> p k n", p=P)).then_inc(s_w, 16)
            sp.dma_start(wb[:], w2.rearrange("(c p) n -> p c n", p=P)).then_inc(s_w, 16)
            with nc.allow_non_contiguous_dma(reason="a bias by partition"):
                sp.dma_start(ba[:], b1.rearrange("(c p) -> p c", p=P)).then_inc(s_w, 16)
            for i, r in enumerate(vectors):
                sp.dma_start(vec[:, i, :], spread(r, D)).then_inc(s_w, 16)

            def store(n, slot):
                sp.wait_ge(s_c, n * per + per)
                for i, r in enumerate(outs):
                    sp.dma_start(pair_rows(r, n), lout[:, slot, i]).then_inc(s_st[slot], 16)

            def turn(n, slot, more):
                if more and tokens is None:
                    load(n + 1, 1 - slot)
                if loads and late(n, 2):
                    sp.wait_ge(s_c, n * per - per)
                for i, r in enumerate(loads):
                    sp.dma_start(lin[:, slot, i], pair_rows(r, n)).then_inc(s_l[slot], 16)
                if late(n, 1):
                    store(n - 1, 1 - slot)
            rounds(sp, turn, count)
            store(count - 1, 0)
            sp.wait_ge(s_st[0], 16 * len(outs) * (count // 2 + 1))
            sp.wait_ge(s_st[1], 16 * len(outs) * (count // 2))

        @block.gpsimd
        def _(pool):
            def turn(n, slot, more):
                for k in range(norms):
                    pool.wait_ge(s_var, n * norms + k + 1)
                    nc.gpsimd.tensor_tensor(stat[:, k, 18:20], stat[:, k, 16:18], g.minus_half[:], ALU.pow).then_inc(s_rstd, 1)

            def gather(n, slot, more):
                if late(n, 2):
                    pool.wait_ge(s_t, n - 1)
                pool.wait_ge(s_idx, n + 1)
                pool.nop(nofuse=True)
                for b in range(2):
                    nc.gpsimd.indirect_dma_start(hx[:, slot, b, :], None, rows,
                                                 bass.IndirectOffsetOnAxis(idx[:, slot, b:b + 1], 0)).then_inc(s_x[slot], 16)
            if norms:
                rounds(pool, turn, count)
            if tokens is not None:
                rounds(pool, gather, count)

        @block.tensor
        def _(pe):
            def transposes(n, slot):
                pe.wait_ge(s_x[slot], (n + (2 - slot)) * x_step)
                if late(n, 1):
                    pe.wait_ge(s_xt, n)
                for b in range(2):
                    for k in range(KC):
                        last = nc.tensor.transpose(ps_t[:, k, b, :], hx[:, slot, b, k * P:(k + 1) * P], g.ident[:])
                last.then_inc(s_t, 1)
            transposes(0, 0)
            pe.wait_ge(s_w, 16 * nw)

            def turn(n, slot, more):
                pe.wait_ge(s_xt, n + 1)
                for c in range(chunks):
                    if late(n, 1) or c >= 4:
                        pe.wait_ge(s_act, n * chunks + c - 3)
                    for k in range(KC):
                        last = nc.tensor.matmul(ps_h[c % 4][:, :], wa[:, k, c * P:(c + 1) * P], xt[:, slot, k, :],
                                                start=(k == 0), stop=(k == KC - 1))
                    last.then_inc(s_up, 1)
                if more:
                    transposes(n + 1, 1 - slot)
                if late(n, 2):
                    pe.wait_ge(s_c, n * per - per)
                for b in range(2):
                    for c in range(chunks):
                        if b == 0:
                            pe.wait_ge(s_act, n * chunks + c + 1)
                        last = nc.tensor.matmul(ps_y[slot][:, b, :], ht[:, slot, c, b * P:(b + 1) * P],
                                                wb[:, c, :], start=(c == 0), stop=(c == chunks - 1))
                last.then_inc(s_y, 1)
            rounds(pe, turn, count)

        @block.scalar
        def _(act):
            act.wait_ge(s_w, 16 * nw)

            def evac_xt(n, slot):
                act.wait_ge(s_t, n + 1)
                nc.scalar.activation(xt[:, slot, :, :], ps_t[:].rearrange("p k b n -> p k (b n)"), ACT.Copy).then_inc(s_xt, 1)

            def index(n, slot):
                if late(n, 2):
                    act.wait_ge(s_x[slot], (n - slot) * x_step)
                nc.scalar.activation(idx[:, slot], tokens[:, bass.ds(n * 2, 2)], ACT.Copy).then_inc(s_idx, 1)
            if tokens is not None:
                index(0, 0)
                index(1, 1)
            evac_xt(0, 0)

            def turn(n, slot, more):
                if tokens is not None and more == 2:
                    index(n + 2, slot)
                if late(n, 2):
                    act.wait_ge(s_y, n - 1)
                for c in range(chunks):
                    act.wait_ge(s_up, n * chunks + c + 1)
                    nc.scalar.activation(ht[:, slot, c, :], ps_h[c % 4][:, :], func,
                                         bias=ba[:, c:c + 1]).then_inc(s_act, 1)
                if more:
                    evac_xt(n + 1, 1 - slot)
            rounds(act, turn, count)

        @block.vector
        def _(v):
            v.wait_ge(s_w, 16 * nw)

            def turn(n, slot, more):
                c = Count(v, s_c, n, per)
                v.wait_ge(s_y, n + 1)
                if loads:
                    v.wait_ge(s_l[slot], (n + (2 - slot)) * (8 * len(loads)))
                if late(n, 2):
                    v.wait_ge(s_st[slot], (n - slot) * (8 * len(outs)))
                epilogue(nc, g, c, n, ps_y[slot], [lin[:, slot, i] for i in range(len(loads))],
                         [vec[:, i, :] for i in range(len(vectors))], [tmp[:, i] for i in range(3)],
                         [lout[:, slot, i] for i in range(len(outs))], [stat[:, k] for k in range(norms)], s_var, s_rstd)
                c.done()
            rounds(v, turn, count)


def wide(row):
    return row.unsqueeze(1).to_broadcast([P, 2, D])


def after_graph(nc, g, c, n, y, loads, vecs, tmp, outs, stats, s_var, s_rstd):
    hid, x = loads
    b2, ln_g, ln_b, wr = vecs
    t, u, z = tmp
    c.then(nc.vector.tensor_tensor(t, y[:], wide(b2), ALU.add))
    c.then(nc.vector.tensor_tensor(t, t, hid, ALU.add))
    norm_pair(nc, c, stats[0], u, t, s_var, s_rstd, 0, 2)
    c.then(nc.vector.tensor_tensor(u, u, wide(ln_g), ALU.mult))
    c.then(nc.vector.tensor_tensor(u, u, wide(ln_b), ALU.add))
    c.then(nc.vector.tensor_tensor(z, u, x, ALU.add))
    norm_pair(nc, c, stats[1], outs[1], z, s_var, s_rstd, 1, 2)
    c.then(nc.vector.tensor_tensor(outs[0], z, outs[1], ALU.add))
    c.then(nc.vector.tensor_tensor(t, outs[1], wide(wr), ALU.mult))
    c.then(nc.vector.tensor_reduce(g.weight[:, bass.ds(n * 2, 2)], t, AX.X, ALU.add))


def biased(nc, g, c, n, y, loads, vecs, tmp, outs, stats, s_var, s_rstd):
    c.then(nc.vector.tensor_tensor(outs[0], y[:], wide(vecs[0]), ALU.add))


HALF_BITS = 16
DIGIT = 4
TRIES = (1 << DIGIT) - 1
assert NPAD < 1 << HALF_BITS


def keep_top(nc, g):
    with Phase(nc, "top") as m:
        br = m.sb("br", [P, 1])
        bits = m.sb("bits", [P, BLOCKS], I32)
        sign = m.sb("sign", [P, BLOCKS], I32)
        half_i = m.sb("half_i", [P, BLOCKS], I32)
        real = m.sb("real", [P, BLOCKS])
        high = m.sb("high", [P, BLOCKS])
        low = m.sb("low", [P, BLOCKS])
        t = m.sb("t", [P, BLOCKS])
        hit = m.sb("hit", [P, TRIES, BLOCKS])
        same = m.sb("same", [P, BLOCKS])
        cnt = m.sb("cnt", [P, TRIES])
        ones = m.sb("ones", [P, P])
        thr = m.sb("thr", [P, 3])
        tries = m.sb("tries", [P, TRIES])
        cand = m.sb("cand", [P, TRIES])
        passed = m.sb("passed", [P, TRIES])
        need = m.sb("need", [P, 1])
        digit = m.sb("digit", [P, 1])
        before = m.sb("before", [P, P])
        run = m.sb("run", [P, BLOCKS + 1])
        zero = m.sb("zero", [P, BLOCKS])
        ps = m.ps("ps", [P, 512])
        ps_r = m.ps("ps_r", [P, 2, BLOCKS])
        s_in, s_v, s_pe, s_cnt, s_pool = (m.sem(x) for x in ("in", "v", "pe", "cnt", "pool"))
        block = m.block()
        counts = 3 * (HALF_BITS // DIGIT) + 2

        @block.sync
        def _(sp):
            sp.dma_start(br[:], g.br.rearrange("(a n) -> a n", a=1).to_broadcast([P, 1])).then_inc(s_in, 16)

        @block.gpsimd
        def _(pool):
            nc.gpsimd.iota(tries[:], [[1, TRIES]], 1, 0, allow_small_or_imprecise_dtypes=True).then_inc(s_pool, 1)
            nc.gpsimd.memset(before[:], 1.0).then_inc(s_pool, 1)
            pool.wait_ge(s_pool, 2)
            nc.gpsimd.affine_select(out=before[:], in_=before[:], compare_op=ALU.is_gt, fill=0.0,
                                    base=0, pattern=[[1, P]], channel_multiplier=-1).then_inc(s_pool, 1)

        @block.tensor
        def _(pe):
            with pe.Fori(0, counts) as i:
                pe.wait_ge(s_cnt, i + 1)
                nc.tensor.matmul(ps[:, 0:TRIES], ones[:], cnt[:], start=True, stop=True).then_inc(s_pe, 1)
            pe.wait_ge(s_cnt, counts + 1)
            pe.wait_ge(s_pool, 3)
            nc.tensor.matmul(ps_r[:, 0, :], before[:], g.keep[:], start=True, stop=True)
            nc.tensor.matmul(ps_r[:, 1, :], ones[:], g.keep[:], start=True, stop=True).then_inc(s_pe, 1)

        @block.vector
        def _(v):
            ch = Chain(v, s_v)
            ts, tt = nc.vector.tensor_scalar, nc.vector.tensor_tensor
            ch.after(nc.vector.memset(ones[:], 1.0))
            ch.after(nc.vector.memset(thr[:], 0.0))
            v.wait_ge(s_in, 16)
            v.wait_ge(s_pool, 1)
            ch.after(ts(g.weight[:], g.weight[:], br[:, 0:1], None, ALU.add))
            ch.after(ts(real[:], g.node[:], float(N), None, ALU.is_lt))
            w = g.weight[:].bitcast(I32)
            ch.after(ts(sign[:], w, 31, None, ALU.arith_shift_right))
            ch.after(ts(sign[:], sign[:], -2147483648, None, ALU.bitwise_or))
            ch.after(tt(bits[:], w, sign[:], ALU.bitwise_xor))
            for half, op, by in ((high, ALU.logical_shift_right, 16), (low, ALU.bitwise_and, 0xFFFF)):
                ch.after(ts(half_i[:], bits[:], by, None, op))
                ch.after(ts(half[:], half_i[:], 1.0, None, ALU.add))
                ch.after(tt(half[:], half[:], real[:], ALU.mult))
                ch.after(ts(half[:], half[:], -1.0, None, ALU.add))
            ch.after(nc.vector.memset(need[:], float(KEEP)))
            done = [0]

            def total():
                nc.vector.tensor_reduce(cnt[:], hit[:], AX.X, ALU.add).then_inc(s_cnt, 1)
                done[0] += 1
                v.wait_ge(s_pe, done[0])

            def search(val, at, op, pred):
                for shift in range(HALF_BITS - DIGIT, -1, -DIGIT):
                    ch.after(ts(cand[:], tries[:], float(1 << shift), thr[:, at:at + 1], ALU.mult, ALU.add))
                    ch.after(tt(hit[:], val[:].unsqueeze(1).to_broadcast([P, TRIES, BLOCKS]),
                                cand[:].unsqueeze(2).to_broadcast([P, TRIES, BLOCKS]), op))
                    total()
                    ch.after(ts(passed[:], ps[:, 0:TRIES], need[:, 0:1], None, pred))
                    ch.after(nc.vector.tensor_reduce(digit[:], passed[:], AX.X, ALU.add))
                    ch.after(ts(digit[:], digit[:], float(1 << shift), None, ALU.mult))
                    ch.after(tt(thr[:, at:at + 1], thr[:, at:at + 1], digit[:], ALU.add))

            def above(val, at):
                ch.after(ts(hit[:, 0, :], val[:], thr[:, at:at + 1], None, ALU.is_gt))
                ch.after(tt(g.keep[:], g.keep[:], hit[:, 0, :], ALU.add))
                total()
                ch.after(tt(need[:], need[:], ps[:, 0:1], ALU.subtract))

            def among(val, at):
                ch.after(ts(t[:], val[:], thr[:, at:at + 1], None, ALU.is_equal))

            ch.after(nc.vector.memset(g.keep[:], 0.0))
            search(high, 0, ALU.is_ge, ALU.is_ge)
            above(high, 0)
            among(high, 0)
            ch.after(ts(low[:], low[:], 1.0, None, ALU.add))
            ch.after(tt(low[:], low[:], t[:], ALU.mult))
            ch.after(ts(low[:], low[:], -1.0, None, ALU.add))
            search(low, 1, ALU.is_ge, ALU.is_ge)
            above(low, 1)
            among(low, 1)
            ch.after(ts(same[:], t[:], -float(NPAD), float(NPAD), ALU.mult, ALU.add))
            ch.after(tt(same[:], same[:], g.node[:], ALU.add))
            search(same, 2, ALU.is_lt, ALU.is_lt)
            ch.after(ts(hit[:, 0, :], same[:], thr[:, 2:3], None, ALU.is_le))
            tt(g.keep[:], g.keep[:], hit[:, 0, :], ALU.add).then_inc(s_cnt, 1)
            assert done[0] == counts
            ch.after(nc.vector.memset(zero[:], 0.0))
            ch.after(nc.vector.memset(run[:], 0.0))
            v.wait_ge(s_pe, counts + 1)
            ch.after(nc.vector.tensor_tensor_scan(run[:, 1:BLOCKS + 1], zero[:], ps_r[:, 1, :], 0.0, ALU.add, ALU.add))
            ch.after(tt(t[:], run[:, 0:BLOCKS], ps_r[:, 0, :], ALU.add))
            ch.after(tt(g.kept_pos[:, 0], t[:], g.keep[:], ALU.mult))
            ch.after(nc.vector.tensor_copy(g.from_kept[:], g.kept_pos[:, 0]))
            ch.after(tt(g.kept_node[:], g.node[:], g.keep[:], ALU.mult))
            ch.after(tt(g.factor[:], g.weight[:], g.keep[:], ALU.mult))


def project_heads(nc, g, s_src, s_dst):
    with Phase(nc, "hds") as m:
        w = m.sb("w", [P, KC, D])
        vec = m.sb("vec", [P, 2, D])
        r = m.sb("r", [P, 2, 2, 2, D])
        x2 = m.sb("x2", [P, 2, 2, D])
        xn = m.sb("xn", [P, 2, 2, D])
        xt = m.sb("xt", [P, 2, KC, 2, P])
        hh = m.sb("hh", [P, 2, 2, D])
        att = m.sb("att", [P, 2, 2, D])
        stat = m.sb("stat", [P, 2, 20])
        idx = m.sb("idx", [P, 2, 2], I32)
        ps_t = [m.ps(f"ps_t{i}", [P, 2, KC, P]) for i in range(2)]
        ps_o = [m.ps(f"ps_o{i}", [P, 2, D]) for i in range(2)]
        s_w, s_ln, s_var, s_rstd, s_t, s_xt, s_mm, s_hh, s_a = (
            m.sem(k) for k in ("w", "ln", "var", "rstd", "t", "xt", "mm", "hh", "a"))
        s_idx, s_y = m.sem("idx"), m.sems_of_pool("y", 2)
        s_x, s_xnst, s_hst, s_sst = ([m.sem(f"{k}{i}") for i in range(2)] for k in ("x", "xnst", "hst", "sst"))
        block = m.block()
        LN, AT = 1 + LN_STEPS, 2

        @block.sync
        def _(sp):
            def load(n, slot):
                sp.dma_start(r[:, slot, 0], pair_rows(g.resid, n)).then_inc(s_x[slot], 16)
            load(0, 0)
            load(1, 1)
            sp.dma_start(w[:], g.W.rearrange("(k p) n -> p k n", p=P)).then_inc(s_w, 16)
            for i, a in enumerate((g.a_src, g.a_dst)):
                sp.dma_start(vec[:, i, :], spread(a.rearrange("h d -> (h d)"), D)).then_inc(s_w, 16)

            def turn(n, slot, more):
                sp.wait_ge(s_ln, n * LN + LN)
                if more == 2:
                    load(n + 2, slot)
                sp.dma_start(pair_rows(g.norm, n), xn[:, slot]).then_inc(s_xnst[slot], 16)
                sp.dma_start(pair_rows(g.x2, n), x2[:, slot]).then_inc(s_xnst[slot], 16)
                sp.wait_ge(s_hh, n + 1)
                sp.dma_start(pair_rows(g.v_rows, n), hh[:, slot]).then_inc(s_hst[slot], 16)
                if late(n, 1):
                    store_src(n - 1, 1 - slot)

            def store_src(n, slot):
                sp.wait_ge(s_a, n * AT * 2 + 2)
                sp.dma_start(pair_rows(g.s_src, n), s_src[:, bass.ds(n * 2, 2), :]).then_inc(s_sst[slot], 16)
            rounds(sp, turn)
            store_src(PAIRS - 1, 0)
            for i, k in enumerate((PAIRS // 2 + 1, PAIRS // 2)):
                sp.wait_ge(s_xnst[i], 32 * k)
                sp.wait_ge(s_hst[i], 16 * k)
                sp.wait_ge(s_sst[i], 16 * k)

        @block.gpsimd
        def _(pool):
            def gather(n, slot):
                if late(n, 2):
                    pool.wait_ge(s_ln, n * LN - LN)
                pool.wait_ge(s_idx, n + 1)
                pool.nop(nofuse=True)
                for b in range(2):
                    nc.gpsimd.indirect_dma_start(r[:, slot, 1, b, :], None, g.kept_y,
                                                 bass.IndirectOffsetOnAxis(idx[:, slot, b:b + 1], 0)).then_inc(s_y[slot], 16)
            gather(0, 0)
            gather(1, 1)

            def turn(n, slot, more):
                pool.wait_ge(s_var, n + 1)
                nc.gpsimd.tensor_tensor(stat[:, slot, 18:20], stat[:, slot, 16:18], g.minus_half[:], ALU.pow).then_inc(s_rstd, 1)
                if more == 2:
                    gather(n + 2, slot)
            rounds(pool, turn)

        @block.vector
        def _(v):
            def begin(n, slot):
                c = Count(v, s_ln, n, LN)
                v.wait_ge(s_x[slot], (n + (2 - slot)) * 8)
                v.wait_ge(s_y[slot], (n + (2 - slot)) * 16)
                if late(n, 2):
                    v.wait_ge(s_xnst[slot], (n - slot) * 16)
                    v.wait_ge(s_t, n - 1)
                for b in range(2):
                    ins = nc.vector.scalar_tensor_tensor(x2[:, slot, b, :], r[:, slot, 1, b, :],
                                                         g.factor[:, bass.ds(n * 2 + b, 1)], r[:, slot, 0, b, :],
                                                         ALU.mult, ALU.add)
                c.then(ins)
                norm_begin(nc, c, stat[:, slot], x2[:, slot], s_var)
                return c

            def end(c, slot):
                norm_end(nc, c, stat[:, slot], xn[:, slot], x2[:, slot], s_rstd, 0, 1)
                c.done()

            def attend(n, slot):
                v.wait_ge(s_hh, n + 1)
                c = Count(v, s_a, n, 2 * AT)
                outs = (s_src[:, bass.ds(n * 2, 2), :], s_dst[:, bass.ds(n * 2, 2), :])
                for i in range(2):
                    c.then(nc.vector.tensor_tensor(att[:, i], hh[:, slot], wide(vec[:, i, :]), ALU.mult))
                    c.then(nc.vector.tensor_reduce(outs[i], att[:, i].rearrange("p b (h d) -> p b h d", h=H), AX.X, ALU.add))
                c.done()

            end(begin(0, 0), 0)
            v.wait_ge(s_w, 48)

            def turn(n, slot, more):
                if more:
                    c = begin(n + 1, 1 - slot)
                if late(n, 1):
                    attend(n - 1, 1 - slot)
                if more:
                    end(c, 1 - slot)
            rounds(v, turn)
            attend(PAIRS - 1, 0)

        @block.tensor
        def _(pe):
            def transposes(n, slot):
                pe.wait_ge(s_ln, n * LN + LN)
                if late(n, 2):
                    pe.wait_ge(s_xt, n - 1)
                for b in range(2):
                    for k in range(KC):
                        last = nc.tensor.transpose(ps_t[slot][:, b, k, :], xn[:, slot, b, k * P:(k + 1) * P], g.ident[:])
                last.then_inc(s_t, 1)
            transposes(0, 0)
            pe.wait_ge(s_w, 48)

            def turn(n, slot, more):
                pe.wait_ge(s_xt, n + 1)
                if late(n, 2):
                    pe.wait_ge(s_hh, n - 1)
                for b in range(2):
                    for k in range(KC):
                        last = nc.tensor.matmul(ps_o[slot][:, b, :], xt[:, slot, k, b, :], w[:, k, :],
                                                start=(k == 0), stop=(k == KC - 1))
                last.then_inc(s_mm, 1)
                if more:
                    transposes(n + 1, 1 - slot)
            rounds(pe, turn)

        @block.scalar
        def _(act):
            def evac_xt(n, slot):
                act.wait_ge(s_t, n + 1)
                if late(n, 2):
                    act.wait_ge(s_mm, n - 1)
                nc.scalar.activation(xt[:, slot].rearrange("p k b n -> p b k n"), ps_t[slot][:], ACT.Copy).then_inc(s_xt, 1)

            def index(n, slot):
                if late(n, 2):
                    act.wait_ge(s_y[slot], (n - slot) * 16)
                nc.scalar.activation(idx[:, slot], g.from_kept[:, bass.ds(n * 2, 2)], ACT.Copy).then_inc(s_idx, 1)
            index(0, 0)
            index(1, 1)
            evac_xt(0, 0)

            def turn(n, slot, more):
                if more == 2:
                    index(n + 2, slot)
                act.wait_ge(s_mm, n + 1)
                if late(n, 2):
                    act.wait_ge(s_hst[slot], (n - slot) * 8)
                    act.wait_ge(s_a, n * 2 * AT - 2 * AT)
                nc.scalar.activation(hh[:, slot], ps_o[slot][:], ACT.Copy).then_inc(s_hh, 1)
                if more:
                    evac_xt(n + 1, 1 - slot)
            rounds(act, turn)


def graph2_out(nc, g, acc, logits, out):
    with Phase(nc, "out2") as m:
        w = m.sb("w", [P, KC, EXPERTS])
        vec = m.sb("vec", [P, 2, D])
        lin = m.sb("lin", [P, 2, 2, 2, D])
        rec = m.sb("rec", [P, BLOCKS, H])
        t = m.sb("t", [P, 2, 2, D])
        u = m.sb("u", [P, 2, D])
        z = m.sb("z", [P, 2, 2, D])
        low = m.sb("low", [P, 2, 2, D])
        el = m.sb("el", [P, 2, 2, D])
        lout = m.sb("lout", [P, 2, 2, 2, D])
        xt = m.sb("xt", [P, 2, KC, 2, P])
        stat = m.sb("stat", [P, 2, 20])
        ps_t = [m.ps(f"ps_t{i}", [P, 2, KC, P]) for i in range(2)]
        ps_l = [m.ps(f"ps_l{i}", [P, 2, EXPERTS]) for i in range(2)]
        s_rec = m.sem("rec")
        s_w, s_a, s_c, s_var, s_rstd, s_var2, s_rstd2, s_t, s_xt, s_mm, s_log, s_low, s_el = (
            m.sem(k) for k in ("w", "a", "c", "var", "rstd", "var2", "rstd2", "t", "xt", "mm", "log", "low", "el"))
        s_norm, s_x2, s_st = ([m.sem(f"{k}{i}") for i in range(2)] for k in ("norm", "x2", "st"))
        block = m.block()
        PER_A, PER = 4 + LN_STEPS, 2 + LN_STEPS

        @block.sync
        def _(sp):
            sp.dma_start(w[:], g.router_t.rearrange("(k p) n -> p k n", p=P)).then_inc(s_w, 16)
            for i, a in enumerate((g.gamma, g.beta)):
                sp.dma_start(vec[:, i, :], spread(a, D)).then_inc(s_w, 16)

            def store(n, slot):
                sp.wait_ge(s_c, n * PER + PER)
                sp.dma_start(pair_rows(out, n), lout[:, slot, 0]).then_inc(s_st[slot], 16)
                sp.dma_start(pair_rows(g.x3n, n), lout[:, slot, 1]).then_inc(s_st[slot], 16)

            def turn(n, slot, more):
                if more == 2:
                    sp.wait_ge(s_a, n * PER_A + PER_A)
                    load_norm(n + 2, slot)
                if late(n, 1):
                    store(n - 1, 1 - slot)
                if more:
                    load_x2(n + 1, 1 - slot)

            def load_norm(n, slot):
                sp.dma_start(lin[:, slot, 0], pair_rows(g.norm, n)).then_inc(s_norm[slot], 16)

            def load_x2(n, slot):
                sp.dma_start(lin[:, slot, 1], pair_rows(g.x2, n)).then_inc(s_x2[slot], 16)

            load_norm(0, 0)
            load_norm(1, 1)
            load_x2(0, 0)
            rounds(sp, turn)
            store(PAIRS - 1, 0)
            sp.wait_ge(s_st[0], 32 * (PAIRS // 2 + 1))
            sp.wait_ge(s_st[1], 32 * (PAIRS // 2))

        @block.gpsimd
        def _(pool):
            def turn(n, slot, more):
                if more:
                    root(n + 1, 0, s_var, s_rstd)
                root(n, 1, s_var2, s_rstd2)

            def root(n, k, variance, done):
                pool.wait_ge(variance, n + 1)
                nc.gpsimd.tensor_tensor(stat[:, k, 18:20], stat[:, k, 16:18], g.minus_half[:], ALU.pow).then_inc(done, 1)
            root(0, 0, s_var, s_rstd)
            rounds(pool, turn)

        @block.scalar
        def _(act):
            def exp(n, slot):
                act.wait_ge(s_low, n + 1)
                if late(n, 2):
                    act.wait_ge(s_c, n * PER - PER)
                nc.scalar.activation(el[:, slot], low[:, slot], ACT.Exp).then_inc(s_el, 1)
            exp(0, 0)

            def turn(n, slot, more):
                if more:
                    exp(n + 1, 1 - slot)
                act.wait_ge(s_t, n + 1)
                if late(n, 2):
                    act.wait_ge(s_mm, n - 1)
                nc.scalar.activation(xt[:, slot].rearrange("p k b n -> p b k n"), ps_t[slot][:], ACT.Copy).then_inc(s_xt, 1)
                act.wait_ge(s_mm, n + 1)
                nc.scalar.activation(logits[:, bass.ds(n * 2, 2), :], ps_l[slot][:], ACT.Copy).then_inc(s_log, 1)
            rounds(act, turn)

        @block.tensor
        def _(pe):
            pe.wait_ge(s_w, 48)

            def turn(n, slot, more):
                pe.wait_ge(s_c, n * PER + PER)
                if late(n, 2):
                    pe.wait_ge(s_xt, n - 1)
                for b in range(2):
                    for k in range(KC):
                        last = nc.tensor.transpose(ps_t[slot][:, b, k, :], lout[:, slot, 1, b, k * P:(k + 1) * P], g.ident[:])
                last.then_inc(s_t, 1)
                pe.wait_ge(s_xt, n + 1)
                if late(n, 2):
                    pe.wait_ge(s_log, n - 1)
                for b in range(2):
                    for k in range(KC):
                        last = nc.tensor.matmul(ps_l[slot][:, b, :], xt[:, slot, k, b, :], w[:, k, :],
                                                start=(k == 0), stop=(k == KC - 1))
                last.then_inc(s_mm, 1)
            rounds(pe, turn)

        @block.vector
        def _(v):
            v.wait_ge(s_w, 48)
            inverse(nc, v, rec, acc, s_rec)
            tt = nc.vector.tensor_tensor

            def a_begin(n, slot):
                c = Count(v, s_a, n, PER_A)
                a = acc[:, bass.ds(n * 2, 2), :]
                c.then(tt(t[:, 0].rearrange("p b (h d) -> p b h d", h=H), a[:, :, 0:D].rearrange("p b (h d) -> p b h d", h=H),
                          rec[:, bass.ds(n * 2, 2), :].unsqueeze(3).to_broadcast([P, 2, H, HD]), ALU.mult))
                v.wait_ge(s_norm[slot], (n + (2 - slot)) * 8)
                c.then(tt(t[:, 0], t[:, 0], lin[:, slot, 0], ALU.add))
                norm_begin(nc, c, stat[:, 0], t[:, 0], s_var)
                return c

            def a_end(c, n, slot):
                norm_end(nc, c, stat[:, 0], u[:], t[:, 0], s_rstd, 0, 1)
                c.then(tt(u[:], u[:], wide(vec[:, 0, :]), ALU.mult))
                c.then(tt(z[:, slot], u[:], wide(vec[:, 1, :]), ALU.add))
                if late(n, 2):
                    v.wait_ge(s_el, n - 1)
                nc.vector.tensor_scalar(low[:, slot], z[:, slot], 0.0, None, ALU.min).then_inc(s_low, 1)
                c.done()

            def b_begin(n, slot):
                c = Count(v, s_c, n, PER)
                v.wait_ge(s_el, n + 1)
                c.then(nc.vector.scalar_tensor_tensor(t[:, 1].rearrange("p b d -> p (b d)"),
                                                      el[:, slot].rearrange("p b d -> p (b d)"), -1.0,
                                                      z[:, slot].rearrange("p b d -> p (b d)"), ALU.add, ALU.max))
                if late(n, 2):
                    v.wait_ge(s_st[slot], (n - slot) * 16)
                    v.wait_ge(s_t, n - 1)
                v.wait_ge(s_x2[slot], (n + (2 - slot)) * 8)
                c.then(tt(lout[:, slot, 0], t[:, 1], lin[:, slot, 1], ALU.add))
                norm_begin(nc, c, stat[:, 1], lout[:, slot, 0], s_var2)
                return c

            def b_end(c, slot):
                norm_end(nc, c, stat[:, 1], lout[:, slot, 1], lout[:, slot, 0], s_rstd2, 0, 1)
                c.done()

            a_end(a_begin(0, 0), 0, 0)

            def turn(n, slot, more):
                if more:
                    a = a_begin(n + 1, 1 - slot)
                b = b_begin(n, slot)
                if more:
                    a_end(a, n + 1, 1 - slot)
                b_end(b, slot)
            rounds(v, turn)
            v.wait_ge(s_log, PAIRS)


def route(nc, g, logits):
    with Phase(nc, "route") as m:
        B, X = BLOCKS, EXPERTS
        col = m.sb("col", [P, B, X])
        mx = m.sb("mx", [P, B])
        e = m.sb("e", [P, B, X])
        eq = m.sb("eq", [P, B, X])
        one = [m.sb(f"one{i}", [P, B, X]) for i in range(2)]
        pr = m.sb("pr", [P, 3, B])
        real = m.sb("real", [P, B])
        both = m.sb("both", [P, B, X])
        before = m.sb("before", [P, P])
        ones = m.sb("ones", [P, P])
        rank = m.sb("rank", [P, B, X])
        tot = m.sb("tot", [P, B, X])
        run = m.sb("run", [P, B + 1, X])
        zero = m.sb("zero", [P, B])
        cnt_i = m.sb("cnt_i", [P, X], I32)
        tiles = m.sb("tiles", [P, X])
        ends = m.sb("ends", [P, X + 1])
        base = m.sb("base", [P, X])
        tile_no = m.sb("tile_no", [P, MAX_TILES])
        over = m.sb("over", [P, MAX_TILES])
        tile_f = m.sb("tile_f", [P, MAX_TILES])
        tmp = m.sb("tmp", [P, B, X])
        ps_r = m.ps("ps_r", [P, 512])
        ps_o = m.ps("ps_o", [P, 512])
        s_i, s_v, s_pe, s_m = (m.sem(x) for x in ("i", "v", "pe", "m"))
        block = m.block()

        @block.sync
        def _(sp):
            for e in range(EXPERTS):
                for i, t in enumerate((g.w1_t, g.w3_t)):
                    sp.dma_start(g.w13[:, e, :, i, :], t[e].rearrange("(k p) h -> p k h", p=P)).then_inc(g.s_experts, 16)
                full = (EC - 1) * P
                sp.dma_start(g.w2_sb[:, e, 0:EC - 1, :], g.w2_t[e, 0:full].rearrange("(c p) d -> p c d", p=P)).then_inc(g.s_experts, 16)
                sp.dma_start(g.w2_sb[0:EH - full, e, EC - 1, :], g.w2_t[e, full:EH]).then_inc(g.s_experts, 16)

        @block.gpsimd
        def _(pool):
            nc.gpsimd.iota(col[:], [[0, B], [1, X]], 0, 0, allow_small_or_imprecise_dtypes=True).then_inc(s_i, 1)
            nc.gpsimd.iota(tile_no[:], [[1, MAX_TILES]], 0, 0, allow_small_or_imprecise_dtypes=True).then_inc(s_i, 1)
            nc.gpsimd.memset(before[:], 1.0).then_inc(s_i, 1)
            pool.wait_ge(s_i, 3)
            nc.gpsimd.affine_select(out=before[:], in_=before[:], compare_op=ALU.is_gt, fill=0.0,
                                    base=0, pattern=[[1, P]], channel_multiplier=-1).then_inc(s_i, 1)

        @block.tensor
        def _(pe):
            pe.wait_ge(s_i, 4)
            pe.wait_ge(s_m, 1)
            flat = both[:].rearrange("p b x -> p (b x)")
            nc.tensor.matmul(ps_r[:, 0:B * X], before[:], flat, start=True, stop=True)
            nc.tensor.matmul(ps_o[:, 0:B * X], ones[:], flat, start=True, stop=True).then_inc(s_pe, 1)

        @block.vector
        def _(v):
            ch = Chain(v, s_v)
            ts, tt, red = nc.vector.tensor_scalar, nc.vector.tensor_tensor, nc.vector.tensor_reduce
            wide_x = lambda a: a.unsqueeze(2).to_broadcast([P, B, X])
            ch.after(nc.vector.memset(ones[:], 1.0))
            ch.after(nc.vector.memset(zero[:], 0.0))
            ch.after(nc.vector.memset(run[:], 0.0))
            ch.after(nc.vector.memset(ends[:], 0.0))
            ch.after(ts(real[:], g.node[:], float(N), None, ALU.is_lt))
            v.wait_ge(s_i, 4)
            ch.after(red(mx[:], logits[:], AX.X, ALU.max))
            ch.after(tt(e[:], logits[:], wide_x(mx[:]), ALU.subtract))
            v.sem_inc(g.s_exp, 1)
            v.wait_ge(g.s_exp, 2)
            ch.after(tt(e[:], g.exp_out[:], wide_x(real[:]), ALU.mult))
            ch.after(red(pr[:, 2], g.exp_out[:], AX.X, ALU.add))
            ch.after(nc.vector.reciprocal(pr[:, 2], pr[:, 2]))
            ch.after(tt(e[:], g.exp_out[:], wide_x(pr[:, 2]), ALU.mult))
            for i in range(2):
                ch.after(red(pr[:, i], e[:], AX.X, ALU.max))
                ch.after(tt(eq[:], e[:], wide_x(pr[:, i]), ALU.is_lt))
                ch.after(ts(eq[:], eq[:], float(X), None, ALU.mult))
                ch.after(tt(eq[:], eq[:], col[:], ALU.add))
                ch.after(red(mx[:], eq[:], AX.X, ALU.min))
                ch.after(tt(one[i][:], col[:], wide_x(mx[:]), ALU.is_equal))
                ch.after(ts(eq[:], one[i][:], -4.0, None, ALU.mult))
                ch.after(tt(e[:], e[:], eq[:], ALU.add))
                ch.after(tt(one[i][:], one[i][:], wide_x(real[:]), ALU.mult))
            ch.after(tt(pr[:, 2], pr[:, 0], pr[:, 1], ALU.add))
            ch.after(ts(pr[:, 2], pr[:, 2], 1e-9, None, ALU.add))
            ch.after(nc.vector.reciprocal(pr[:, 2], pr[:, 2]))
            for i in range(2):
                ch.after(tt(g.listed[:, i], pr[:, i], pr[:, 2], ALU.mult))
            tt(both[:], one[0][:], one[1][:], ALU.add).then_inc(s_m, 1)
            v.wait_ge(s_pe, 1)
            ch.after(nc.vector.tensor_copy(rank[:].rearrange("p b x -> p (b x)"), ps_r[:, 0:B * X]))
            ch.after(nc.vector.tensor_copy(tot[:].rearrange("p b x -> p (b x)"), ps_o[:, 0:B * X]))
            for x in range(X):
                ch.after(nc.vector.tensor_tensor_scan(run[:, 1:B + 1, x], zero[:], tot[:, :, x], 0.0, ALU.add, ALU.add))
            ch.after(ts(cnt_i[:], run[:, B, :], float(P - 1), None, ALU.add))
            ch.after(ts(cnt_i[:], cnt_i[:], 7, None, ALU.arith_shift_right))
            ch.after(nc.vector.tensor_copy(tiles[:], cnt_i[:]))
            ch.after(nc.vector.tensor_tensor_scan(ends[:, 1:X + 1], zero[:, 0:X], tiles[:], 0.0, ALU.add, ALU.add))
            ch.after(ts(base[:], ends[:, 0:X], float(P), None, ALU.mult))
            ch.after(tt(rank[:], rank[:], run[:, 0:B, :], ALU.add))
            ch.after(tt(rank[:], rank[:], base[:].unsqueeze(1).to_broadcast([P, B, X]), ALU.add))
            ch.after(ts(g.listed[:, 2], g.node[:], 1.0, None, ALU.add))
            for i in range(3):
                ch.after(tt(g.listed[:, i], g.listed[:, i], real[:], ALU.mult))
            for i in range(2):
                ch.after(tt(tmp[:], one[i][:], rank[:], ALU.mult))
                ch.after(red(g.pos[:, i], tmp[:], AX.X, ALU.add))
            ch.after(nc.vector.memset(tile_f[:], 0.0))
            for x in range(1, X):
                ch.after(ts(over[:], tile_no[:], ends[:, x:x + 1], None, ALU.is_ge))
                ch.after(tt(tile_f[:], tile_f[:], over[:], ALU.add))
            ch.after(nc.vector.tensor_copy(g.tile_expert[0:1, 0:MAX_TILES], tile_f[0:1, :]))

        @block.scalar
        def _(act):
            act.wait_ge(g.s_exp, 1)
            nc.scalar.activation(g.exp_out[:], e[:], ACT.Exp).then_inc(g.s_exp, 1)


def invert(nc, g, pos, values, tiles, outs):
    lists, part = pos.shape[1], 10
    parts = lists * BLOCKS // part
    assert BLOCKS % part == 0
    with Phase(nc, g.next_name("inv")) as m:
        pos_i = m.sb("pos_i", [P, lists, BLOCKS], I32)
        piece_i = m.sb("piece_i", [P, 2, lists, BLOCKS], I32)
        piece = m.sb("piece", [P, 2, lists, BLOCKS])
        tile_no = m.sb("tile_no", [P, tiles])
        lanes = m.sb("lanes", [P, 2, part, P])
        mark = m.sb("mark", [P, part, tiles])
        marks = m.sb("marks", [P, 2, part, len(values), tiles])
        ps = m.ps("ps", [P, 512])
        s_i, s_v, s_ready, s_mm = (m.sem(k) for k in ("i", "v", "ready", "mm"))
        block = m.block()

        @block.gpsimd
        def _(pool):
            nc.gpsimd.iota(tile_no[:], [[1, tiles]], 0, 0, allow_small_or_imprecise_dtypes=True).then_inc(s_i, 1)

        @block.tensor
        def _(pe):
            for n in range(parts):
                pe.wait_ge(s_ready, (n + 1) * (1 + len(values)))
                for b in range(part):
                    last = nc.tensor.matmul(ps[:, 0:len(values) * tiles], lanes[:, n % 2, b, :],
                                            marks[:, n % 2, b].rearrange("p q t -> p (q t)"),
                                            start=(n == 0 and b == 0), stop=(n == parts - 1 and b == part - 1))
                last.then_inc(s_mm, 1)

        @block.vector
        def _(v):
            ch = Chain(v, s_v)
            ch.after(nc.vector.tensor_copy(pos_i[:], pos[:]))
            ch.after(nc.vector.tensor_scalar(piece_i[:, 0], pos_i[:], P - 1, None, ALU.bitwise_and))
            ch.after(nc.vector.tensor_scalar(piece_i[:, 1], pos_i[:], 7, None, ALU.arith_shift_right))
            ch.after(nc.vector.tensor_copy(piece[:], piece_i[:]))
            v.wait_ge(s_i, 1)
            for n in range(parts):
                k, b0 = n * part // BLOCKS, n * part % BLOCKS
                each = lambda a, width: a.unsqueeze(2).to_broadcast([P, part, width])
                row = lambda a, width: a.unsqueeze(1).to_broadcast([P, part, width])
                if n >= 2:
                    v.wait_ge(s_mm, n - 1)
                nc.vector.tensor_tensor(lanes[:, n % 2], each(piece[:, 0, k, b0:b0 + part], P), row(g.lane[:], P),
                                        ALU.is_equal).then_inc(s_ready, 1)
                if n >= 1:
                    v.wait_ge(s_ready, n * (1 + len(values)))
                ch.after(nc.vector.tensor_tensor(mark[:], each(piece[:, 1, k, b0:b0 + part], tiles),
                                                 row(tile_no[:], tiles), ALU.is_equal))
                for i, value in enumerate(values):
                    nc.vector.tensor_tensor(marks[:, n % 2, :, i, :], mark[:], each(value[k][:, b0:b0 + part], tiles),
                                            ALU.mult).then_inc(s_ready, 1)
            v.wait_ge(s_mm, parts)
            for i, out in enumerate(outs):
                ch.after(nc.vector.tensor_copy(out[:], ps[:, i * tiles:(i + 1) * tiles]))


def experts(nc, g, out):
    with Phase(nc, "moe") as m:
        w13, w2 = g.w13, g.w2_sb
        x = m.sb("x", [P, 2, D])
        idx = m.sb("idx", [P, 2], I32)
        to_row = m.sb("to_row", [P, 2], I32)
        spare = m.sb("spare", [P, 1])
        unused = m.sb("unused", [P, MAX_TILES])
        tokens = m.sb("tokens", [P, MAX_TILES], I32)
        xt = m.sb("xt", [P, 2, KC, P])
        act_ = m.sb("act", [P, EH])
        gl = m.sb("gl", [P, 2, EH])
        gt = m.sb("gt", [P, EC, P])
        y = m.sb("y", [P, 2, D])
        ps_x = m.ps("ps_x", [P, KC, P])
        ps_h = [m.ps(f"ps_h{i}", [P, 512]) for i in range(4)]
        ps_g = [m.ps(f"ps_g{i}", [P, 4, P]) for i in range(2)]
        ps_y = m.ps("ps_y", [P, D])
        s_xt, s_xtc, s_up, s_silu, s_mul, s_gt, s_gtc, s_y, s_yc = (
            m.sem(k) for k in ("xt", "xtc", "up", "silu", "mul", "gt", "gtc", "y", "yc"))
        s_idx = m.sem("idx")
        s_tokens = m.sem("tokens")
        s_x = m.sems_of_pool("x", 2)
        s_added, = m.sems_of_pool("added", 1)
        block = m.block()
        T = MAX_TILES
        rest = EH - (EC - 1) * P

        @block.gpsimd
        def _(pool):
            def turn(n, slot, more):
                if late(n, 2):
                    pool.wait_ge(s_xt, n - 1)
                pool.wait_ge(s_idx, n + 1)
                pool.nop(nofuse=True)
                nc.gpsimd.indirect_dma_start(x[:, slot], None, g.x3n,
                                             bass.IndirectOffsetOnAxis(idx[:, slot:slot + 1], 0)).then_inc(s_x[slot], 16)
                if late(n, 3):
                    scatter(n - 3, 1 - slot, late(n, 4))

            def scatter(n, slot, again):
                pool.wait_ge(s_yc, n + 1)
                if again:
                    pool.wait_ge(s_added, n * 16)
                pool.nop(nofuse=True)
                nc.gpsimd.indirect_dma_start(out, bass.IndirectOffsetOnAxis(to_row[:, slot:slot + 1], 0),
                                             y[:, slot], None, compute_op=ALU.add).then_inc(s_added, 16)
            rounds(pool, turn, T, 4)
            scatter(T - 3, 0, True)
            scatter(T - 2, 1, True)
            scatter(T - 1, 0, True)
            pool.wait_ge(s_added, T * 16)

        @block.tensor
        def _(pe):
            def expert_of(n):
                return nc.values_load_multi_w_load_instructions(
                    g.tile_expert[0:1, bass.ds(n, 1)], [mybir.EngineType.PE], min_val=0, max_val=EXPERTS - 1,
                    skip_runtime_bounds_check_because="made on the chip, at most EXPERTS - 1")[1][0]

            def transposes(n, slot):
                pe.wait_ge(s_x[slot], (n + (2 - slot)) * 8)
                if late(n, 1):
                    pe.wait_ge(s_xtc, n)
                for k in range(KC):
                    last = nc.tensor.transpose(ps_x[:, k, :], x[:, slot, k * P:(k + 1) * P], g.ident[:])
                last.then_inc(s_xt, 1)

            def down(n, slot):
                e = expert_of(n)
                if late(n, 1):
                    pe.wait_ge(s_yc, n)
                for c in range(EC):
                    if c % 4 == 0:
                        pe.wait_ge(s_gtc, n * 2 + c // 4 + 1)
                    size = P if c < EC - 1 else rest
                    last = nc.tensor.matmul(ps_y[:], gt[0:size, c, :], w2[0:size, :, c, :][:, bass.ds(e, 1), :].rearrange("p a d -> p (a d)"),
                                            start=(c == 0), stop=(c == EC - 1))
                last.then_inc(s_y, 1)

            transposes(0, 0)
            pe.wait_ge(g.s_experts, 16 * 4 * EXPERTS)

            def turn(n, slot, more):
                e = expert_of(n)
                pe.wait_ge(s_xtc, n + 1)
                for i in range(2):
                    for hf in range(2):
                        if late(n, 1):
                            pe.wait_ge(s_mul, n * 2 - 1 + hf)
                        for k in range(KC):
                            last = nc.tensor.matmul(ps_h[2 * i + hf][:, 0:EHALF], xt[:, slot, k, :],
                                                    w13[:, :, k, i, hf * EHALF:(hf + 1) * EHALF][:, bass.ds(e, 1), :].rearrange("p a h -> p (a h)"),
                                                    start=(k == 0), stop=(k == KC - 1))
                        last.then_inc(s_up, 1)
                if more:
                    transposes(n + 1, 1 - slot)
                if late(n, 1):
                    down(n - 1, 1 - slot)
                pe.wait_ge(s_mul, n * 2 + 2)
                for c in range(EC):
                    size = P if c < EC - 1 else rest
                    last = nc.tensor.transpose(ps_g[c // 4][0:size, c % 4, :], gl[:, slot, c * P:c * P + size], g.ident[:])
                    if c in (3, EC - 1):
                        last.then_inc(s_gt, 1)
            rounds(pe, turn, T)
            down(T - 1, 0)

        @block.scalar
        def _(act):
            def index(n, slot):
                if late(n, 2):
                    act.wait_ge(s_x[slot], (n - slot) * 8)
                nc.scalar.activation(idx[:, slot:slot + 1], tokens[:, bass.ds(n, 1)], ACT.Copy).then_inc(s_idx, 1)
            act.wait_ge(s_tokens, 4)
            index(0, 0)
            index(1, 1)

            def evac_xt(n, slot):
                act.wait_ge(s_xt, n + 1)
                nc.scalar.activation(xt[:, slot], ps_x[:], ACT.Copy).then_inc(s_xtc, 1)
            evac_xt(0, 0)

            def scale(n, slot, again):
                act.wait_ge(s_y, n + 1)
                if again:
                    act.wait_ge(s_added, (n - 1) * 16)
                nc.scalar.activation(to_row[:, slot:slot + 1], tokens[:, bass.ds(n, 1)], ACT.Copy)
                nc.scalar.activation(y[:, slot], ps_y[:], ACT.Copy, scale=g.tile_gate[:, bass.ds(n, 1)]).then_inc(s_yc, 1)

            def turn(n, slot, more):
                if more == 2:
                    index(n + 2, slot)
                for hf in range(2):
                    act.wait_ge(s_up, n * 4 + hf + 1)
                    if late(n, 1):
                        act.wait_ge(s_mul, n * 2 - 1 + hf)
                    nc.scalar.activation(act_[:, hf * EHALF:(hf + 1) * EHALF], ps_h[hf][:, 0:EHALF], ACT.Silu).then_inc(s_silu, 1)
                if more:
                    evac_xt(n + 1, 1 - slot)
                if late(n, 1):
                    scale(n - 1, 1 - slot, late(n, 3))
                for i in range(2):
                    act.wait_ge(s_gt, n * 2 + i + 1)
                    if i == 0:
                        nc.scalar.activation(gt[:, 0:4, :], ps_g[0][:], ACT.Copy).then_inc(s_gtc, 1)
                    else:
                        nc.scalar.activation(gt[:, 4:5, :], ps_g[1][:, 0:1, :], ACT.Copy)
                        nc.scalar.activation(gt[0:rest, 5:6, :], ps_g[1][0:rest, 1:2, :], ACT.Copy).then_inc(s_gtc, 1)
            rounds(act, turn, T, 4)
            scale(T - 1, 0, True)

        @block.vector
        def _(v):
            v_op = nc.vector.tensor_scalar
            v_op(spare[:], g.node[:, 0:1], float(N + 1), None, ALU.add).then_inc(s_tokens, 1)
            v.wait_ge(s_tokens, 1)
            v_op(unused[:], g.tile_list[:], 0.0, spare[:, 0:1], ALU.is_equal, ALU.mult).then_inc(s_tokens, 1)
            v.wait_ge(s_tokens, 2)
            nc.vector.tensor_tensor(unused[:], unused[:], g.tile_list[:], ALU.add).then_inc(s_tokens, 1)
            v.wait_ge(s_tokens, 3)
            v_op(tokens[:], unused[:], -1.0, None, ALU.add).then_inc(s_tokens, 1)

            def turn(n, slot, more):
                for hf in range(2):
                    v.wait_ge(s_silu, n * 2 + hf + 1)
                    v.wait_ge(s_up, n * 4 + hf + 3)
                    if late(n, 2):
                        v.wait_ge(s_gt, n * 2 - 2)
                    nc.vector.tensor_tensor(gl[:, slot, hf * EHALF:(hf + 1) * EHALF], ps_h[2 + hf][:, 0:EHALF],
                                            act_[:, hf * EHALF:(hf + 1) * EHALF], ALU.mult).then_inc(s_mul, 1)
            rounds(v, turn, T)


class Plan:

    def __init__(self, ins):
        self.names = {}
        (self.x, self.src_rows, self.dst_rows, self.bias_rows,
         self.Wq, self.Wk, self.Wv, self.Wp, self.bp, self.ln1_g, self.ln1_b, self.ln2_g, self.ln2_b,
         self.W1, self.b1, self.W2, self.b2, self.wr, self.br, self.w1, self.fb1, self.w2, self.fb2,
         self.W, self.a_src, self.a_dst, self.gamma, self.beta,
         self.router_t, self.w1_t, self.w3_t, self.w2_t) = (ins[k] for k in INPUTS)

    def next_name(self, name):
        self.names[name] = self.names.get(name, 0) + 1
        return f"{name}{self.names[name]}"


def set_constants(nc, g):
    with Phase(nc, "const") as m:
        s_c, s_half = m.sem("c"), m.sem("half")
        block = m.block()

        @block.vector
        def _(v):
            nc.vector.memset(g.minus_half[:], -0.5).then_inc(s_half, 1)
            v.wait_ge(s_half, 1)

        @block.gpsimd
        def _(pool):
            nc.gpsimd.memset(g.ident[:], 0.0).then_inc(s_c, 1)
            pool.wait_ge(s_c, 1)
            nc.gpsimd.affine_select(out=g.ident[:], in_=g.ident[:], compare_op=ALU.not_equal, fill=1.0,
                                    base=0, pattern=[[-1, P]], channel_multiplier=1).then_inc(s_c, 1)
            nc.gpsimd.iota(g.lane[:], [[1, P]], 0, 0, allow_small_or_imprecise_dtypes=True).then_inc(s_c, 1)
            nc.gpsimd.iota(g.node[:], [[P, BLOCKS]], 0, 1, allow_small_or_imprecise_dtypes=True).then_inc(s_c, 1)
            pool.wait_ge(s_c, 4)


INPUTS = {
    "x": (NPAD, D), "src_rows": (TILE_ROWS, P), "dst_rows": (TILE_ROWS, P), "bias_rows": (TILE_ROWS, P),
    "Wq": (D, D), "Wk": (D, D), "Wv": (D, D), "Wp": (D, D), "bp": (D,), "ln1_g": (D,), "ln1_b": (D,),
    "ln2_g": (D,), "ln2_b": (D,), "W1": (D, FF), "b1": (FF,), "W2": (FF, D), "b2": (D,),
    "wr": (D,), "br": (1,), "w1": (D, FF), "fb1": (FF,), "w2": (FF, D), "fb2": (D,),
    "W": (D, D), "a_src": (H, HD), "a_dst": (H, HD), "gamma": (D,), "beta": (D,),
    "router_t": (D, EXPERTS), "w1_t": (EXPERTS, D, EH), "w3_t": (EXPERTS, D, EH), "w2_t": (EXPERTS, EH, D),
}


def program(nc, ins, out):
    g = Plan(ins)

    def dram(name, shape):
        return nc.dram_tensor(name, shape, F32).ap()

    g.norm, g.k_rows, g.v_rows, g.hidden, g.resid, g.x1n, g.x2, g.x3n = (
        dram(n, (NPAD, D)) for n in ("norm", "k_rows", "v_rows", "hidden", "resid", "x1n", "x2", "x3n"))
    g.s_src = dram("s_src", (NPAD, H))
    g.dst_lane_rows, g.src_lane_rows, g.src_block_rows = (
        nc.dram_tensor(n, (STEPS, P), BF16).ap() for n in ("dst_lane_rows", "src_lane_rows", "src_block_rows"))
    g.kept_y = dram("kept_y", (KEPT_BLOCKS * P, D))

    with Phase(nc, "all") as top:
        g.ident, g.lane = top.sb("ident", [P, P]), top.sb("lane", [P, P])
        g.minus_half = top.sb("minus_half", [P, 2])
        g.node = top.sb("node", [P, BLOCKS])
        g.logits = top.sb("logits", [P, BLOCKS, EXPERTS])
        g.weight, g.keep = top.sb("weight", [P, BLOCKS]), top.sb("keep", [P, BLOCKS])
        g.factor = top.sb("factor", [P, BLOCKS])
        g.kept_pos, g.kept_node = top.sb("kept_pos", [P, 1, BLOCKS]), top.sb("kept_node", [P, BLOCKS])
        g.from_kept, g.kept_tokens = top.sb("from_kept", [P, BLOCKS], I32), top.sb("kept_tokens", [P, KEPT_BLOCKS], I32)
        g.step_dst, g.step_src = top.sb("step_dst", [P, STEPS]), top.sb("step_src", [P, STEPS], I32)
        g.step_block = top.sb("step_block", [1, STEPS], I32)
        g.run_bias, g.run_off, g.run_new = (top.sb("run_bias", [P, STEPS]), top.sb("run_off", [P, STEPS]),
                                            top.sb("run_new", [P, STEPS + 1]))
        set_constants(nc, g)
        step_tables(nc, g)

        with Phase(nc, "graph1") as m:
            scores = m.sb("scores", [P, STEPS, H])
            with Phase(nc, "q") as mq:
                q = mq.sb("q", [P, BLOCKS, D])
                project_qkv(nc, g, q)
                dot_scores(nc, g, scores, g.k_rows, q)
            with Phase(nc, "values1") as mv:
                src = Rows(nc, g, mv, g.v_rows, D)
                edge_softmax(nc, g, scores, g.run_bias, float(HD) ** -0.5, src)
                acc = mv.sb("acc", [P, BLOCKS, AGG])
                aggregate(nc, g, acc, scores, src)
                attention_out(nc, g, acc)
        ffn(nc, g, "ffn1", g.hidden, g.W1, g.b1, g.W2, ACT.Gelu, [g.hidden, g.x], [g.b2, g.ln2_g, g.ln2_b, g.wr],
            [g.resid, g.x1n], after_graph, 8 + 2 * LN_STEPS, 2)
        keep_top(nc, g)
        invert(nc, g, g.kept_pos, [[g.kept_node]], KEPT_BLOCKS, [g.kept_tokens])
        ffn(nc, g, "ffn2", g.x1n, g.w1, g.fb1, g.w2, ACT.Gelu_apprx_tanh, [], [g.fb2],
            [g.kept_y], biased, 1, tokens=g.kept_tokens)

        with Phase(nc, "graph2") as m:
            scores = m.sb("scores", [P, STEPS, H])
            s_src, s_dst = m.sb("s_src", [P, BLOCKS, H]), m.sb("s_dst", [P, BLOCKS, H])
            project_heads(nc, g, s_src, s_dst)
            sum_scores(nc, g, scores, g.s_src, s_src, s_dst)
            with Phase(nc, "values2") as mv:
                src = Rows(nc, g, mv, g.v_rows, D)
                edge_softmax(nc, g, scores, g.run_off, 1.0, src)
                acc = mv.sb("acc", [P, BLOCKS, AGG])
                aggregate(nc, g, acc, scores, src)
                graph2_out(nc, g, acc, g.logits, out)
        with Phase(nc, "experts") as m:
            g.listed = m.sb("listed", [P, 3, BLOCKS])
            g.pos = m.sb("pos", [P, 2, BLOCKS])
            g.tile_list, g.tile_gate = m.sb("tile_list", [P, MAX_TILES]), m.sb("tile_gate", [P, MAX_TILES])
            g.tile_expert = m.sb("tile_expert", [1, MAX_TILES], I32)
            g.exp_out = m.sb("exp_out", [P, BLOCKS, EXPERTS])
            g.w13, g.w2_sb = m.sb("w13", [P, EXPERTS, KC, 2, EH]), m.sb("w2", [P, EXPERTS, EC, D])
            g.s_exp, g.s_experts = m.sem("exp"), m.sem("experts")
            route(nc, g, g.logits)
            invert(nc, g, g.pos, [[g.listed[:, 2]] * 2, [g.listed[:, 0], g.listed[:, 1]]], MAX_TILES,
                   [g.tile_list, g.tile_gate])
            experts(nc, g, out)


def kernel(**inputs):
    import numpy as np
    import concourse.bacc as bacc
    from concourse.bass_utils import run_bass_kernel_spmd

    def rows(a, pad):
        flat = np.full((EPAD,), pad, a.dtype)
        flat[:E] = a.reshape(-1)
        return flat.reshape(TILE_ROWS, P)

    i = {k: np.asarray(v) for k, v in inputs.items()}
    x = np.zeros((NPAD, D), np.float32)
    x[:N] = i["x"]
    arrays = {"x": x, "src_rows": rows(i["src"], 0), "dst_rows": rows(i["dst"], DST_PAD),
              "bias_rows": rows(i["edge_weight1"], 0)}
    for k in ("Wq", "Wk", "Wv", "Wp", "bp", "ln1_g", "ln1_b", "ln2_g", "ln2_b", "W1", "b1", "W2", "b2"):
        arrays[k] = i["L0_gnn_" + k]
    arrays |= {"wr": i["L0_ffn_wr"].reshape(-1), "br": i["L0_ffn_br"], "w1": i["L0_ffn_w1"], "fb1": i["L0_ffn_b1"],
               "w2": i["L0_ffn_w2"], "fb2": i["L0_ffn_b2"]}
    for k in ("W", "a_src", "a_dst", "gamma", "beta"):
        arrays[k] = i["L1_gnn_" + k]
    arrays |= {"router_t": i["L1_ffn_router_w"].T, "w1_t": i["L1_ffn_w1"].transpose(0, 2, 1),
               "w3_t": i["L1_ffn_w3"].transpose(0, 2, 1), "w2_t": i["L1_ffn_w2"].transpose(0, 2, 1)}

    nc = bacc.Bacc("TRN2", target_bir_lowering=False, num_devices=1)
    ins, fed = {}, {}
    for k, shape in INPUTS.items():
        a = np.ascontiguousarray(arrays[k])
        assert a.shape == shape
        fed[f"in_{k}"] = a
        ins[k] = nc.dram_tensor(f"in_{k}", shape, mybir.dt.from_np(a.dtype), kind="ExternalInput").ap()
    out = nc.dram_tensor("out", (NPAD, D), F32, kind="ExternalOutput").ap()
    program(nc, ins, out)
    r = run_bass_kernel_spmd(nc, [fed], core_ids=[0])
    return r.results[0]["out"][:N]
```
